# Optimizing a Trainium2 kernel written in Bass

```python
import numpy as np
import jax
import jax.numpy as jnp

def _softmax(x, axis=-1):
    return jax.nn.softmax(x, axis=axis)

def _gelu(x):
    return jax.nn.gelu(x, approximate=True)

def _silu(x):
    return jax.nn.silu(x)

def _sigmoid(x):
    return jax.nn.sigmoid(x)

def _layernorm(x, axis=-1, eps=1e-05):
    m = jnp.mean(x, axis=axis, keepdims=True)
    v = jnp.var(x, axis=axis, keepdims=True)
    return (x - m) / jnp.sqrt(v + eps)

def _scatter_add(tgt, idx, src, axis=0):
    return tgt.at[idx].add(src)

def _segment_sum(src, seg, n):
    return jax.ops.segment_sum(src, seg, n)
kernel_name = 'mk_gnn_resnorm_d2_gnn_r32_ecfaff'

def setup_inputs(seed: int=0):
    np.random.seed(seed)
    _w = jnp.asarray

    def _rec_inputs():
        import jax
        import jax.numpy as jnp
        _gk = jax.random.key(seed)
        x = -0.0005121 + 1.001 * jax.random.normal(jax.random.fold_in(_gk, 1), (3125, 160), jnp.float32)
        src = jax.random.randint(jax.random.fold_in(_gk, 2), (100000,), 0, 3125, jnp.int32)
        dst = jnp.minimum((3125 * jax.random.uniform(jax.random.fold_in(_gk, 3), (100000,)) ** 2.0).astype(jnp.int32), 99999)
        _o = jnp.argsort(dst, stable=True)
        src = src[_o]
        dst = dst[_o]
        edge_attr_16 = -0.000191324 + 0.999809 * jax.random.normal(jax.random.fold_in(_gk, 12), (100000, 16), jnp.float32)
        edge_attr_3 = 0.00047201 + 1.00023 * jax.random.normal(jax.random.fold_in(_gk, 13), (100000, 3), jnp.float32)
        edge_attr_4 = 0.000126197 + 0.999763 * jax.random.normal(jax.random.fold_in(_gk, 14), (100000, 4), jnp.float32)
        edge_attr_64 = 0.000279952 + 1.00013 * jax.random.normal(jax.random.fold_in(_gk, 15), (100000, 64), jnp.float32)
        node_vec1 = jax.random.uniform(jax.random.fold_in(_gk, 17), (3125, 1), jnp.float32, 0.0, 1)
        return (x, src, dst, edge_attr_16, edge_attr_3, edge_attr_4, edge_attr_64, node_vec1)
    x, src, dst, edge_attr_16, edge_attr_3, edge_attr_4, edge_attr_64, node_vec1 = _rec_inputs()

    def _L0_gnn_setup():
        import jax, jax.numpy as jnp
        import numpy as np
        N = 625
        E = 10000
        MUL0 = 64
        MUL1 = 32
        FC_IN = 16
        FC_H = 64
        WNUM = 192
        key = jax.random.key(seed)
        ks = jax.random.split(key, 16)
        return {'x': jax.random.normal(ks[0], (N, MUL0 + 3 * MUL1), jnp.float32), 'node_attr': jnp.ones((N, 1), jnp.float32), 'edge_scalars': jax.random.normal(ks[1], (E, FC_IN), jnp.float32), 'edge_attr_sh': jax.random.normal(ks[2], (E, 4), jnp.float32), 'edge_src': jax.random.randint(ks[3], (E,), 0, N), 'edge_dst': jax.random.randint(ks[4], (E,), 0, N), 'Wfc1': jax.random.normal(ks[5], (FC_IN, FC_H), jnp.float32), 'Wfc2': jax.random.normal(ks[6], (FC_H, WNUM), jnp.float32), 'Wsc0': jax.random.normal(ks[7], (MUL0, MUL0), jnp.float32), 'Wsc1': jax.random.normal(ks[8], (MUL1, MUL1), jnp.float32), 'Wl1_0': jax.random.normal(ks[9], (MUL0, MUL0), jnp.float32), 'Wl1_1': jax.random.normal(ks[10], (MUL1, MUL1), jnp.float32), 'Wl2_s': jax.random.normal(ks[11], (MUL0 + MUL1, MUL0), jnp.float32), 'Wl2_v': jax.random.normal(ks[12], (MUL0 + MUL1, MUL1), jnp.float32), 'Wa': 0.1 * jax.random.normal(ks[13], (MUL0 + MUL1, 1), jnp.float32)}
    _L0_gnn_all = _L0_gnn_setup()
    _L0_gnn_in = {k: v for k, v in _L0_gnn_all.items() if k in ('Wfc1', 'Wfc2', 'Wsc0', 'Wsc1', 'Wl1_0', 'Wl1_1', 'Wl2_s', 'Wl2_v', 'Wa')}
    del _L0_gnn_all

    def _L1_gnn_setup():
        import jax, jax.numpy as jnp
        import numpy as np
        N_NODES = 10000
        N_EDGES = 10000
        MUL0, MUL1 = (64, 32)
        EDGE_DIM = 64
        W_NUMEL = 224
        DENOM = 32.0
        SQRT3 = 3.0 ** 0.5
        INV_SQRT3 = 1.0 / SQRT3
        INV_SQRT2 = 2.0 ** (-0.5)

        def _forward(node_feature, edge_attr, edge_feature, W_skip0, W_skip1, W_nl0, W_nl1, W_fc1, W_fc2, W_out_s, W_out_v, edge_index):
            N = node_feature.shape[0]
            E = edge_attr.shape[0]
            s = node_feature[:, :MUL0]
            v = node_feature[:, MUL0:].reshape(N, MUL1, 3)
            skip_s = s @ W_skip0
            skip_v = jnp.einsum('nmi,mk->nki', v, W_skip1)
            s = s @ W_nl0
            v = jnp.einsum('nmi,mk->nki', v, W_nl1)
            rhat = edge_attr / jnp.linalg.norm(edge_attr, axis=-1, keepdims=True)
            sh1 = SQRT3 * rhat
            w = jax.nn.relu(edge_feature @ W_fc1) @ W_fc2
            w0, w1, w2, w3, w4 = jnp.split(w, [64, 128, 160, 192], axis=-1)
            src, dst = (edge_index[0], edge_index[1])
            xs = s[dst]
            xv = v[dst]
            out0a = w0 * xs
            out0b = w3 * (jnp.einsum('emi,ei->em', xv, sh1) * INV_SQRT3)
            out1a = (w1 * xs)[:, :, None] * sh1[:, None, :]
            out1b = w2[:, :, None] * xv
            out1c = w4[:, :, None] * (jnp.cross(xv, sh1[:, None, :]) * INV_SQRT2)
            tp = jnp.concatenate([out0a, out0b, out1a.reshape(E, -1), out1b.reshape(E, -1), out1c.reshape(E, -1)], axis=-1)
            agg = jax.ops.segment_sum(tp, src, num_segments=N) / DENOM
            agg_s = agg[:, :96]
            agg_v = agg[:, 96:].reshape(N, 128, 3)
            out_s = agg_s @ W_out_s + skip_s
            out_v = jnp.einsum('nmi,mk->nki', agg_v, W_out_v) + skip_v
            fs = jax.nn.silu(out_s[:, :MUL0])
            gate = jax.nn.sigmoid(out_s[:, MUL0:MUL0 + 32])
            gv = gate[:, :, None] * out_v
            return jnp.concatenate([fs, gv.reshape(N, -1)], axis=-1)
        key = jax.random.key(seed)
        ks = jax.random.split(key, 12)

        def lin(k, fi, fo):
            return jax.random.normal(k, (fi, fo), jnp.float32) / np.float32(np.sqrt(fi))
        return {'node_feature': jax.random.normal(ks[0], (N_NODES, MUL0 + 3 * MUL1), jnp.float32), 'edge_attr': jax.random.normal(ks[1], (N_EDGES, 3), jnp.float32), 'edge_feature': jax.random.normal(ks[2], (N_EDGES, EDGE_DIM), jnp.float32), 'W_skip0': lin(ks[3], MUL0, 96), 'W_skip1': lin(ks[4], MUL1, 32), 'W_nl0': lin(ks[5], MUL0, MUL0), 'W_nl1': lin(ks[6], MUL1, MUL1), 'W_fc1': lin(ks[7], EDGE_DIM, 64), 'W_fc2': lin(ks[8], 64, W_NUMEL), 'W_out_s': lin(ks[9], 96, 96), 'W_out_v': lin(ks[10], 128, 32), 'edge_index': jax.random.randint(ks[11], (2, N_EDGES), 0, N_NODES)}
    _L1_gnn_all = _L1_gnn_setup()
    _L1_gnn_in = {k: v for k, v in _L1_gnn_all.items() if k in ('W_skip0', 'W_skip1', 'W_nl0', 'W_nl1', 'W_fc1', 'W_fc2', 'W_out_s', 'W_out_v')}
    del _L1_gnn_all
    return {'x': x, 'src': src, 'dst': dst, 'edge_attr_16': edge_attr_16, 'edge_attr_3': edge_attr_3, 'edge_attr_4': edge_attr_4, 'edge_attr_64': edge_attr_64, 'node_vec1': node_vec1, 'L0_gnn_Wfc1': _L0_gnn_in['Wfc1'], 'L0_gnn_Wfc2': _L0_gnn_in['Wfc2'], 'L0_gnn_Wsc0': _L0_gnn_in['Wsc0'], 'L0_gnn_Wsc1': _L0_gnn_in['Wsc1'], 'L0_gnn_Wl1_0': _L0_gnn_in['Wl1_0'], 'L0_gnn_Wl1_1': _L0_gnn_in['Wl1_1'], 'L0_gnn_Wl2_s': _L0_gnn_in['Wl2_s'], 'L0_gnn_Wl2_v': _L0_gnn_in['Wl2_v'], 'L0_gnn_Wa': _L0_gnn_in['Wa'], 'L1_gnn_W_skip0': _L1_gnn_in['W_skip0'], 'L1_gnn_W_skip1': _L1_gnn_in['W_skip1'], 'L1_gnn_W_nl0': _L1_gnn_in['W_nl0'], 'L1_gnn_W_nl1': _L1_gnn_in['W_nl1'], 'L1_gnn_W_fc1': _L1_gnn_in['W_fc1'], 'L1_gnn_W_fc2': _L1_gnn_in['W_fc2'], 'L1_gnn_W_out_s': _L1_gnn_in['W_out_s'], 'L1_gnn_W_out_v': _L1_gnn_in['W_out_v']}

def reference(x, src, dst, edge_attr_16, edge_attr_3, edge_attr_4, edge_attr_64, node_vec1, L0_gnn_Wfc1, L0_gnn_Wfc2, L0_gnn_Wsc0, L0_gnn_Wsc1, L0_gnn_Wl1_0, L0_gnn_Wl1_1, L0_gnn_Wl2_s, L0_gnn_Wl2_v, L0_gnn_Wa, L1_gnn_W_skip0, L1_gnn_W_skip1, L1_gnn_W_nl0, L1_gnn_W_nl1, L1_gnn_W_fc1, L1_gnn_W_fc2, L1_gnn_W_out_s, L1_gnn_W_out_v):
    import jax
    import jax.numpy as jnp

    def _L0_gnn_ref(x, node_attr, edge_scalars, edge_attr_sh, edge_src, edge_dst, Wfc1, Wfc2, Wsc0, Wsc1, Wl1_0, Wl1_1, Wl2_s, Wl2_v, Wa):
        import jax, jax.numpy as jnp
        import numpy as np
        N = 625
        E = 10000
        MUL0 = 64
        MUL1 = 32
        FC_IN = 16
        FC_H = 64
        WNUM = 192
        n = x.shape[0]
        x0 = x[:, :MUL0]
        x1 = x[:, MUL0:].reshape(n, MUL1, 3)
        a = node_attr
        h = jax.nn.silu(edge_scalars @ (Wfc1 / jnp.sqrt(jnp.float32(FC_IN))))
        w = h @ (Wfc2 / jnp.sqrt(jnp.float32(FC_H)))
        w0 = w[:, :64]
        w1 = w[:, 64:128]
        w2 = w[:, 128:160]
        w3 = w[:, 160:192]
        inv8 = 1.0 / jnp.sqrt(jnp.float32(MUL0))
        inv32 = 1.0 / jnp.sqrt(jnp.float32(MUL1))
        sc = jnp.concatenate([x0 @ Wsc0 * a * inv8, (jnp.einsum('num,uv->nvm', x1, Wsc1) * a[..., None] * inv32).reshape(n, 3 * MUL1)], axis=1)
        f0 = x0 @ Wl1_0 * a * inv8
        f1 = jnp.einsum('num,uv->nvm', x1, Wl1_1) * a[..., None] * inv32
        e0 = f0[edge_src]
        e1 = f1[edge_src]
        sh0 = edge_attr_sh[:, :1]
        sh1 = edge_attr_sh[:, 1:4]
        mid0 = w0 * e0 * sh0
        mid1 = w3 * jnp.einsum('eum,em->eu', e1, sh1) / jnp.sqrt(3.0)
        mid2 = w1[:, :, None] * e0[:, :, None] * sh1[:, None, :]
        mid3 = w2[:, :, None] * e1 * sh0[:, :, None]
        cnt = jnp.clip(jax.ops.segment_sum(jnp.ones(edge_dst.shape, x.dtype), edge_dst, num_segments=n), 1.0)

        def smean(v):
            s = jax.ops.segment_sum(v, edge_dst, num_segments=n)
            return s / cnt.reshape((n,) + (1,) * (v.ndim - 1))
        n0, n1 = (smean(mid0), smean(mid1))
        n2, n3 = (smean(mid2), smean(mid3))
        scal = jnp.concatenate([n0, n1], axis=1)
        vec = jnp.concatenate([n2, n3], axis=1)
        inv96 = 1.0 / jnp.sqrt(jnp.float32(MUL0 + MUL1))
        alpha = scal @ Wa * a * inv96
        out_s = scal @ Wl2_s * a * inv96
        out_v = jnp.einsum('num,uv->nvm', vec, Wl2_v) * a[..., None] * inv96
        conv = jnp.concatenate([out_s, out_v.reshape(n, 3 * MUL1)], axis=1)
        return sc + alpha * conv

    def _L1_gnn_ref(node_feature, edge_attr, edge_feature, W_skip0, W_skip1, W_nl0, W_nl1, W_fc1, W_fc2, W_out_s, W_out_v, edge_index):
        import jax, jax.numpy as jnp
        import numpy as np
        N_NODES = 10000
        N_EDGES = 10000
        MUL0, MUL1 = (64, 32)
        EDGE_DIM = 64
        W_NUMEL = 224
        DENOM = 32.0
        SQRT3 = 3.0 ** 0.5
        INV_SQRT3 = 1.0 / SQRT3
        INV_SQRT2 = 2.0 ** (-0.5)

        def _forward(node_feature, edge_attr, edge_feature, W_skip0, W_skip1, W_nl0, W_nl1, W_fc1, W_fc2, W_out_s, W_out_v, edge_index):
            N = node_feature.shape[0]
            E = edge_attr.shape[0]
            s = node_feature[:, :MUL0]
            v = node_feature[:, MUL0:].reshape(N, MUL1, 3)
            skip_s = s @ W_skip0
            skip_v = jnp.einsum('nmi,mk->nki', v, W_skip1)
            s = s @ W_nl0
            v = jnp.einsum('nmi,mk->nki', v, W_nl1)
            rhat = edge_attr / jnp.linalg.norm(edge_attr, axis=-1, keepdims=True)
            sh1 = SQRT3 * rhat
            w = jax.nn.relu(edge_feature @ W_fc1) @ W_fc2
            w0, w1, w2, w3, w4 = jnp.split(w, [64, 128, 160, 192], axis=-1)
            src, dst = (edge_index[0], edge_index[1])
            xs = s[dst]
            xv = v[dst]
            out0a = w0 * xs
            out0b = w3 * (jnp.einsum('emi,ei->em', xv, sh1) * INV_SQRT3)
            out1a = (w1 * xs)[:, :, None] * sh1[:, None, :]
            out1b = w2[:, :, None] * xv
            out1c = w4[:, :, None] * (jnp.cross(xv, sh1[:, None, :]) * INV_SQRT2)
            tp = jnp.concatenate([out0a, out0b, out1a.reshape(E, -1), out1b.reshape(E, -1), out1c.reshape(E, -1)], axis=-1)
            agg = jax.ops.segment_sum(tp, src, num_segments=N) / DENOM
            agg_s = agg[:, :96]
            agg_v = agg[:, 96:].reshape(N, 128, 3)
            out_s = agg_s @ W_out_s + skip_s
            out_v = jnp.einsum('nmi,mk->nki', agg_v, W_out_v) + skip_v
            fs = jax.nn.silu(out_s[:, :MUL0])
            gate = jax.nn.sigmoid(out_s[:, MUL0:MUL0 + 32])
            gv = gate[:, :, None] * out_v
            return jnp.concatenate([fs, gv.reshape(N, -1)], axis=-1)
        return _forward(node_feature, edge_attr, edge_feature, W_skip0, W_skip1, W_nl0, W_nl1, W_fc1, W_fc2, W_out_s, W_out_v, edge_index)
    edge_index = jnp.stack([src, dst])
    x = _layernorm(x + _L0_gnn_ref(x, node_vec1, edge_attr_16, edge_attr_4, src, dst, L0_gnn_Wfc1, L0_gnn_Wfc2, L0_gnn_Wsc0, L0_gnn_Wsc1, L0_gnn_Wl1_0, L0_gnn_Wl1_1, L0_gnn_Wl2_s, L0_gnn_Wl2_v, L0_gnn_Wa), axis=-1)
    x = _layernorm(x + _L1_gnn_ref(x, edge_attr_3, edge_attr_64, L1_gnn_W_skip0, L1_gnn_W_skip1, L1_gnn_W_nl0, L1_gnn_W_nl1, L1_gnn_W_fc1, L1_gnn_W_fc2, L1_gnn_W_out_s, L1_gnn_W_out_v, edge_index), axis=-1)
    return x

_drawn_inputs = setup_inputs


def setup_inputs(seed=0):
    import zlib

    import numpy as np

    out = dict(_drawn_inputs(seed))
    spreads = {}
    factors = {'edge_attr_16': 8.0,
     'edge_attr_4': 8.0,
     'L0_gnn_Wfc1': 8.0,
     'L0_gnn_Wfc2': 8.0,
     'L0_gnn_Wl1_0': 8.0,
     'L0_gnn_Wl1_1': 8.0,
     'L0_gnn_Wl2_s': 8.0,
     'L0_gnn_Wl2_v': 8.0,
     'L0_gnn_Wa': 8.0}
    for name, (base, spread) in spreads.items():
        noise = np.random.default_rng([zlib.crc32(name.encode()), seed]).standard_normal(out[name].shape)
        drawn = base * np.exp(spread * noise) if base else spread * noise
        out[name] = jnp.asarray(drawn.astype(out[name].dtype))
    for name, factor in factors.items():
        out[name] = (out[name] * factor).astype(out[name].dtype)
    return out
```

```python
from contextlib import ExitStack

import concourse.bass as bass
from concourse import mybir

F32 = mybir.dt.float32
I32 = mybir.dt.int32
ALU = mybir.AluOpType
ACT = mybir.ActivationFunctionType
AX = mybir.AxisListType

N = 3125
E = 100000
S, V = 64, 32
F = S + 3 * V
BN = 125
NB = N // BN
GB = 5
NG = NB // GB
EP = 125
EC = E // EP
TILE = 128
T = 4
STEP = T * TILE
NSTEP = NB + (E - NB) // STEP
UN = 4
CH = 16
NCH = EC // CH
MW = 480
CNT = 448
PW = 256
SIDE = 192
ROUND = 1.5 * 2 ** 23
EPS = 1e-5
assert NB * BN == N and EP * EC == E and NSTEP % UN == 0 and NCH * CH == EC and NCH % 2 == 0

ROWW = (22, 70)
SH = (17, 64)
IDX = (20, 68)
KEY = (21, 69)
KEEP = (F, SIDE)
OPS = (9, 14)
FIN = (13, 9)
ROOT = (11, 7)
N_W = 31


def gnn_kernel(nc, x, src, dst, edge_attr_16, edge_attr_3, edge_attr_4, edge_attr_64, node_vec1,
               Wfc1, Wfc2, Wsc0, Wsc1, Wl1_0, Wl1_1, Wl2_s, Wl2_v, Wa,
               W_skip0, W_skip1, W_nl0, W_nl1, W_fc1, W_fc2, W_out_s, W_out_v, out):
    with ExitStack() as ctx:
        def sb(name, shape, dt=F32):
            return ctx.enter_context(nc.sbuf_tensor(name, shape, dt))

        def sem(name):
            return ctx.enter_context(nc.semaphore(name))

        table = [nc.dram_tensor(f"table{k}", (N, F), F32).ap() for k in range(2)]
        ordered = [nc.dram_tensor(f"ordered{k}", (E + STEP, ROWW[k]), F32).ap() for k in range(2)]

        iota_i = sb("iota_i", [128, NSTEP], I32)
        part_i = sb("part_i", [128, 1], I32)
        iota = sb("iota", [128, NSTEP])
        part = sb("part", [128, 1])
        ident = sb("ident", [128, 128])
        below = sb("below", [128, 128])
        upto = sb("upto", [128, 128])
        ones = sb("ones", [128, 128])
        x_sb = sb("x_sb", [BN, NB * F])
        xp = sb("xp", [BN, NB * F])
        side = sb("side", [BN, NB * SIDE])
        acc = sb("acc", [BN, NB * MW])
        attr = sb("attr", [BN, NB])
        xn = sb("xn", [BN, GB, F])
        xT = sb("xT", [96, GB, 2, BN])
        st = sb("st", [BN, GB, MW])
        sT = sb("sT", [128, 2, 4 * BN])
        tm = sb("tm", [BN, GB, SIDE])
        y = sb("y", [BN, GB, F])
        fs = sb("fs", [BN, GB, 96])
        small = sb("small", [BN, 8, GB])
        stats = sb("stats", [BN, GB, 6])
        mv = sb("mv", [BN, GB, 2])
        raw_v = sb("raw_v", [96, 4, V])
        comp = sb("comp", [96, 3])
        comp3 = sb("comp3", [96, 3])
        raw_s = sb("raw_s", [S, 2, S])
        raw_fc2 = sb("raw_fc2", [128, 192])
        node_s = [sb("node_s0", [S, 2 * S]), sb("node_s1", [S, S + 96])]
        node_v = [sb("node_v0", [96, 192]), sb("node_v1", [96, 192])]
        fc1 = [sb("fc1_0", [S, 2, 128]), sb("fc1_1", [128, 128])]
        fc2 = [sb("fc2_0", [128, 192]), sb("fc2_1", [128, 224])]
        out_s = [sb("out_s0", [96, S + 1]), sb("out_s1", [96, 96])]
        out_v = [sb("out_v0", [96, V]), sb("out_v1", [128, V])]
        cnt = sb("cnt", [EP, 2, NB])
        viol = sb("viol", [EP, 1])
        tot = sb("tot", [NB, 2])
        nst = sb("nst", [NB, 2])
        cum = sb("cum", [NB, 2])
        wgt = sb("wgt", [NB, 2])
        big = sb("big", [NB, 1])
        isblk = sb("isblk", [NB, 128])
        totb = sb("totb", [NB, 2, 128])
        reach = sb("reach", [NB, 2, NSTEP])
        pre = sb("pre", [EP, 2, NB])
        blk125 = sb("blk125", [128, 2, NSTEP])
        start_f = sb("start_f", [1, NSTEP])
        start_i = [sb("start_i0", [1, NSTEP], I32), sb("start_i1", [1, NSTEP], I32)]
        accoff_i = [sb("accoff_i0", [1, NSTEP], I32), sb("accoff_i1", [1, NSTEP], I32)]
        flag_i = sb("flag_i", [1, 1], I32)
        at = [sb("at0", [EP, 2, CH], I32), sb("at1", [EP, 2, CH], I32)]
        rows = [sb("rows0", [128, UN, T * ROWW[0]]), sb("rows1", [128, UN, T * ROWW[1]])]
        gath = sb("gath", [128, UN, T * F])
        flat = sb("flat", [128, 2, T * 64])
        efT = sb("efT", [128, 2, 2 * 128])
        hT = sb("hT", [128, 2, 2, 128])
        msg = sb("msg", [128, 2, T, MW])
        hot = sb("hot", [128, 2, T, BN])
        kl = sb("kl", [128, T])
        tu = sb("tu", [128, T, 96])
        tq = sb("tq", [128, T, S])
        ta = sb("ta", [128, T, 3 * V])
        tb = sb("tb", [128, T, 3 * V])
        td = sb("td", [128, T, V])

        def carve(whole, at_, *shape):
            n = 1
            for s in shape:
                n *= s
            flat = whole[0:EP, at_:at_ + n]
            return flat if len(shape) == 1 else flat.rearrange(
                "p (a b) -> p a b" if len(shape) == 2 else "p (a b c) -> p a b c",
                **dict(zip("abc", shape)))

        dst_i = acc[:, 0:EC].bitcast(I32)
        src_i = acc[:, EC:2 * EC].bitcast(I32)
        key_i = [dst_i, src_i]
        next_i = acc[:, 2 * EC:3 * EC].bitcast(I32)
        blk = [acc[:, 3 * EC:4 * EC], acc[:, 4 * EC:5 * EC]]
        oh = acc[:, 5 * EC:6 * EC]
        run = acc[:, 6 * EC:7 * EC]
        tmp = acc[:, 7 * EC:8 * EC]
        pos_f = acc[:, 8 * EC:9 * EC]
        pos_i = [acc[:, 9 * EC:10 * EC].bitcast(I32), acc[:, 10 * EC:11 * EC].bitcast(I32)]
        sh_all = acc[:, 11 * EC:14 * EC].rearrange("p (c m) -> p c m", m=3)
        ones_row = acc[:, 14 * EC:15 * EC]
        ea3 = st[:, :, :].rearrange("p g w -> p (g w)").rearrange("p (c m) -> p c m", m=3)
        gflat = gath[:, :, :].rearrange("p u w -> p (u w)")
        mflat = msg[:, :, :, :].rearrange("p b t w -> p (b t w)")
        row = [carve(mflat, 2688, 2, CH, ROWW[0]), carve(gflat, 0, 2, CH, ROWW[1])]
        in64 = carve(mflat, 0, 2, CH, 64)
        in16 = carve(mflat, 2048, 2, CH, 16)
        in4 = carve(mflat, 2560, 2, CH, 4)

        pw = ctx.enter_context(nc.psum_tensor("pw", [128, 2, T, PW], F32))
        pz = ctx.enter_context(nc.psum_tensor("pz", [128, 2, 512], F32))
        pa = ctx.enter_context(nc.psum_tensor("pa", [128, 2, 512], F32))
        po = pw[0:BN, :, :, :].rearrange("p b t w -> p (b t) w")[:, 0:GB, :]

        s_keys = sem("s_keys")
        s_x = sem("s_x")
        s_e3 = sem("s_e3")
        s_w = sem("s_w")
        s_iota = sem("s_iota")
        s_const = sem("s_const")
        s_zero = sem("s_zero")
        s_kron = sem("s_kron")
        s_scaled = sem("s_scaled")
        s_sort = sem("s_sort")
        s_count = sem("s_count")
        s_cnt = sem("s_cnt")
        s_tot = sem("s_tot")
        s_nst = sem("s_nst")
        s_cum = sem("s_cum")
        s_reach = sem("s_reach")
        s_tab = sem("s_tab")
        s_tabs = sem("s_tabs")
        s_flag = sem("s_flag")
        s_posd = sem("s_posd")
        s_pd = sem("s_pd")
        s_pdd = sem("s_pdd")
        s_ps = sem("s_ps")
        s_poss = sem("s_poss")
        s_sq = sem("s_sq")
        s_len = sem("s_len")
        s_shd = sem("s_shd")
        s_tail = sem("s_tail")
        s_tailw = sem("s_tailw")
        s_load = [sem("s_load0"), sem("s_load1")]
        s_made = sem("s_made")
        s_row0 = [sem("s_row00"), sem("s_row01")]
        s_row1 = [sem("s_row10"), sem("s_row11")]
        s_clear = sem("s_clear")
        s_table = [sem("s_table0"), sem("s_table1")]
        s_out = sem("s_out")
        passed = [sem("passed_sp"), sem("passed_pool"), sem("passed_dve"), sem("passed_pe")]
        s_xn = [sem("s_xn0"), sem("s_xn1")]
        s_xt = [sem("s_xt0"), sem("s_xt1")]
        s_xc = [sem("s_xc0"), sem("s_xc1")]
        s_mm = [sem("s_mm0"), sem("s_mm1")]
        s_ev = [sem("s_ev0"), sem("s_ev1")]
        s_st = [sem("s_st0"), sem("s_st1")]
        s_at = [sem("s_at0"), sem("s_at1")]
        s_ac = [sem("s_ac0"), sem("s_ac1")]
        s_ao = [sem("s_ao0"), sem("s_ao1")]
        s_fin = [sem("s_fin0"), sem("s_fin1")]
        s_act = [sem("s_act0"), sem("s_act1")]
        s_rt = [sem("s_rt0"), sem("s_rt1")]
        s_put = sem("s_put")
        rows_in = [[sem(f"rows_in{k}{u}") for u in range(UN)] for k in range(2)]
        gathered = [[sem(f"gathered{k}{u}") for u in range(UN)] for k in range(2)]
        flattened = [sem("flattened0"), sem("flattened1")]
        transposed = [sem("transposed0"), sem("transposed1")]
        copied = [sem("copied0"), sem("copied1")]
        hidden = [sem("hidden0"), sem("hidden1")]
        activated = [sem("activated0"), sem("activated1")]
        weighted = [sem("weighted0"), sem("weighted1")]
        products = [sem("products0"), sem("products1")]
        scattered = [sem("scattered0"), sem("scattered1")]
        added = [sem("added0"), sem("added1")]

        block = ctx.enter_context(nc.Block())

        def turns(eng, body, after):
            for u in range(UN):
                body(u, u, 0)
            with eng.Fori(1, NSTEP // UN) as i:
                for u in range(UN):
                    body(i * UN + u, u, i)
            for s in range(NSTEP, NSTEP + after):
                body(s, s % UN, s // UN)

        def groups(eng, body):
            body(0)
            with eng.Fori(1, NG) as g:
                body(g)

        def group_of(t, g, width):
            return t[:, bass.ds(g * (GB * width), GB * width)].rearrange("p (b w) -> p b w", w=width)

        @block.sync
        def _(sp):
            last = EC - 1
            kd = dst.rearrange("(p c) -> p c", p=EP)
            ks = src.rearrange("(p c) -> p c", p=EP)
            sp.dma_start(dst_i, kd).then_inc(s_keys, 16)
            sp.dma_start(src_i, ks).then_inc(s_keys, 16)
            nxt = dst[1:1 + (EP - 1) * EC].rearrange("(p c) -> p c", p=EP - 1)
            sp.wait_ge(s_sort, 1)
            sp.dma_start(next_i[0:EP - 1, :], nxt).then_inc(s_keys, 16)
            sp.dma_start(next_i[EP - 1:EP, 0:last], dst[E - EC + 1:E].rearrange("(a c) -> a c", a=1)).then_inc(s_keys, 16)
            sp.dma_start(x_sb[:, :].rearrange("p (b f) -> p b f", f=F), x.rearrange("(b p) f -> p b f", p=BN)).then_inc(s_x, 16)
            with nc.allow_non_contiguous_dma(reason="one number of each node"):
                sp.dma_start(attr[:, :].unsqueeze(2), node_vec1.rearrange("(b p) f -> p b f", p=BN)).then_inc(s_x, 16)
            sp.dma_start(st[:, :, :].rearrange("p g w -> p (g w)"), edge_attr_3.rearrange("(p c) m -> p (c m)", p=EP)).then_inc(s_e3, 16)
            for k, w in enumerate((Wl1_1, Wsc1, W_nl1, W_skip1)):
                for m in range(3):
                    sp.dma_start(raw_v[m:96:3, k, :], w).then_inc(s_w, 16)
            sp.dma_start(raw_s[:, 0, :], Wl1_0).then_inc(s_w, 16)
            sp.dma_start(raw_s[:, 1, :], Wsc0).then_inc(s_w, 16)
            sp.dma_start(node_s[1][:, 0:S], W_nl0).then_inc(s_w, 16)
            sp.dma_start(node_s[1][:, S:S + 96], W_skip0).then_inc(s_w, 16)
            for h in range(2):
                sp.dma_start(raw_fc2[S * h:S * h + S, :], Wfc2).then_inc(s_w, 16)
                sp.dma_start(fc2[1][S * h:S * h + S, :], W_fc2).then_inc(s_w, 16)
            sp.dma_start(out_s[0][:, 0:S], Wl2_s).then_inc(s_w, 16)
            sp.dma_start(out_s[0][:, S:S + 1], Wa).then_inc(s_w, 16)
            sp.dma_start(out_v[0][:, :], Wl2_v).then_inc(s_w, 16)
            sp.dma_start(out_s[1][:, :], W_out_s).then_inc(s_w, 16)
            sp.dma_start(out_v[1][:, :], W_out_v).then_inc(s_w, 16)
            sp.wait_ge(s_zero, 1)
            for t in range(T):
                sp.dma_start(fc1[0][16 * t:16 * t + 16, t % 2, S * (t // 2):S * (t // 2) + S], Wfc1).then_inc(s_w, 16)
            for h in range(2):
                sp.dma_start(fc1[1][S * h:S * h + S, S * h:S * h + S], W_fc1).then_inc(s_w, 16)
            sp.wait_ge(s_tail, 1)
            for k in range(2):
                for q in range(T):
                    dram = ordered[k][E + q * TILE:E + (q + 1) * TILE, :]
                    sp.dma_start(dram, rows[k][:, 0, 0:ROWW[k]]).then_inc(s_tailw, 16)

            d16 = edge_attr_16.rearrange("(p c) f -> p (c f)", p=EP)
            d4 = edge_attr_4.rearrange("(p c) f -> p (c f)", p=EP)
            d64 = edge_attr_64.rearrange("(p c) f -> p (c f)", p=EP)
            o0 = ordered[0][0:E, :].rearrange("(p c) w -> p (c w)", p=EP)

            def load(j, u):
                for t, d, w in ((in16, d16, 16), (in4, d4, 4), (in64, d64, 64)):
                    sp.dma_start(t[:, u, :, :].rearrange("p c w -> p (c w)"),
                                 d[:, bass.ds(j * (CH * w), CH * w)]).then_inc(s_load[u], 16)

            def store(j, u):
                sp.wait_ge(s_made, j + 1)
                sp.sem_inc(passed[0], 1)
                with sp.If(unsorted == 0):
                    n = CH // 2 * ROWW[0]
                    for h in range(2):
                        sp.dma_start(o0[:, bass.ds(j * (2 * n) + h * n, n)],
                                     row[0][:, u, :, :].rearrange("p c w -> p (c w)")[:, h * n:h * n + n]).then_inc(s_row0[u], 8 * CH)

            sp.wait_ge(s_flag, 1)
            unsorted = sp.value_load(flag_i[0:1, 0:1], min_val=0, max_val=E)
            load(0, 0)
            load(1, 1)
            with sp.Fori(0, NCH // 2 - 1) as i:
                for u in range(2):
                    store(i * 2 + u, u)
                    load(i * 2 + u + 2, u)
            for u in range(2):
                store(NCH - 2 + u, u)
            for u in range(2):
                sp.wait_ge(s_row0[u], 16 * CH * (NCH // 2))
                sp.wait_ge(s_row1[u], 16 * CH * (NCH // 2))
            sp.wait_ge(s_tailw, 16 * 2 * T)

            def put_table(k, staging):
                sp.wait_ge(s_ev[k], 2 * NB)
                sp.dma_start(table[k].rearrange("(b p) f -> p b f", p=BN),
                             staging[:, :].rearrange("p (b f) -> p b f", f=F)).then_inc(s_table[k], 16)

            def edge_rows(k):
                flat = ordered[k].rearrange("e w -> (e w)")
                n = STEP * ROWW[k]

                def body(s, u, turn):
                    if not (isinstance(turn, int) and turn == 0):
                        sp.wait_ge(products[k], s * OPS[k] - (UN - 1) * OPS[k])
                    at_ = sp.value_load(start_i[k][0:1, bass.ds(s, 1)], min_val=0, max_val=E * ROWW[k])
                    sp.dma_start(rows[k][:, u, :], flat[bass.ds(at_, n)].rearrange("(p w) -> p w", p=128)).then_inc(rows_in[k][u], 16)
                turns(sp, body, 0)

            put_table(0, xp)
            edge_rows(0)
            put_table(1, x_sb)
            edge_rows(1)

            def put(g):
                sp.wait_ge(s_fin[1], (g + 1) * FIN[1])
                sp.dma_start(out.rearrange("(b p) f -> p b f", p=BN)[:, bass.ds(g * GB, GB), :], xn[:, :, :]).then_inc(s_put, 16)
            groups(sp, put)
            sp.wait_ge(s_put, 16 * NG)

        @block.gpsimd
        def _(pool):
            nc.gpsimd.iota(iota_i[:, :], [[1, NSTEP]], base=0, channel_multiplier=0).then_inc(s_iota, 1)
            nc.gpsimd.iota(part_i[:, :], [[1, 1]], base=0, channel_multiplier=1).then_inc(s_iota, 1)
            pool.wait_ge(s_flag, 1)
            unsorted = pool.value_load(flag_i[0:1, 0:1], min_val=0, max_val=E)
            pool.wait_ge(s_posd, 1)
            pool.wait_ge(s_poss, 1)

            def scatter(k, u, done):
                for c in range(CH):
                    pool.indirect_dma_start(ordered[k][0:E, :], bass.IndirectOffsetOnAxis(ap=at[k][:, u, c:c + 1], axis=0),
                                            row[k][:, u, c, :], None).then_inc(done, 16)

            with pool.Fori(0, NCH // 2) as i:
                for u in range(2):
                    pool.wait_ge(s_made, i * 2 + u + 1)
                    pool.sem_inc(passed[1], 1)
                    scatter(1, u, s_row1[u])
                    with pool.If(unsorted != 0):
                        scatter(0, u, s_row0[u])
            for u in range(2):
                pool.wait_ge(s_row1[u], 16 * CH * (NCH // 2))
                pool.wait_ge(s_row0[u], 16 * CH * (NCH // 2))

            def edge_gather(k):
                pool.wait_ge(s_table[k], 16)

                def body(s, u, turn):
                    pool.wait_ge(rows_in[k][u], (turn + 1) * 16)
                    if not (isinstance(turn, int) and turn == 0):
                        pool.wait_ge(products[k], s * OPS[k] - (UN - 1) * OPS[k])
                    pool.sem_inc(passed[1], 1)
                    for t in range(T):
                        i_ap = rows[k][:, u, t * ROWW[k] + IDX[k]:t * ROWW[k] + IDX[k] + 1].bitcast(I32)
                        pool.indirect_dma_start(gath[:, u, t * F:(t + 1) * F], None, table[k],
                                                bass.IndirectOffsetOnAxis(ap=i_ap, axis=0)).then_inc(gathered[k][u], 16)
                turns(pool, body, 0)
            edge_gather(0)
            edge_gather(1)

        def node_columns(k):
            w = node_s[k].shape[1]
            return [(node_s[k][:, 0:S], 0, 0), (node_v[k][:, 0:96], 1, S),
                    (node_s[k][:, S:w], 0, F), (node_v[k][:, 96:192], 1, F + w - S)]

        @block.tensor
        def _(pe):
            def mm(o, l, r, start=True, stop=True):
                return nc.tensor.matmul(o, l, r, start=start, stop=stop)

            def node_prep_group(k, g):
                pe.wait_ge(s_xn[k], g + 1)
                first = isinstance(g, int) and g == 0
                for j in range(GB):
                    if not (first and j < 1):
                        pe.wait_ge(s_xc[k], g * GB + max(j - 1, 0))
                    pe.sem_inc(passed[3], 1)
                    nc.tensor.transpose(pz[0:S, j % 2, 0:BN], xn[:, j, 0:S], ident[0:BN, 0:BN])
                    nc.tensor.transpose(pz[0:96, j % 2, 128:128 + BN], xn[:, j, S:F],
                                        ident[0:BN, 0:BN]).then_inc(s_xt[k], 1)
                for j in range(GB):
                    pe.wait_ge(s_xc[k], g * GB + j + 1)
                    if not (first and j < 1):
                        pe.wait_ge(s_ev[k], g * (2 * GB) + 2 * max(j - 1, 0))
                    for n, (w, c, col) in enumerate(node_columns(k)):
                        rws = S if c == 0 else 96
                        last = mm(pa[0:BN, j % 2, col:col + w.shape[1]], xT[0:rws, j, c, :], w)
                    last.then_inc(s_mm[k], 1)

            def finish_group(k, g):
                first = isinstance(g, int) and g == 0
                vw = 96 if k == 0 else 128
                pe.wait_ge(s_st[k], g + 1)
                for j in range(GB + 1):
                    if j < GB:
                        if not (first and j < 1):
                            pe.wait_ge(s_ac[k], g * GB + max(j - 1, 0))
                        nc.tensor.transpose(pz[0:96, j % 2, 0:BN], st[:, j, 0:96], ident[0:BN, 0:BN])
                        for m in range(3):
                            last = nc.tensor.transpose(pz[0:vw, j % 2, BN * (m + 1):BN * (m + 2)],
                                                       st[:, j, 96 + vw * m:96 + vw * (m + 1)], ident[0:BN, 0:BN])
                        last.then_inc(s_at[k], 1)
                    if j >= 1:
                        q = j - 1
                        pe.wait_ge(s_ac[k], g * GB + q + 1)
                        sw = S if k == 0 else 96
                        mm(po[:, q, 0:sw], sT[0:96, q % 2, 0:BN], out_s[k][:, 0:sw])
                        if k == 0:
                            mm(po[:, q, F:F + 1], sT[0:96, q % 2, 0:BN], out_s[0][:, S:S + 1])
                        for m in range(3):
                            last = mm(po[:, q, sw + V * m:sw + V * (m + 1)], sT[0:vw, q % 2, BN * (m + 1):BN * (m + 2)],
                                      out_v[k][0:vw, :])
                        last.then_inc(s_ao[k], 1)

            def edge_loop(k):
                w1, w2 = fc1[k], fc2[k]
                ww = w2.shape[1]
                ew = 16 if k == 0 else 64

                def is_step(s):
                    return not isinstance(s, int) or 0 <= s < NSTEP

                def body(s, u, turn):
                    if is_step(s):
                        pe.wait_ge(flattened[k], s + 1)
                        if not (isinstance(s, int) and s < 1):
                            pe.wait_ge(copied[k], s)
                        pe.sem_inc(passed[3], 1)
                        if k == 0:
                            last = nc.tensor.transpose(pz[0:T * ew, 0, 0:128], flat[:, u % 2, 0:T * ew], ident[:, :])
                        else:
                            for j in range(2):
                                last = nc.tensor.transpose(pz[:, 0, 128 * j:128 * (j + 1)], flat[:, u % 2, 128 * j:128 * (j + 1)], ident[:, :])
                        last.then_inc(transposed[k], 1)
                    s1, b1 = s - 1, (u + 1) % 2
                    if is_step(s1):
                        pe.wait_ge(copied[k], s1 + 1)
                        if not (isinstance(s1, int) and s1 < 1):
                            pe.wait_ge(activated[k], s1)
                        if k == 0:
                            for j in range(2):
                                last = mm(pz[:, 1, 128 * j:128 * (j + 1)], w1[:, j, :], efT[0:S, b1, 0:128])
                        else:
                            last = mm(pz[:, 1, 0:256], w1[:, :], efT[:, b1, :])
                        last.then_inc(hidden[k], 1)
                    s2, b2 = s - 2, u % 2
                    if is_step(s2):
                        pe.wait_ge(activated[k], s2 + 1)
                        if not (isinstance(s2, int) and s2 < 2):
                            pe.wait_ge(products[k], s2 * OPS[k] - OPS[k])
                        for t in range(T):
                            h = S * (t // 2)
                            last = mm(pw[:, b2, t, 0:ww], hT[h:h + S, b2, t % 2, :], w2[h:h + S, :])
                        last.then_inc(weighted[k], 1)
                    s3, b3 = s - 3, (u + 1) % 2
                    if is_step(s3):
                        pe.wait_ge(products[k], s3 * OPS[k] + OPS[k])
                        if not (isinstance(s3, int) and s3 < 2):
                            pe.wait_ge(added[k], s3 - 1)
                        mw = CNT + 1 if k == 0 else MW
                        for t in range(T):
                            last = mm(pa[0:BN, b3, 0:mw], hot[:, b3, t, :], msg[:, b3, t, 0:mw], start=(t == 0), stop=(t == T - 1))
                        last.then_inc(scattered[k], 1)
                turns(pe, body, 3)

            pe.wait_ge(s_const, 1)
            pe.wait_ge(s_cnt, 1)
            for k in range(2):
                mm(pa[0:NB, 0, k:k + 1], cnt[:, k, :], ones[0:EP, 0:1])
            mm(pa[0:1, 0, 8:9], viol[:, :], ones[0:EP, 0:1]).then_inc(s_tot, 1)
            pe.wait_ge(s_nst, 1)
            mm(pa[0:NB, 0, 16:18], upto[0:NB, 0:NB], nst[:, :]).then_inc(s_cum, 1)
            pe.wait_ge(s_reach, 1)
            for k in range(2):
                mm(pa[0:1, k, 32:32 + NSTEP], wgt[:, k:k + 1], reach[:, k, :])
                mm(pa[:, k, 256:256 + NSTEP], isblk[:, :], reach[:, k, :])
                mm(pz[0:EP, k, 0:NB], below[0:EP, 0:EP], cnt[:, k, :], stop=False)
                last = mm(pz[0:EP, k, 0:NB], totb[:, k, 0:EP], below[0:NB, 0:NB], start=False)
            last.then_inc(s_tab, 1)

            pe.wait_ge(s_tabs, 1)
            pe.wait_ge(s_w, 16 * N_W)
            pe.wait_ge(s_scaled, 1)
            groups(pe, lambda g: node_prep_group(0, g))
            pe.wait_ge(s_ev[0], 2 * NB)
            edge_loop(0)
            pe.wait_ge(added[0], NSTEP)

            def between(g):
                finish_group(0, g)
                node_prep_group(1, g)
            groups(pe, between)
            pe.wait_ge(s_ev[1], 2 * NB)
            edge_loop(1)
            pe.wait_ge(added[1], NSTEP)
            groups(pe, lambda g: finish_group(1, g))

        @block.scalar
        def _(act):
            def node_prep_group(k, g):
                first = isinstance(g, int) and g == 0
                for j in range(GB):
                    act.wait_ge(s_xt[k], g * GB + j + 1)
                    if not first:
                        act.wait_ge(s_mm[k], g * GB + j + 1 - GB)
                    nc.scalar.copy(xT[0:S, j, 0, :], pz[0:S, j % 2, 0:BN])
                    nc.scalar.copy(xT[:, j, 1, :], pz[0:96, j % 2, 128:128 + BN]).then_inc(s_xc[k], 1)
                staging = xp if k == 0 else x_sb
                for j in range(GB):
                    act.wait_ge(s_mm[k], g * GB + j + 1)
                    b = g * GB + j
                    t_out = staging[:, bass.ds(b * F, F)]
                    s_out_ = side[:, bass.ds(b * SIDE, KEEP[k])]
                    if k == 0:
                        a = attr[:, bass.ds(b, 1)]
                        nc.scalar.activation(t_out, pa[0:BN, j % 2, 0:F], ACT.Copy, scale=a).then_inc(s_ev[k], 1)
                        nc.scalar.activation(s_out_, pa[0:BN, j % 2, F:F + KEEP[k]], ACT.Copy, scale=a).then_inc(s_ev[k], 1)
                    else:
                        nc.scalar.copy(t_out, pa[0:BN, j % 2, 0:F]).then_inc(s_ev[k], 1)
                        nc.scalar.copy(s_out_, pa[0:BN, j % 2, F:F + KEEP[k]]).then_inc(s_ev[k], 1)

            def finish_group(k, g):
                first = isinstance(g, int) and g == 0
                for j in range(GB):
                    act.wait_ge(s_at[k], g * GB + j + 1)
                    if not (first and j < 2):
                        act.wait_ge(s_ao[k], g * GB + j - 1 if j >= 2 else g * GB)
                    if k == 0:
                        nc.scalar.copy(sT[0:96, j % 2, :], pz[0:96, j % 2, 0:4 * BN]).then_inc(s_ac[k], 1)
                    else:
                        nc.scalar.copy(sT[0:96, j % 2, 0:BN], pz[0:96, j % 2, 0:BN])
                        nc.scalar.copy(sT[:, j % 2, BN:4 * BN], pz[:, j % 2, BN:4 * BN]).then_inc(s_ac[k], 1)
                if k == 1:
                    act.wait_ge(s_fin[1], g * FIN[1] + 2)
                    nc.scalar.activation(fs[:, :, 0:S], tm[:, :, 0:S], ACT.Silu)
                    nc.scalar.activation(fs[:, :, S:96], tm[:, :, S:96], ACT.Sigmoid).then_inc(s_act[1], 1)
                act.wait_ge(s_fin[k], g * FIN[k] + ROOT[k])
                nc.scalar.activation(small[:, 6, :], small[:, 5, :], ACT.Sqrt).then_inc(s_rt[k], 1)

            def edge_loop(k):
                def is_step(s):
                    return not isinstance(s, int) or 0 <= s < NSTEP

                ew = 16 if k == 0 else 64

                def body(s, u, turn):
                    if is_step(s):
                        act.wait_ge(rows_in[k][u], (turn + 1) * 16)
                        if not (isinstance(s, int) and s < 2):
                            act.wait_ge(transposed[k], s - 1)
                        if k == 0:
                            f = flat[:, u % 2, 0:T * ew].rearrange("p (t w) -> p t w", t=T)
                            r = rows[k][:, u, :].rearrange("p (t w) -> p t w", t=T)[:, :, 0:ew]
                        else:
                            f = flat[:, u % 2, :].rearrange("p (j h w) -> p j h w", j=2, h=2)
                            r = rows[k][:, u, :].rearrange("p (h j w) -> p j h w", h=2, j=2)[:, :, :, 0:ew]
                        nc.scalar.copy(f, r).then_inc(flattened[k], 1)
                    s1, b1 = s - 1, (u + 1) % 2
                    if is_step(s1):
                        act.wait_ge(transposed[k], s1 + 1)
                        if not (isinstance(s1, int) and s1 < 2):
                            act.wait_ge(hidden[k], s1 - 1)
                        if k == 0:
                            nc.scalar.copy(efT[0:S, b1, 0:128], pz[0:S, 0, 0:128]).then_inc(copied[k], 1)
                        else:
                            nc.scalar.copy(efT[:, b1, :], pz[:, 0, 0:256]).then_inc(copied[k], 1)
                    s2, b2 = s - 2, u % 2
                    if is_step(s2):
                        act.wait_ge(hidden[k], s2 + 1)
                        if not (isinstance(s2, int) and s2 < 2):
                            act.wait_ge(weighted[k], s2 - 1)
                        h = hT[:, b2, :, :].rearrange("p j e -> p (j e)")
                        if k == 0:
                            nc.scalar.activation(h, pz[:, 1, 0:256], ACT.Silu, scale=0.25).then_inc(activated[k], 1)
                        else:
                            nc.scalar.activation(h, pz[:, 1, 0:256], ACT.Relu).then_inc(activated[k], 1)
                turns(act, body, 2)

            act.wait_ge(s_w, 16 * N_W)
            act.wait_ge(s_const, 1)
            inv8, inv32 = S ** -0.5, V ** -0.5
            nc.scalar.mul(node_s[0][:, 0:S], raw_s[:, 0, :], inv8)
            nc.scalar.mul(node_s[0][:, S:2 * S], raw_s[:, 1, :], inv8)
            for m in range(3):
                is_m = comp[:, m:m + 1]
                nc.scalar.activation(node_v[0][:, V * m:V * m + V], raw_v[:, 0, :], ACT.Copy, scale=is_m)
                nc.scalar.activation(node_v[0][:, 96:192].rearrange("p (v m) -> p v m", m=3)[:, :, m], raw_v[:, 1, :], ACT.Copy, scale=is_m)
                nc.scalar.activation(node_v[1][:, V * m:V * m + V], raw_v[:, 2, :], ACT.Copy, scale=is_m)
                last = nc.scalar.activation(node_v[1][:, 96 + V * m:96 + V * m + V], raw_v[:, 3, :], ACT.Copy, scale=is_m)
                if m == 2:
                    last.then_inc(s_kron, 1)
            act.wait_ge(s_kron, 1)
            nc.scalar.mul(node_v[0][:, :], node_v[0][:, :], inv32)
            for o, i, w in ((0, 0, 64), (64, 128, 32), (96, 64, 64), (160, 160, 32)):
                nc.scalar.mul(fc2[0][:, o:o + w], raw_fc2[:, i:i + w], inv8)
            for k, w in ((0, S + 1), (1, 96)):
                nc.scalar.mul(out_s[k][S:96, 0:w], out_s[k][S:96, 0:w], 3 ** -0.5)
            nc.scalar.mul(out_v[1][96:128, :], out_v[1][96:128, :], 2 ** -0.5).then_inc(s_scaled, 1)

            act.wait_ge(s_x, 32)

            def prep(g):
                if not (isinstance(g, int) and g == 0):
                    act.wait_ge(s_xt[0], g * GB)
                nc.scalar.copy(xn[:, :, :], group_of(x_sb, g, F)).then_inc(s_xn[0], 1)
                node_prep_group(0, g)

            act.wait_ge(s_sq, 1)
            nc.scalar.activation(run, tmp, ACT.Sqrt).then_inc(s_len, 1)
            groups(act, prep)

            act.wait_ge(s_shd, 1)
            act.wait_ge(s_posd, 1)
            act.wait_ge(s_poss, 1)

            def assemble(j, u, turn):
                act.wait_ge(s_load[u], (turn + 1) * 48)
                if not (isinstance(turn, int) and turn == 0):
                    act.wait_ge(s_row0[u], turn * (16 * CH))
                    act.wait_ge(s_row1[u], turn * (16 * CH))
                c = bass.ds(j * CH, CH)
                r0, r1 = row[0][:, u, :, :], row[1][:, u, :, :]
                nc.scalar.copy(r1[:, :, 0:64], in64[:, u, :, :])
                nc.scalar.copy(r0[:, :, 0:16], in16[:, u, :, :])
                nc.scalar.copy(r0[:, :, 16:20], in4[:, u, :, :])
                nc.scalar.copy(r1[:, :, 64:67], sh_all[:, c, :])
                nc.scalar.copy(r1[:, :, 67:68], sh_all[:, c, 0:1])
                for k, r in ((0, r0), (1, r1)):
                    ri = r.bitcast(I32)
                    nc.scalar.copy(ri[:, :, IDX[k]:IDX[k] + 1], key_i[1 - k][:, c].unsqueeze(2))
                    nc.scalar.copy(ri[:, :, KEY[k]:KEY[k] + 1], key_i[k][:, c].unsqueeze(2))
                    last = nc.scalar.copy(at[k][:, u, :], pos_i[k][:, c])
                last.then_inc(s_made, 1)
            for u in range(2):
                assemble(u, u, 0)
            with act.Fori(1, NCH // 2) as i:
                for u in range(2):
                    assemble(i * 2 + u, u, i)

            edge_loop(0)

            def between(g):
                finish_group(0, g)
                node_prep_group(1, g)
            groups(act, between)
            edge_loop(1)
            groups(act, lambda g: finish_group(1, g))

        @block.vector
        def _(dve):
            chain = [0]

            def link(ins):
                chain[0] += 1
                ins.then_inc(s_sort, 1)
                dve.wait_ge(s_sort, chain[0])

            tt, ts, stt, cp = nc.vector.tensor_tensor, nc.vector.tensor_scalar, nc.vector.scalar_tensor_tensor, nc.vector.tensor_copy
            link(nc.vector.memset(next_i[:, EC - 1:EC], N))
            nc.vector.memset(fc1[0][:, :, :], 0.0)
            nc.vector.memset(fc1[1][:, :], 0.0).then_inc(s_zero, 1)
            nc.vector.memset(ones_row, 1.0)
            nc.vector.memset(ones[:, :], 1.0)
            for k in range(2):
                link(nc.vector.memset(rows[k][:, 0, 0:ROWW[k]], 0.0))
            for k in range(2):
                last = nc.vector.memset(rows[k][:, 0, KEY[k]:KEY[k] + 1].bitcast(I32), 2 * N)
            last.then_inc(s_tail, 1)
            link(nc.vector.memset(pos_i[0], 0))
            dve.wait_ge(s_iota, 2)
            cp(iota[:, :], iota_i[:, :])
            link(cp(part[:, :], part_i[:, :]))
            r96 = part[0:96, 0:1].to_broadcast([96, 3])
            link(ts(comp3[:, :], r96, 1.0 / 3, -1.0 / 3, ALU.mult, ALU.add))
            link(ts(comp3[:, :], comp3[:, :], ROUND, ROUND, ALU.add, ALU.subtract))
            link(stt(comp3[:, :], comp3[:, :], 3.0, iota[0:96, 0:3], ALU.mult, ALU.add))
            ts(comp[:, :], comp3[:, :], part[0:96, 0:1], None, ALU.is_equal)
            ts(ident[:, :], iota[:, 0:128], part[:, 0:1], None, ALU.is_equal)
            ts(below[:, :], iota[:, 0:128], part[:, 0:1], None, ALU.is_gt)
            ts(upto[:, :], iota[:, 0:128], part[:, 0:1], None, ALU.is_ge).then_inc(s_const, 1)
            ts(big[:, :], part[0:NB, :], NB - 1.0, 1e6, ALU.is_equal, ALU.mult)
            ts(isblk[:, :], part[0:NB, 0:1].to_broadcast([NB, 128]), NB - 1.0, None, ALU.is_lt)
            dve.wait_ge(s_keys, 64)
            for k in range(2):
                link(ts(oh, key_i[k], 1.0 / BN, 0.5 / BN - 0.5, ALU.mult, ALU.add))
                link(ts(blk[k], oh, ROUND, ROUND, ALU.add, ALU.subtract))
            junk = (tmp, run)

            def count(b, first):
                for k in range(2):
                    if not first:
                        dve.wait_ge(s_count, b * 2 + k - 1)
                    ts(junk[k], blk[k], iota[0:EP, bass.ds(b, 1)], 0.0, ALU.is_equal, ALU.add,
                       accum_out=cnt[:, k, bass.ds(b, 1)]).then_inc(s_count, 1)
            count(0, True)
            with dve.Fori(1, NB) as b:
                count(b, False)
            dve.wait_ge(s_count, 2 * NB)
            link(tt(tmp, dst_i, next_i, ALU.is_gt))
            nc.vector.reduce_sum(viol[:, :], tmp, AX.X).then_inc(s_cnt, 1)
            dve.wait_ge(s_tot, 1)
            cp(flag_i[0:1, 0:1], pa[0:1, 0, 8:9]).then_inc(s_flag, 1)
            link(cp(tot[:, :], pa[0:NB, 0, 0:2]))
            link(ts(nst[:, :], tot[:, :], 1.0 / STEP, (STEP - 1.0) / STEP - 0.5 + 0.5 / STEP, ALU.mult, ALU.add))
            ts(nst[:, :], nst[:, :], ROUND, ROUND, ALU.add, ALU.subtract).then_inc(s_nst, 1)
            dve.wait_ge(s_nst, 1)
            link(stt(wgt[:, :], nst[:, :], -float(STEP), tot[:, :], ALU.mult, ALU.add))
            link(ts(wgt[:, :], wgt[:, :], big[:, 0:1], None, ALU.add))
            dve.wait_ge(s_cum, 1)
            link(cp(cum[:, :], pa[0:NB, 0, 16:18]))
            for k in range(2):
                ts(totb[:, k, :], ones[0:NB, :], tot[:, k:k + 1], None, ALU.mult)
                last = ts(reach[:, k, :], iota[0:NB, :], cum[:, k:k + 1], None, ALU.is_ge)
            last.then_inc(s_reach, 1)
            dve.wait_ge(s_tab, 1)
            for k in range(2):
                link(stt(start_f[:, :], iota[0:1, :], float(STEP), pa[0:1, k, 32:32 + NSTEP], ALU.mult, ALU.add))
                ts(start_i[k][:, :], start_f[:, :], float(E), float(ROWW[k]), ALU.min, ALU.mult)
                ts(accoff_i[k][:, :], pa[0:1, k, 256:256 + NSTEP], float(MW), None, ALU.mult)
                ts(blk125[:, k, :], pa[:, k, 256:256 + NSTEP], float(BN), None, ALU.mult)
                link(cp(pre[:, k, :], pz[0:EP, k, 0:NB]))
            nc.vector.memset(oh, 0.0).then_inc(s_tabs, 1)

            dve.wait_ge(s_e3, 16)
            link(tt(sh_all, ea3, ea3, ALU.mult))
            nc.vector.tensor_reduce(tmp, sh_all, AX.X, ALU.add).then_inc(s_sq, 1)
            dve.wait_ge(s_len, 1)
            link(nc.vector.reciprocal(oh, run))
            link(ts(oh, oh, 3 ** 0.5, None, ALU.mult))
            tt(sh_all, ea3, oh.unsqueeze(2).to_broadcast([EP, EC, 3]), ALU.mult).then_inc(s_shd, 1)
            dve.wait_ge(s_shd, 1)

            def places(k, sem_chain, done, ready):
                nc.vector.memset(pos_f, 0.0).then_inc(sem_chain, 1)

                def one(b, n):
                    dve.wait_ge(sem_chain, n)
                    ts(oh, blk[k], iota[0:EP, bass.ds(b, 1)], None, ALU.is_equal).then_inc(sem_chain, 1)
                    dve.wait_ge(sem_chain, n + 1)
                    nc.vector.tensor_tensor_scan(run, ones_row, oh, pre[:, k, bass.ds(b, 1)], ALU.mult, ALU.add).then_inc(sem_chain, 1)
                    dve.wait_ge(sem_chain, n + 2)
                    tt(tmp, run, oh, ALU.mult).then_inc(sem_chain, 1)
                    dve.wait_ge(sem_chain, n + 3)
                    tt(pos_f, pos_f, tmp, ALU.add).then_inc(sem_chain, 1)
                with dve.Fori(0, NB) as b:
                    one(b, b * 4 + 1)
                dve.wait_ge(sem_chain, 4 * NB + 1)
                ts(pos_i[k], pos_f, -1.0, None, ALU.add).then_inc(done, 1)
                dve.wait_ge(done, ready)

            unsorted = dve.value_load(flag_i[0:1, 0:1], min_val=0, max_val=E)
            with dve.If(unsorted != 0):
                places(0, s_pd, s_pdd, 1)
            nc.vector.memset(kl[:, :], 0.0).then_inc(s_posd, 1)
            places(1, s_ps, s_poss, 1)

            def clear(k):
                nc.vector.memset(acc[:, :], 0.0).then_inc(s_clear, 1)
                dve.wait_ge(s_clear, k + 1)

            def edge_loop(k):
                P = products[k]

                def is_step(s):
                    return not isinstance(s, int) or 0 <= s < NSTEP

                def add(s, b):
                    at_ = dve.value_load(accoff_i[k][0:1, bass.ds(s, 1)], min_val=0, max_val=(NB - 1) * MW)
                    dve.wait_ge(scattered[k], s + 1)
                    if not (isinstance(s, int) and s < 1):
                        dve.wait_ge(added[k], s)
                    mw = CNT + 1 if k == 0 else MW
                    a = acc[:, bass.ds(at_, mw)]
                    tt(a, a, pa[0:BN, b, 0:mw], ALU.add).then_inc(added[k], 1)

                def body(s, u, turn):
                    if is_step(s):
                        b = u % 2
                        R = rows[k][:, u, :].rearrange("p (t w) -> p t w", t=T)
                        G = gath[:, u, :].rearrange("p (t f) -> p t f", t=T)
                        Gs = G[:, :, 0:S]
                        Gv = G[:, :, S:F].rearrange("p t (m v) -> p t m v", m=3)
                        Wt = pw[:, b, :, :]
                        M = msg[:, b, :, :]
                        vw = 96 if k == 0 else 128
                        Mv = M[:, :, 96:480].rearrange("p t (m w) -> p t m w", m=3) if k == 1 else \
                            M[:, :, 160:448].rearrange("p t (m w) -> p t m w", m=3)
                        sh = R[:, :, SH[k]:SH[k] + 3].unsqueeze(3)
                        shv = sh.to_broadcast([128, T, 3, V])
                        shs = sh.to_broadcast([128, T, 3, S])
                        tqb = tq[:, :, :].unsqueeze(2).to_broadcast([128, T, 3, S])

                        def wv(o):
                            return Wt[:, :, o:o + V].unsqueeze(2).to_broadcast([128, T, 3, V])

                        A4 = ta[:, :, :].rearrange("p t (m v) -> p t m v", m=3)
                        B4 = tb[:, :, :].rearrange("p t (m v) -> p t m v", m=3)
                        base = s * OPS[k]

                        def after(n):
                            dve.wait_ge(P, base + n)

                        dve.wait_ge(rows_in[k][u], (turn + 1) * 16)
                        if not (isinstance(s, int) and s < 1):
                            after(0)
                        key = R[:, :, KEY[k]:KEY[k] + 1].rearrange("p t o -> p (t o)").bitcast(I32)
                        ts(kl[:, :], key, blk125[:, k, bass.ds(s, 1)], None, ALU.subtract).then_inc(P, 1)
                        if not (isinstance(s, int) and s < 2):
                            dve.wait_ge(scattered[k], s - 1)
                        dve.wait_ge(weighted[k], s + 1)
                        dve.wait_ge(gathered[k][u], (turn + 1) * (16 * T))
                        if k == 0:
                            tt(tu[:, :, :], Wt[:, :, 0:96], R[:, :, 16:17].to_broadcast([128, T, 96]), ALU.mult).then_inc(P, 1)
                            tt(tq[:, :, :], Wt[:, :, 96:160], Gs, ALU.mult).then_inc(P, 1)
                            tt(A4, Gv, shv, ALU.mult).then_inc(P, 1)
                            after(1)
                            tt(hot[:, b, :, :], iota[:, 0:BN].unsqueeze(1).to_broadcast([128, T, BN]),
                               kl[:, :].unsqueeze(2).to_broadcast([128, T, BN]), ALU.is_equal).then_inc(P, 1)
                            after(2)
                            tt(M[:, :, 0:S], tu[:, :, 0:S], Gs, ALU.mult).then_inc(P, 1)
                            tt(Mv[:, :, :, S:96], tu[:, :, S:96].unsqueeze(2).to_broadcast([128, T, 3, V]), Gv, ALU.mult).then_inc(P, 1)
                            after(3)
                            tt(Mv[:, :, :, 0:S], tqb, shs, ALU.mult).then_inc(P, 1)
                            after(4)
                            tt(M[:, :, S:F].rearrange("p t (m v) -> p t m v", m=3), A4, wv(160), ALU.mult).then_inc(P, 1)
                        else:
                            def s4(m):
                                return R[:, :, SH[1] + m:SH[1] + m + 1].to_broadcast([128, T, V])
                            tt(A4, Gv, shv, ALU.mult).then_inc(P, 1)
                            tt(tq[:, :, :], Wt[:, :, S:2 * S], Gs, ALU.mult).then_inc(P, 1)
                            after(1)
                            tt(hot[:, b, :, :], iota[:, 0:BN].unsqueeze(1).to_broadcast([128, T, BN]),
                               kl[:, :].unsqueeze(2).to_broadcast([128, T, BN]), ALU.is_equal).then_inc(P, 1)
                            after(2)
                            nc.vector.tensor_reduce(td[:, :, :], ta[:, :, :].rearrange("p t (m v) -> p t v m", m=3),
                                                    AX.X, ALU.add).then_inc(P, 1)
                            tt(M[:, :, 0:S], Wt[:, :, 0:S], Gs, ALU.mult).then_inc(P, 1)
                            after(3)
                            tt(Mv[:, :, :, 0:S], tqb, shs, ALU.mult).then_inc(P, 1)
                            after(5)
                            sh23 = R[:, :, SH[1] + 2:SH[1] + 4].unsqueeze(3).to_broadcast([128, T, 2, V])
                            tt(A4[:, :, 0:2, :], Gv[:, :, 1:3, :], sh23, ALU.mult).then_inc(P, 1)
                            tt(A4[:, :, 2, :], Gv[:, :, 0, :], s4(1), ALU.mult).then_inc(P, 1)
                            tt(B4[:, :, 1:3, :], Gv[:, :, 0:2, :], sh23, ALU.mult).then_inc(P, 1)
                            tt(B4[:, :, 0, :], Gv[:, :, 2, :], s4(1), ALU.mult).then_inc(P, 1)
                            tt(M[:, :, S:96], td[:, :, :], Wt[:, :, 160:192], ALU.mult).then_inc(P, 1)
                            after(11)
                            tt(ta[:, :, :], ta[:, :, :], tb[:, :, :], ALU.subtract).then_inc(P, 1)
                            tt(Mv[:, :, :, S:96], Gv, wv(128), ALU.mult)
                            after(13)
                            tt(Mv[:, :, :, 96:128], A4, wv(192), ALU.mult).then_inc(P, 1)
                    s1 = s - 1
                    if is_step(s1):
                        add(s1, (u + 1) % 2)
                turns(dve, body, 1)
                dve.wait_ge(added[k], NSTEP)

            def normalise(k, g, n, base):
                C = s_fin[k]

                def after(m):
                    dve.wait_ge(C, base + m)
                for j in range(GB):
                    last = nc.vector.bn_stats(stats[:, j, :], y[:, j, :])
                last.then_inc(C, 1)
                after(n + 1)
                dve.sem_inc(passed[2], 1)
                for j in range(GB):
                    last = nc.vector.bn_aggr(mv[:, j, :], stats[:, j, :])
                last.then_inc(C, 1)
                after(n + 2)
                ts(small[:, 5, :].unsqueeze(2), mv[:, :, 1:2], EPS, None, ALU.add).then_inc(C, 1)
                dve.wait_ge(s_rt[k], g + 1)
                nc.vector.reciprocal(small[:, 7, :], small[:, 6, :]).then_inc(C, 1)
                after(n + 4)

            def scaled_out(j):
                return ts(xn[:, j, :], y[:, j, :], mv[:, j, 0:1], small[:, 7, j:j + 1], ALU.subtract, ALU.mult)

            def between(g):
                first = isinstance(g, int) and g == 0
                C = s_fin[0]
                base = g * FIN[0]

                def after(m):
                    dve.wait_ge(C, base + m)
                if not first:
                    after(0)
                a = group_of(acc, g, MW)
                ts(small[:, 0, :].unsqueeze(2), a[:, :, CNT:CNT + 1], 1.0, None, ALU.max).then_inc(C, 1)
                if not first:
                    dve.wait_ge(s_at[0], g * GB)
                cp(st[:, :, 0:S], a[:, :, 0:S])
                nc.vector.tensor_reduce(st[:, :, S:96], a[:, :, S:F].rearrange("p b (m v) -> p b v m", m=3), AX.X, ALU.add)
                cp(st[:, :, 96:384], a[:, :, F:CNT]).then_inc(s_st[0], 1)
                after(1)
                nc.vector.reciprocal(small[:, 1, :], small[:, 0, :]).then_inc(C, 1)
                after(2)
                stt(small[:, 2, :], small[:, 1, :], 96 ** -0.5, attr[:, bass.ds(g * GB, GB)], ALU.mult, ALU.mult).then_inc(C, 1)
                after(3)
                tt(small[:, 3, :], small[:, 2, :], small[:, 2, :], ALU.mult).then_inc(C, 1)
                tt(y[:, :, :], group_of(x_sb, g, F), group_of(side, g, SIDE)[:, :, 0:F], ALU.add).then_inc(C, 1)
                dve.wait_ge(s_ao[0], g * GB + GB)
                after(4)
                tt(small[:, 4, :].unsqueeze(2), po[:, :, F:F + 1], small[:, 3, :].unsqueeze(2), ALU.mult).then_inc(C, 1)
                after(6)
                tt(tm[:, :, 0:F], po[:, :, 0:F], small[:, 4, :].unsqueeze(2).to_broadcast([BN, GB, F]), ALU.mult).then_inc(C, 1)
                after(7)
                tt(y[:, :, 0:S], y[:, :, 0:S], tm[:, :, 0:S], ALU.add)
                yv = y[:, :, S:F].rearrange("p b (v m) -> p b m v", m=3)
                tt(yv, yv, tm[:, :, S:F].rearrange("p b (m v) -> p b m v", m=3), ALU.add).then_inc(C, 1)
                after(8)
                normalise(0, g, 8, base)
                if not first:
                    dve.wait_ge(s_xt[1], g * GB)
                for j in range(GB):
                    last = scaled_out(j)
                last.then_inc(C, 1)
                after(13)
                cp(group_of(xp, g, F), xn[:, :, :]).then_inc(s_xn[1], 1)

            def last_stage(g):
                first = isinstance(g, int) and g == 0
                C = s_fin[1]
                base = g * FIN[1]

                def after(m):
                    dve.wait_ge(C, base + m)
                if not first:
                    after(0)
                    dve.wait_ge(s_at[1], g * GB)
                ts(st[:, :, :], group_of(acc, g, MW), 1.0 / 32, None, ALU.mult).then_inc(s_st[1], 1)
                dve.wait_ge(s_ao[1], g * GB + GB)
                tt(tm[:, :, :], po[:, :, 0:SIDE], group_of(side, g, SIDE), ALU.add).then_inc(C, 1)
                nc.vector.memset(small[:, 0, :], 0.0).then_inc(C, 1)
                dve.wait_ge(s_act[1], g + 1)
                X = group_of(xp, g, F)
                tt(y[:, :, 0:S], X[:, :, 0:S], fs[:, :, 0:S], ALU.add)
                tv = tm[:, :, 96:192].rearrange("p b (m v) -> p b m v", m=3)
                tt(tv, tv, fs[:, :, S:96].unsqueeze(2).to_broadcast([BN, GB, 3, V]), ALU.mult).then_inc(C, 1)
                after(3)
                tt(y[:, :, S:F].rearrange("p b (v m) -> p b m v", m=3), X[:, :, S:F].rearrange("p b (v m) -> p b m v", m=3), tv,
                   ALU.add).then_inc(C, 1)
                after(4)
                normalise(1, g, 4, base)
                if not first:
                    dve.wait_ge(s_put, 16 * g)
                for j in range(GB):
                    last = scaled_out(j)
                last.then_inc(C, 1)

            dve.wait_ge(s_made, NCH)
            for u in range(2):
                dve.wait_ge(s_row0[u], 16 * CH * (NCH // 2))
            clear(0)
            link(nc.vector.memset(msg[:, :, :, CNT:CNT + 1], 1.0))
            edge_loop(0)
            groups(dve, between)
            clear(1)
            edge_loop(1)
            groups(dve, last_stage)


_INS = ["x", "src", "dst", "edge_attr_16", "edge_attr_3", "edge_attr_4", "edge_attr_64", "node_vec1",
        "L0_gnn_Wfc1", "L0_gnn_Wfc2", "L0_gnn_Wsc0", "L0_gnn_Wsc1", "L0_gnn_Wl1_0", "L0_gnn_Wl1_1",
        "L0_gnn_Wl2_s", "L0_gnn_Wl2_v", "L0_gnn_Wa",
        "L1_gnn_W_skip0", "L1_gnn_W_skip1", "L1_gnn_W_nl0", "L1_gnn_W_nl1", "L1_gnn_W_fc1", "L1_gnn_W_fc2",
        "L1_gnn_W_out_s", "L1_gnn_W_out_v"]


def kernel(**inputs):
    import numpy as _np
    import concourse.bacc as _bacc
    from concourse.bass_utils import run_bass_kernel_spmd as _run

    nc = _bacc.Bacc("TRN2", target_bir_lowering=False, num_devices=1)
    arrays, args = {}, []
    for name in _INS:
        a = _np.ascontiguousarray(inputs[name])
        arrays[f"in_{name}"] = a
        args.append(nc.dram_tensor(f"in_{name}", a.shape, mybir.dt.from_np(a.dtype), kind="ExternalInput").ap())
    args.append(nc.dram_tensor("out_0", (N, F), F32, kind="ExternalOutput").ap())
    gnn_kernel(nc, *args)
    r = _run(nc, [arrays], core_ids=[0])
    return r.results[0]["out_0"]
```

```python
from contextlib import ExitStack

import concourse.bass as bass
from concourse import mybir

F32 = mybir.dt.float32
I32 = mybir.dt.int32
ALU = mybir.AluOpType
ACT = mybir.ActivationFunctionType
AX = mybir.AxisListType

N = 3125
E = 100000
S, V = 64, 32
F = S + 3 * V
BN = 125
NB = N // BN
GB = 5
NG = NB // GB
EP = 125
EC = E // EP
TILE = 128
T = 4
STEP = T * TILE
NSTEP = NB + (E - NB) // STEP
UN = 8
SL = 4
CH = 16
NCH = EC // CH
SC = 4
MOVES = EC // SC // UN
LOOPED = MOVES - NG
META = 7
MW = 480
CNT = 448
PW = 256
SIDE = 192
ROUND = 1.5 * 2 ** 23
EPS = 1e-5
assert NB * BN == N and EP * EC == E and NSTEP % SL == 0 and NCH * CH == EC and NCH % 2 == 0
assert MOVES * UN * SC == EC and LOOPED < NSTEP // UN

ROWW = (22, 70)
SH = (17, 64)
IDX = (20, 68)
KEY = (21, 69)
KEEP = (F, SIDE)
OPS = (9, 10)
FIN = (13, 9)
ROOT = (11, 7)
N_W = 31


def gnn_kernel(nc, x, src, dst, edge_attr_16, edge_attr_3, edge_attr_4, edge_attr_64, node_vec1,
               Wfc1, Wfc2, Wsc0, Wsc1, Wl1_0, Wl1_1, Wl2_s, Wl2_v, Wa,
               W_skip0, W_skip1, W_nl0, W_nl1, W_fc1, W_fc2, W_out_s, W_out_v, out):
    with ExitStack() as ctx:
        def sb(name, shape, dt=F32):
            return ctx.enter_context(nc.sbuf_tensor(name, shape, dt))

        def sem(name):
            return ctx.enter_context(nc.semaphore(name))

        table = [nc.dram_tensor(f"table{k}", (N, F), F32).ap() for k in range(2)]
        ordered = [nc.dram_tensor(f"ordered{k}", (E + STEP, ROWW[k]), F32).ap() for k in range(2)]
        meta_d = nc.dram_tensor("meta", (EP, EC * META), F32).ap()

        iota_i = sb("iota_i", [128, NSTEP], I32)
        part_i = sb("part_i", [128, 1], I32)
        iota = sb("iota", [128, NSTEP])
        part = sb("part", [128, 1])
        ident = sb("ident", [128, 128])

        ones = sb("ones", [128, 128])
        x_sb = sb("x_sb", [BN, NB * F])
        xp = sb("xp", [BN, NB * F])
        side = sb("side", [BN, NB * SIDE])
        acc = sb("acc", [BN, NB * MW])
        attr = sb("attr", [BN, NB])
        xn = sb("xn", [BN, GB, F])
        xT = sb("xT", [96, GB, 2, BN])
        st = sb("st", [BN, GB, MW])
        sT = sb("sT", [128, 2, 4 * BN])
        tm = sb("tm", [BN, GB, SIDE])
        y = sb("y", [BN, GB, F])
        fs = sb("fs", [BN, GB, 96])
        small = sb("small", [BN, 8, GB])
        stats = sb("stats", [BN, GB, 6])
        mv = sb("mv", [BN, GB, 2])

        comp = sb("comp", [96, 3])
        comp3 = sb("comp3", [96, 3])

        node_s = [sb("node_s0", [S, 2 * S]), sb("node_s1", [S, S + 96])]
        node_v = [sb("node_v0", [96, 192]), sb("node_v1", [96, 192])]
        fc1 = [sb("fc1_0", [S, 2, 128]), sb("fc1_1", [128, 128])]
        fc2 = [sb("fc2_0", [128, 192]), sb("fc2_1", [128, 224])]
        out_s = [sb("out_s0", [96, S + 1]), sb("out_s1", [96, 96])]
        out_v = [sb("out_v0", [96, V]), sb("out_v1", [128, V])]
        cnt = sb("cnt", [EP, 2, NB])
        viol = sb("viol", [EP, 1])
        tot = sb("tot", [NB, 2])
        nst = sb("nst", [NB, 2])
        cum = sb("cum", [NB, 2])
        wgt = sb("wgt", [NB, 2])
        big = sb("big", [NB, 1])

        pre = sb("pre", [EP, 2, NB])
        blk125 = sb("blk125", [128, 2, NSTEP])
        start_f = sb("start_f", [1, NSTEP])
        start_i = [sb("start_i0", [1, NSTEP], I32), sb("start_i1", [1, NSTEP], I32)]
        accoff_i = [sb("accoff_i0", [1, NSTEP], I32), sb("accoff_i1", [1, NSTEP], I32)]
        flag_i = sb("flag_i", [1, 1], I32)
        at = sb("at", [EP, 2, CH], I32)
        rows1 = sb("rows1", [128, UN, T * ROWW[1]])
        rows0 = rows1[:, :, :].rearrange("p u w -> p (u w)")[:, 0:UN * T * ROWW[0]]
        rows = [rows0.rearrange("p (u w) -> p u w", u=UN), rows1[:, :, :]]
        tail = [rows[0][:, 0, 0:ROWW[0]], rows[1][:, UN - 1, 0:ROWW[1]]]
        gath = sb("gath", [128, SL, T * F])
        flat = sb("flat", [128, 2, T * 64])
        efT = sb("efT", [128, 2, 2 * 128])
        hT = sb("hT", [128, 2, 2, 128])
        msg = sb("msg", [128, 2, T, MW])
        hot = sb("hot", [128, 2, T, BN])
        kl = sb("kl", [128, T])
        tu = sb("tu", [128, T, 96])
        tq = sb("tq", [128, T, S])
        ta = sb("ta", [128, T, 3 * V])
        td = sb("td", [128, T, V])
        gsh = sb("gsh", [128, 2, T, 3 * F])

        gathf = gath[:, :, :].rearrange("p u w -> p (u w)")
        isblk = gathf[0:NB, 0:128]
        totb = gathf[0:NB, 128:384].rearrange("p (k w) -> p k w", k=2)
        reach = gathf[0:NB, 384:384 + 2 * NSTEP].rearrange("p (k w) -> p k w", k=2)
        below = gathf[:, 840:968]
        upto = gathf[:, 968:1096]
        raw_v = gathf[0:96, 1096:1224].rearrange("p (k v) -> p k v", k=4)
        raw_s = gathf[0:S, 1224:1352].rearrange("p (k v) -> p k v", k=2)
        raw_fc2 = gathf[:, 1352:1544]

        def carve(whole, at_, *shape):
            n = 1
            for s in shape:
                n *= s
            flat = whole[0:EP, at_:at_ + n]
            return flat if len(shape) == 1 else flat.rearrange(
                "p (a b) -> p a b" if len(shape) == 2 else "p (a b c) -> p a b c",
                **dict(zip("abc", shape)))

        dst_i = acc[:, 0:EC].bitcast(I32)
        src_i = acc[:, EC:2 * EC].bitcast(I32)
        key_i = [dst_i, src_i]
        next_i = acc[:, 2 * EC:3 * EC].bitcast(I32)
        blk = [acc[:, 3 * EC:4 * EC], acc[:, 4 * EC:5 * EC]]
        gflat = gsh[:, :, :, :].rearrange("p b t w -> p (b t w)")
        oh = carve(gflat, 0, EC)
        run = carve(gflat, EC, EC)
        tmp = carve(gflat, 2 * EC, EC)
        pos_f = carve(gflat, 3 * EC, EC)
        ones_row = acc[:, 5 * EC:6 * EC]
        meta = acc[:, 6 * EC:(6 + META) * EC].rearrange("p (c m) -> p c m", m=META)
        sh_all = meta[:, :, 0:3]
        dst_at = acc[:, 13 * EC:14 * EC].bitcast(I32)
        pos_i = [dst_at.unsqueeze(2), meta[:, :, 6:7].bitcast(I32)]
        ea3 = st[:, :, :].rearrange("p g w -> p (g w)").rearrange("p (c m) -> p c m", m=3)
        mflat = msg[:, :, :, :].rearrange("p b t w -> p (b t w)")
        row0 = carve(mflat, 0, 2, CH, ROWW[0])
        in16 = carve(mflat, 704, 2, CH, 16)
        in4 = carve(mflat, 1216, 2, CH, 4)
        in64 = carve(gflat, 0, SL, SC, 64)
        inmeta = carve(gflat, SL * SC * 64, SL, SC, META)
        row1 = carve(gflat, SL * SC * (64 + META), SL, SC, ROWW[1])

        pw = ctx.enter_context(nc.psum_tensor("pw", [128, 2, T, PW], F32))
        pz = ctx.enter_context(nc.psum_tensor("pz", [128, 2, 512], F32))
        pa = ctx.enter_context(nc.psum_tensor("pa", [128, 2, 512], F32))
        po = pw[0:BN, :, :, :].rearrange("p b t w -> p (b t) w")[:, 0:GB, :]

        s_keys = sem("s_keys")
        s_x = sem("s_x")
        s_e3 = sem("s_e3")
        s_w = sem("s_w")
        s_iota = sem("s_iota")
        s_const = sem("s_const")
        s_zero = sem("s_zero")
        s_kron = sem("s_kron")
        s_scaled = sem("s_scaled")
        s_sort = sem("s_sort")
        s_count = sem("s_count")
        s_cnt = sem("s_cnt")
        s_tot = sem("s_tot")
        s_nst = sem("s_nst")
        s_cum = sem("s_cum")
        s_reach = sem("s_reach")
        s_tab = sem("s_tab")
        s_tabs = sem("s_tabs")
        s_flag = sem("s_flag")
        s_posd = sem("s_posd")
        s_pd = sem("s_pd")
        s_pdd = sem("s_pdd")
        s_ps = sem("s_ps")
        s_sq = sem("s_sq")
        s_len = sem("s_len")
        s_shd = sem("s_shd")
        s_tail = sem("s_tail")
        s_tailw = sem("s_tailw")
        s_load = [sem("s_load0"), sem("s_load1")]
        s_made = sem("s_made")
        s_row0 = [sem("s_row00"), sem("s_row01")]
        s_meta = sem("s_meta")
        s_metaw = sem("s_metaw")
        s_load1 = [sem(f"s_load1{u}") for u in range(SL)]
        s_made1 = sem("s_made1")
        s_row1 = [sem(f"s_row1{u}") for u in range(SL)]
        scaled = sem("scaled")
        s_clear = sem("s_clear")
        s_table = [sem("s_table0"), sem("s_table1")]
        s_out = sem("s_out")
        passed = [sem("passed_sp"), sem("passed_pool"), sem("passed_dve"), sem("passed_pe")]
        s_xn = [sem("s_xn0"), sem("s_xn1")]
        s_xt = [sem("s_xt0"), sem("s_xt1")]
        s_xc = [sem("s_xc0"), sem("s_xc1")]
        s_mm = [sem("s_mm0"), sem("s_mm1")]
        s_ev = [sem("s_ev0"), sem("s_ev1")]
        s_st = [sem("s_st0"), sem("s_st1")]
        s_at = [sem("s_at0"), sem("s_at1")]
        s_ac = [sem("s_ac0"), sem("s_ac1")]
        s_ao = [sem("s_ao0"), sem("s_ao1")]
        s_fin = [sem("s_fin0"), sem("s_fin1")]
        s_act = [sem("s_act0"), sem("s_act1")]
        s_rt = [sem("s_rt0"), sem("s_rt1")]
        s_put = sem("s_put")
        rows_in = [[sem(f"rows_in{k}{u}") for u in range(UN)] for k in range(2)]
        gathered = [[sem(f"gathered{k}{u}") for u in range(SL)] for k in range(2)]
        flattened = [sem("flattened0"), sem("flattened1")]
        transposed = [sem("transposed0"), sem("transposed1")]
        copied = [sem("copied0"), sem("copied1")]
        hidden = [sem("hidden0"), sem("hidden1")]
        activated = [sem("activated0"), sem("activated1")]
        weighted = [sem("weighted0"), sem("weighted1")]
        products = [sem("products0"), sem("products1")]
        scattered = [sem("scattered0"), sem("scattered1")]
        added = [sem("added0"), sem("added1")]

        block = ctx.enter_context(nc.Block())

        def turns(eng, body, after, moves=None):
            for u in range(UN):
                body(u, u, 0)
                if moves:
                    moves(u, u, 0)
            for a, b, m in ((1, LOOPED, moves), (LOOPED, NSTEP // UN, None)) if moves else ((1, NSTEP // UN, None),):
                with eng.Fori(a, b) as i:
                    for u in range(UN):
                        body(i * UN + u, u, i)
                        if m:
                            m(i * UN + u, u, i)
            for s in range(NSTEP // UN * UN, NSTEP + after):
                body(s, s % UN, s // UN)

        def before(s, n):
            return isinstance(s, int) and s < n

        def use(u, turn):
            return turn * (UN // SL) + u // SL

        def groups(eng, body):
            body(0)
            with eng.Fori(1, NG) as g:
                body(g)

        def group_of(t, g, width):
            return t[:, bass.ds(g * (GB * width), GB * width)].rearrange("p (b w) -> p b w", w=width)

        @block.sync
        def _(sp):
            last = EC - 1
            kd = dst.rearrange("(p c) -> p c", p=EP)
            ks = src.rearrange("(p c) -> p c", p=EP)
            sp.dma_start(dst_i, kd).then_inc(s_keys, 16)
            sp.dma_start(src_i, ks).then_inc(s_keys, 16)
            nxt = dst[1:1 + (EP - 1) * EC].rearrange("(p c) -> p c", p=EP - 1)
            sp.wait_ge(s_sort, 1)
            sp.dma_start(next_i[0:EP - 1, :], nxt).then_inc(s_keys, 16)
            sp.dma_start(next_i[EP - 1:EP, 0:last], dst[E - EC + 1:E].rearrange("(a c) -> a c", a=1)).then_inc(s_keys, 16)
            sp.dma_start(x_sb[:, :].rearrange("p (b f) -> p b f", f=F), x.rearrange("(b p) f -> p b f", p=BN)).then_inc(s_x, 16)
            with nc.allow_non_contiguous_dma(reason="one number of each node"):
                sp.dma_start(attr[:, :].unsqueeze(2), node_vec1.rearrange("(b p) f -> p b f", p=BN)).then_inc(s_x, 16)
            sp.dma_start(st[:, :, :].rearrange("p g w -> p (g w)"), edge_attr_3.rearrange("(p c) m -> p (c m)", p=EP)).then_inc(s_e3, 16)
            for k, w in enumerate((Wl1_1, Wsc1, W_nl1, W_skip1)):
                for m in range(3):
                    sp.dma_start(raw_v[m:96:3, k, :], w).then_inc(s_w, 16)
            sp.dma_start(raw_s[:, 0, :], Wl1_0).then_inc(s_w, 16)
            sp.dma_start(raw_s[:, 1, :], Wsc0).then_inc(s_w, 16)
            sp.dma_start(node_s[1][:, 0:S], W_nl0).then_inc(s_w, 16)
            sp.dma_start(node_s[1][:, S:S + 96], W_skip0).then_inc(s_w, 16)
            for h in range(2):
                sp.dma_start(raw_fc2[S * h:S * h + S, :], Wfc2).then_inc(s_w, 16)
                sp.dma_start(fc2[1][S * h:S * h + S, :], W_fc2).then_inc(s_w, 16)
            sp.dma_start(out_s[0][:, 0:S], Wl2_s).then_inc(s_w, 16)
            sp.dma_start(out_s[0][:, S:S + 1], Wa).then_inc(s_w, 16)
            sp.dma_start(out_v[0][:, :], Wl2_v).then_inc(s_w, 16)
            sp.dma_start(out_s[1][:, :], W_out_s).then_inc(s_w, 16)
            sp.dma_start(out_v[1][:, :], W_out_v).then_inc(s_w, 16)
            sp.wait_ge(s_zero, 1)
            for t in range(T):
                sp.dma_start(fc1[0][16 * t:16 * t + 16, t % 2, S * (t // 2):S * (t // 2) + S], Wfc1).then_inc(s_w, 16)
            for h in range(2):
                sp.dma_start(fc1[1][S * h:S * h + S, S * h:S * h + S], W_fc1).then_inc(s_w, 16)
            sp.wait_ge(s_tail, 1)
            for k in range(2):
                for q in range(T):
                    dram = ordered[k][E + q * TILE:E + (q + 1) * TILE, :]
                    sp.dma_start(dram, tail[k]).then_inc(s_tailw, 16)

            d16 = edge_attr_16.rearrange("(p c) f -> p (c f)", p=EP)
            d4 = edge_attr_4.rearrange("(p c) f -> p (c f)", p=EP)
            d64 = edge_attr_64.rearrange("(p c) f -> p (c f)", p=EP)
            o0 = ordered[0][0:E, :].rearrange("(p c) w -> p (c w)", p=EP)

            def load(j, u):
                for t, d, w in ((in16, d16, 16), (in4, d4, 4)):
                    sp.dma_start(t[:, u, :, :].rearrange("p c w -> p (c w)"),
                                 d[:, bass.ds(j * (CH * w), CH * w)]).then_inc(s_load[u], 16)

            def store(j, u):
                sp.wait_ge(s_made, j + 1)
                sp.sem_inc(passed[0], 1)
                with sp.If(unsorted == 0):
                    n = CH // 2 * ROWW[0]
                    for h in range(2):
                        sp.dma_start(o0[:, bass.ds(j * (2 * n) + h * n, n)],
                                     row0[:, u, :, :].rearrange("p c w -> p (c w)")[:, h * n:h * n + n]).then_inc(s_row0[u], 8 * CH)

            sp.wait_ge(s_flag, 1)
            unsorted = sp.value_load(flag_i[0:1, 0:1], min_val=0, max_val=E)
            load(0, 0)
            load(1, 1)
            with sp.Fori(0, NCH // 2 - 1) as i:
                for u in range(2):
                    store(i * 2 + u, u)
                    load(i * 2 + u + 2, u)
            for u in range(2):
                store(NCH - 2 + u, u)
            sp.wait_ge(s_meta, 1)
            sp.dma_start(meta_d, meta.rearrange("p c m -> p (c m)")).then_inc(s_metaw, 16)
            for u in range(2):
                sp.wait_ge(s_row0[u], 16 * CH * (NCH // 2))
            sp.wait_ge(s_tailw, 16 * 2 * T)

            def put_table(k, staging):
                sp.wait_ge(s_ev[k], 2 * NB)
                sp.dma_start(table[k].rearrange("(b p) f -> p b f", p=BN),
                             staging[:, :].rearrange("p (b f) -> p b f", f=F)).then_inc(s_table[k], 16)

            def edge_rows(k):
                flat = ordered[k].rearrange("e w -> (e w)")
                n = STEP * ROWW[k]

                def body(s, u, turn):
                    if not before(s, UN):
                        sp.wait_ge(products[k], s * OPS[k] - (UN - 1) * OPS[k])
                    at_ = sp.value_load(start_i[k][0:1, bass.ds(s, 1)], min_val=0, max_val=E * ROWW[k])
                    sp.dma_start(rows[k][:, u, :], flat[bass.ds(at_, n)].rearrange("(p w) -> p w", p=128)).then_inc(rows_in[k][u], 16)

                def moves(s, u, turn):
                    v = u % SL
                    if not before(s, SL):
                        sp.wait_ge(s_row1[v], use(u, turn) * (16 * SC))
                    sp.dma_start(in64[:, v, :, :].rearrange("p c w -> p (c w)"),
                                 d64[:, bass.ds(s * (SC * 64), SC * 64)]).then_inc(s_load1[v], 16)
                    sp.dma_start(inmeta[:, v, :, :].rearrange("p c w -> p (c w)"),
                                 meta_d[:, bass.ds(s * (SC * META), SC * META)]).then_inc(s_load1[v], 16)
                turns(sp, body, 0, moves if k == 0 else None)
                if k == 0:
                    with sp.Fori(LOOPED, MOVES) as i:
                        for u in range(UN):
                            moves(i * UN + u, u, i)

            put_table(0, xp)
            sp.wait_ge(s_metaw, 16)
            edge_rows(0)
            put_table(1, x_sb)
            for v in range(SL):
                sp.wait_ge(s_row1[v], 16 * SC * MOVES * (UN // SL))
            edge_rows(1)

            def put(g):
                sp.wait_ge(s_fin[1], (g + 1) * FIN[1])
                sp.dma_start(out.rearrange("(b p) f -> p b f", p=BN)[:, bass.ds(g * GB, GB), :], xn[:, :, :]).then_inc(s_put, 16)
            groups(sp, put)
            sp.wait_ge(s_put, 16 * NG)

        @block.gpsimd
        def _(pool):
            nc.gpsimd.iota(iota_i[:, :], [[1, NSTEP]], base=0, channel_multiplier=0).then_inc(s_iota, 1)
            nc.gpsimd.iota(part_i[:, :], [[1, 1]], base=0, channel_multiplier=1).then_inc(s_iota, 1)
            pool.wait_ge(s_flag, 1)
            unsorted = pool.value_load(flag_i[0:1, 0:1], min_val=0, max_val=E)
            pool.wait_ge(s_posd, 1)

            with pool.If(unsorted != 0):
                with pool.Fori(0, NCH // 2) as i:
                    for u in range(2):
                        pool.wait_ge(s_made, i * 2 + u + 1)
                        pool.sem_inc(passed[1], 1)
                        for c in range(CH):
                            pool.indirect_dma_start(ordered[0][0:E, :], bass.IndirectOffsetOnAxis(ap=at[:, u, c:c + 1], axis=0),
                                                    row0[:, u, c, :], None).then_inc(s_row0[u], 16)

            def edge_gather(k):
                pool.wait_ge(s_table[k], 16)

                def body(s, u, turn):
                    pool.wait_ge(rows_in[k][u], (turn + 1) * 16)
                    if not before(s, SL):
                        pool.wait_ge(products[k], s * OPS[k] - (SL - 1) * OPS[k])
                    pool.sem_inc(passed[1], 1)
                    for t in range(T):
                        i_ap = rows[k][:, u, t * ROWW[k] + IDX[k]:t * ROWW[k] + IDX[k] + 1].bitcast(I32)
                        pool.indirect_dma_start(gath[:, u % SL, t * F:(t + 1) * F], None, table[k],
                                                bass.IndirectOffsetOnAxis(ap=i_ap, axis=0)).then_inc(gathered[k][u % SL], 16)

                def moves(s, u, turn):
                    pool.wait_ge(s_made1, s + 1)
                    pool.sem_inc(passed[1], 1)
                    v = u % SL
                    for c in range(SC):
                        pool.indirect_dma_start(ordered[1][0:E, :],
                                                bass.IndirectOffsetOnAxis(ap=inmeta[:, v, c, META - 1:META].bitcast(I32), axis=0),
                                                row1[:, v, c, :], None).then_inc(s_row1[v], 16)
                turns(pool, body, 0, moves if k == 0 else None)
                if k == 0:
                    with pool.Fori(LOOPED, MOVES) as i:
                        for u in range(UN):
                            moves(i * UN + u, u, i)
            edge_gather(0)
            edge_gather(1)

        def node_columns(k):
            w = node_s[k].shape[1]
            return [(node_s[k][:, 0:S], 0, 0), (node_v[k][:, 0:96], 1, S),
                    (node_s[k][:, S:w], 0, F), (node_v[k][:, 96:192], 1, F + w - S)]

        @block.tensor
        def _(pe):
            def mm(o, l, r, start=True, stop=True):
                return nc.tensor.matmul(o, l, r, start=start, stop=stop)

            def node_prep_group(k, g):
                pe.wait_ge(s_xn[k], g + 1)
                first = isinstance(g, int) and g == 0
                for j in range(GB):
                    if not (first and j < 1):
                        pe.wait_ge(s_xc[k], g * GB + max(j - 1, 0))
                    pe.sem_inc(passed[3], 1)
                    nc.tensor.transpose(pz[0:S, j % 2, 0:BN], xn[:, j, 0:S], ident[0:BN, 0:BN])
                    nc.tensor.transpose(pz[0:96, j % 2, 128:128 + BN], xn[:, j, S:F],
                                        ident[0:BN, 0:BN]).then_inc(s_xt[k], 1)
                for j in range(GB):
                    pe.wait_ge(s_xc[k], g * GB + j + 1)
                    if not (first and j < 1):
                        pe.wait_ge(s_ev[k], g * (2 * GB) + 2 * max(j - 1, 0))
                    for n, (w, c, col) in enumerate(node_columns(k)):
                        rws = S if c == 0 else 96
                        last = mm(pa[0:BN, j % 2, col:col + w.shape[1]], xT[0:rws, j, c, :], w)
                    last.then_inc(s_mm[k], 1)

            def finish_group(k, g):
                first = isinstance(g, int) and g == 0
                vw = 96 if k == 0 else 128
                pe.wait_ge(s_st[k], g + 1)
                for j in range(GB + 1):
                    if j < GB:
                        if not (first and j < 1):
                            pe.wait_ge(s_ac[k], g * GB + max(j - 1, 0))
                        nc.tensor.transpose(pz[0:96, j % 2, 0:BN], st[:, j, 0:96], ident[0:BN, 0:BN])
                        for m in range(3):
                            last = nc.tensor.transpose(pz[0:vw, j % 2, BN * (m + 1):BN * (m + 2)],
                                                       st[:, j, 96 + vw * m:96 + vw * (m + 1)], ident[0:BN, 0:BN])
                        last.then_inc(s_at[k], 1)
                    if j >= 1:
                        q = j - 1
                        pe.wait_ge(s_ac[k], g * GB + q + 1)
                        sw = S if k == 0 else 96
                        mm(po[:, q, 0:sw], sT[0:96, q % 2, 0:BN], out_s[k][:, 0:sw])
                        if k == 0:
                            mm(po[:, q, F:F + 1], sT[0:96, q % 2, 0:BN], out_s[0][:, S:S + 1])
                        for m in range(3):
                            last = mm(po[:, q, sw + V * m:sw + V * (m + 1)], sT[0:vw, q % 2, BN * (m + 1):BN * (m + 2)],
                                      out_v[k][0:vw, :])
                        last.then_inc(s_ao[k], 1)

            def edge_loop(k):
                w1, w2 = fc1[k], fc2[k]
                ww = w2.shape[1]
                ew = 16 if k == 0 else 64

                def is_step(s):
                    return not isinstance(s, int) or 0 <= s < NSTEP

                def body(s, u, turn):
                    if is_step(s):
                        pe.wait_ge(flattened[k], s + 1)
                        if not (isinstance(s, int) and s < 1):
                            pe.wait_ge(copied[k], s)
                        pe.sem_inc(passed[3], 1)
                        if k == 0:
                            last = nc.tensor.transpose(pz[0:T * ew, 0, 0:128], flat[:, u % 2, 0:T * ew], ident[:, :])
                        else:
                            for j in range(2):
                                last = nc.tensor.transpose(pz[:, 0, 128 * j:128 * (j + 1)], flat[:, u % 2, 128 * j:128 * (j + 1)], ident[:, :])
                        last.then_inc(transposed[k], 1)
                    s1, b1 = s - 1, (u + 1) % 2
                    if is_step(s1):
                        pe.wait_ge(copied[k], s1 + 1)
                        if not (isinstance(s1, int) and s1 < 1):
                            pe.wait_ge(activated[k], s1)
                        if k == 0:
                            for j in range(2):
                                last = mm(pz[:, 1, 128 * j:128 * (j + 1)], w1[:, j, :], efT[0:S, b1, 0:128])
                        else:
                            last = mm(pz[:, 1, 0:256], w1[:, :], efT[:, b1, :])
                        last.then_inc(hidden[k], 1)
                    s2, b2 = s - 2, u % 2
                    if is_step(s2):
                        pe.wait_ge(activated[k], s2 + 1)
                        if not (isinstance(s2, int) and s2 < 2):
                            pe.wait_ge(products[k], s2 * OPS[k] - OPS[k])
                        for t in range(T):
                            h = S * (t // 2)
                            last = mm(pw[:, b2, t, 0:ww], hT[h:h + S, b2, t % 2, :], w2[h:h + S, :])
                        last.then_inc(weighted[k], 1)
                    s3, b3 = s - 3, (u + 1) % 2
                    if is_step(s3):
                        pe.wait_ge(products[k], s3 * OPS[k] + OPS[k])
                        if not (isinstance(s3, int) and s3 < 2):
                            pe.wait_ge(added[k], s3 - 1)
                        mw = CNT + 1 if k == 0 else MW
                        for t in range(T):
                            last = mm(pa[0:BN, b3, 0:mw], hot[:, b3, t, :], msg[:, b3, t, 0:mw], start=(t == 0), stop=(t == T - 1))
                        last.then_inc(scattered[k], 1)
                turns(pe, body, 3)

            pe.wait_ge(s_const, 1)
            pe.wait_ge(s_cnt, 1)
            for k in range(2):
                mm(pa[0:NB, 0, k:k + 1], cnt[:, k, :], ones[0:EP, 0:1])
            mm(pa[0:1, 0, 8:9], viol[:, :], ones[0:EP, 0:1]).then_inc(s_tot, 1)
            pe.wait_ge(s_nst, 1)
            mm(pa[0:NB, 0, 16:18], upto[0:NB, 0:NB], nst[:, :]).then_inc(s_cum, 1)
            pe.wait_ge(s_reach, 1)
            for k in range(2):
                mm(pa[0:1, k, 32:32 + NSTEP], wgt[:, k:k + 1], reach[:, k, :])
                mm(pa[:, k, 256:256 + NSTEP], isblk, reach[:, k, :])
                mm(pz[0:EP, k, 0:NB], below[0:EP, 0:EP], cnt[:, k, :], stop=False)
                last = mm(pz[0:EP, k, 0:NB], totb[:, k, 0:EP], below[0:NB, 0:NB], start=False)
            last.then_inc(s_tab, 1)

            pe.wait_ge(s_tabs, 1)
            pe.wait_ge(s_w, 16 * N_W)
            pe.wait_ge(s_scaled, 1)
            groups(pe, lambda g: node_prep_group(0, g))
            pe.wait_ge(s_ev[0], 2 * NB)
            edge_loop(0)
            pe.wait_ge(added[0], NSTEP)

            def between(g):
                finish_group(0, g)
                node_prep_group(1, g)
            groups(pe, between)
            pe.wait_ge(s_ev[1], 2 * NB)
            edge_loop(1)
            pe.wait_ge(added[1], NSTEP)
            groups(pe, lambda g: finish_group(1, g))

        @block.scalar
        def _(act):
            def node_prep_group(k, g):
                first = isinstance(g, int) and g == 0
                for j in range(GB):
                    act.wait_ge(s_xt[k], g * GB + j + 1)
                    if not first:
                        act.wait_ge(s_mm[k], g * GB + j + 1 - GB)
                    nc.scalar.copy(xT[0:S, j, 0, :], pz[0:S, j % 2, 0:BN])
                    nc.scalar.copy(xT[:, j, 1, :], pz[0:96, j % 2, 128:128 + BN]).then_inc(s_xc[k], 1)
                staging = xp if k == 0 else x_sb
                for j in range(GB):
                    act.wait_ge(s_mm[k], g * GB + j + 1)
                    b = g * GB + j
                    t_out = staging[:, bass.ds(b * F, F)]
                    s_out_ = side[:, bass.ds(b * SIDE, KEEP[k])]
                    if k == 0:
                        a = attr[:, bass.ds(b, 1)]
                        nc.scalar.activation(t_out, pa[0:BN, j % 2, 0:F], ACT.Copy, scale=a).then_inc(s_ev[k], 1)
                        nc.scalar.activation(s_out_, pa[0:BN, j % 2, F:F + KEEP[k]], ACT.Copy, scale=a).then_inc(s_ev[k], 1)
                    else:
                        nc.scalar.copy(t_out, pa[0:BN, j % 2, 0:F]).then_inc(s_ev[k], 1)
                        nc.scalar.copy(s_out_, pa[0:BN, j % 2, F:F + KEEP[k]]).then_inc(s_ev[k], 1)

            def finish_group(k, g):
                first = isinstance(g, int) and g == 0
                for j in range(GB):
                    act.wait_ge(s_at[k], g * GB + j + 1)
                    if not (first and j < 2):
                        act.wait_ge(s_ao[k], g * GB + j - 1 if j >= 2 else g * GB)
                    if k == 0:
                        nc.scalar.copy(sT[0:96, j % 2, :], pz[0:96, j % 2, 0:4 * BN]).then_inc(s_ac[k], 1)
                    else:
                        nc.scalar.copy(sT[0:96, j % 2, 0:BN], pz[0:96, j % 2, 0:BN])
                        nc.scalar.copy(sT[:, j % 2, BN:4 * BN], pz[:, j % 2, BN:4 * BN]).then_inc(s_ac[k], 1)
                if k == 1:
                    act.wait_ge(s_fin[1], g * FIN[1] + 2)
                    nc.scalar.activation(fs[:, :, 0:S], tm[:, :, 0:S], ACT.Silu)
                    nc.scalar.activation(fs[:, :, S:96], tm[:, :, S:96], ACT.Sigmoid).then_inc(s_act[1], 1)
                act.wait_ge(s_fin[k], g * FIN[k] + ROOT[k])
                nc.scalar.activation(small[:, 6, :], small[:, 5, :], ACT.Sqrt).then_inc(s_rt[k], 1)

            def moves(s, u, turn):
                v = u % SL
                act.wait_ge(s_load1[v], (use(u, turn) + 1) * 32)
                if not before(s, SL):
                    act.wait_ge(s_row1[v], use(u, turn) * (16 * SC))
                r = row1[:, v, :, :]
                nc.scalar.copy(r[:, :, 0:64], in64[:, v, :, :])
                nc.scalar.copy(r[:, :, 64:68], inmeta[:, v, :, 0:4])
                nc.scalar.copy(r[:, :, 68:70].bitcast(I32), inmeta[:, v, :, 4:6].bitcast(I32)).then_inc(s_made1, 1)

            def edge_loop(k):
                def is_step(s):
                    return not isinstance(s, int) or 0 <= s < NSTEP

                ew = 16 if k == 0 else 64

                def body(s, u, turn):
                    if is_step(s):
                        act.wait_ge(rows_in[k][u], (turn + 1) * 16)
                        if not (isinstance(s, int) and s < 2):
                            act.wait_ge(transposed[k], s - 1)
                        if k == 0:
                            f = flat[:, u % 2, 0:T * ew].rearrange("p (t w) -> p t w", t=T)
                            r = rows[k][:, u, :].rearrange("p (t w) -> p t w", t=T)[:, :, 0:ew]
                        else:
                            f = flat[:, u % 2, :].rearrange("p (j h w) -> p j h w", j=2, h=2)
                            r = rows[k][:, u, :].rearrange("p (h j w) -> p j h w", h=2, j=2)[:, :, :, 0:ew]
                        nc.scalar.copy(f, r).then_inc(flattened[k], 1)
                    s1, b1 = s - 1, (u + 1) % 2
                    if is_step(s1):
                        act.wait_ge(transposed[k], s1 + 1)
                        if not (isinstance(s1, int) and s1 < 2):
                            act.wait_ge(hidden[k], s1 - 1)
                        if k == 0:
                            nc.scalar.copy(efT[0:S, b1, 0:128], pz[0:S, 0, 0:128]).then_inc(copied[k], 1)
                        else:
                            nc.scalar.copy(efT[:, b1, :], pz[:, 0, 0:256]).then_inc(copied[k], 1)
                    s2, b2 = s - 2, u % 2
                    if is_step(s2):
                        act.wait_ge(hidden[k], s2 + 1)
                        if not (isinstance(s2, int) and s2 < 2):
                            act.wait_ge(weighted[k], s2 - 1)
                        h = hT[:, b2, :, :].rearrange("p j e -> p (j e)")
                        if k == 0:
                            nc.scalar.activation(h, pz[:, 1, 0:256], ACT.Silu, scale=0.25).then_inc(activated[k], 1)
                        else:
                            nc.scalar.activation(h, pz[:, 1, 0:256], ACT.Relu).then_inc(activated[k], 1)
                            u2, turn2 = (u - 2) % UN, s2 // UN if isinstance(s2, int) else turn - 1 if u < 2 else turn
                            act.wait_ge(gathered[1][u2 % SL], (use(u2, turn2) + 1) * (16 * T))
                            if not (isinstance(s2, int) and s2 < 2):
                                act.wait_ge(products[1], s2 * OPS[1] - OPS[1])
                            for t in range(T):
                                for m in range(3):
                                    h_m = rows[1][:, u2, t * ROWW[1] + SH[1] + m:t * ROWW[1] + SH[1] + m + 1]
                                    last = nc.scalar.activation(gsh[:, b2, t, m * F:(m + 1) * F], gath[:, u2 % SL, t * F:(t + 1) * F],
                                                                ACT.Copy, scale=h_m)
                            last.then_inc(scaled, 1)

                turns(act, body, 2, moves if k == 0 else None)

            act.wait_ge(s_w, 16 * N_W)
            act.wait_ge(s_const, 1)
            inv8, inv32 = S ** -0.5, V ** -0.5
            nc.scalar.mul(node_s[0][:, 0:S], raw_s[:, 0, :], inv8)
            nc.scalar.mul(node_s[0][:, S:2 * S], raw_s[:, 1, :], inv8)
            for m in range(3):
                is_m = comp[:, m:m + 1]
                nc.scalar.activation(node_v[0][:, V * m:V * m + V], raw_v[:, 0, :], ACT.Copy, scale=is_m)
                nc.scalar.activation(node_v[0][:, 96:192].rearrange("p (v m) -> p v m", m=3)[:, :, m], raw_v[:, 1, :], ACT.Copy, scale=is_m)
                nc.scalar.activation(node_v[1][:, V * m:V * m + V], raw_v[:, 2, :], ACT.Copy, scale=is_m)
                last = nc.scalar.activation(node_v[1][:, 96 + V * m:96 + V * m + V], raw_v[:, 3, :], ACT.Copy, scale=is_m)
                if m == 2:
                    last.then_inc(s_kron, 1)
            act.wait_ge(s_kron, 1)
            nc.scalar.mul(node_v[0][:, :], node_v[0][:, :], inv32)
            for o, i, w in ((0, 0, 64), (64, 128, 32), (96, 64, 64), (160, 160, 32)):
                nc.scalar.mul(fc2[0][:, o:o + w], raw_fc2[:, i:i + w], inv8)
            for k, w in ((0, S + 1), (1, 96)):
                nc.scalar.mul(out_s[k][S:96, 0:w], out_s[k][S:96, 0:w], 3 ** -0.5)
            nc.scalar.mul(out_v[1][96:128, :], out_v[1][96:128, :], 2 ** -0.5).then_inc(s_scaled, 1)

            act.wait_ge(s_x, 32)

            def prep(g):
                if not (isinstance(g, int) and g == 0):
                    act.wait_ge(s_xt[0], g * GB)
                nc.scalar.copy(xn[:, :, :], group_of(x_sb, g, F)).then_inc(s_xn[0], 1)
                node_prep_group(0, g)

            act.wait_ge(s_sq, 1)
            nc.scalar.activation(run, tmp, ACT.Sqrt).then_inc(s_len, 1)
            groups(act, prep)

            act.wait_ge(s_posd, 1)

            def assemble(j, u, turn):
                act.wait_ge(s_load[u], (turn + 1) * 32)
                if not (isinstance(turn, int) and turn == 0):
                    act.wait_ge(s_row0[u], turn * (16 * CH))
                c = bass.ds(j * CH, CH)
                r0 = row0[:, u, :, :]
                nc.scalar.copy(r0[:, :, 0:16], in16[:, u, :, :])
                nc.scalar.copy(r0[:, :, 16:20], in4[:, u, :, :])
                ri = r0.bitcast(I32)
                nc.scalar.copy(ri[:, :, IDX[0]:IDX[0] + 1], src_i[:, c].unsqueeze(2))
                nc.scalar.copy(ri[:, :, KEY[0]:KEY[0] + 1], dst_i[:, c].unsqueeze(2))
                nc.scalar.copy(at[:, u, :], dst_at[:, c]).then_inc(s_made, 1)
            for u in range(2):
                assemble(u, u, 0)
            with act.Fori(1, NCH // 2) as i:
                for u in range(2):
                    assemble(i * 2 + u, u, i)

            edge_loop(0)

            def between(g):
                finish_group(0, g)
                for u in range(SL):
                    moves(g * UN + LOOPED * UN + u, u, g + LOOPED)
                node_prep_group(1, g)
                for u in range(SL, UN):
                    moves(g * UN + LOOPED * UN + u, u, g + LOOPED)
            groups(act, between)
            edge_loop(1)
            groups(act, lambda g: finish_group(1, g))

        @block.vector
        def _(dve):
            chain = [0]

            def link(ins):
                chain[0] += 1
                ins.then_inc(s_sort, 1)
                dve.wait_ge(s_sort, chain[0])

            tt, ts, stt, cp = nc.vector.tensor_tensor, nc.vector.tensor_scalar, nc.vector.scalar_tensor_tensor, nc.vector.tensor_copy
            link(nc.vector.memset(next_i[:, EC - 1:EC], N))
            nc.vector.memset(fc1[0][:, :, :], 0.0)
            nc.vector.memset(fc1[1][:, :], 0.0).then_inc(s_zero, 1)
            nc.vector.memset(ones_row, 1.0)
            nc.vector.memset(ones[:, :], 1.0)
            for k in range(2):
                link(nc.vector.memset(tail[k], 0.0))
            for k in range(2):
                last = nc.vector.memset(tail[k][:, KEY[k]:KEY[k] + 1].bitcast(I32), 2 * N)
            last.then_inc(s_tail, 1)
            link(nc.vector.memset(dst_at, 0))
            dve.wait_ge(s_iota, 2)
            cp(iota[:, :], iota_i[:, :])
            link(cp(part[:, :], part_i[:, :]))
            r96 = part[0:96, 0:1].to_broadcast([96, 3])
            link(ts(comp3[:, :], r96, 1.0 / 3, -1.0 / 3, ALU.mult, ALU.add))
            link(ts(comp3[:, :], comp3[:, :], ROUND, ROUND, ALU.add, ALU.subtract))
            link(stt(comp3[:, :], comp3[:, :], 3.0, iota[0:96, 0:3], ALU.mult, ALU.add))
            ts(comp[:, :], comp3[:, :], part[0:96, 0:1], None, ALU.is_equal)
            ts(ident[:, :], iota[:, 0:128], part[:, 0:1], None, ALU.is_equal)
            ts(below, iota[:, 0:128], part[:, 0:1], None, ALU.is_gt)
            ts(upto, iota[:, 0:128], part[:, 0:1], None, ALU.is_ge).then_inc(s_const, 1)
            ts(big[:, :], part[0:NB, :], NB - 1.0, 1e6, ALU.is_equal, ALU.mult)
            ts(isblk, part[0:NB, 0:1].to_broadcast([NB, 128]), NB - 1.0, None, ALU.is_lt)
            dve.wait_ge(s_keys, 64)
            for k in range(2):
                link(ts(oh, key_i[k], 1.0 / BN, 0.5 / BN - 0.5, ALU.mult, ALU.add))
                link(ts(blk[k], oh, ROUND, ROUND, ALU.add, ALU.subtract))
            junk = (tmp, run)

            def count(b, first):
                for k in range(2):
                    if not first:
                        dve.wait_ge(s_count, b * 2 + k - 1)
                    ts(junk[k], blk[k], iota[0:EP, bass.ds(b, 1)], 0.0, ALU.is_equal, ALU.add,
                       accum_out=cnt[:, k, bass.ds(b, 1)]).then_inc(s_count, 1)
            count(0, True)
            with dve.Fori(1, NB) as b:
                count(b, False)
            dve.wait_ge(s_count, 2 * NB)
            link(tt(tmp, dst_i, next_i, ALU.is_gt))
            nc.vector.reduce_sum(viol[:, :], tmp, AX.X).then_inc(s_cnt, 1)
            dve.wait_ge(s_tot, 1)
            cp(flag_i[0:1, 0:1], pa[0:1, 0, 8:9]).then_inc(s_flag, 1)
            link(cp(tot[:, :], pa[0:NB, 0, 0:2]))
            link(ts(nst[:, :], tot[:, :], 1.0 / STEP, (STEP - 1.0) / STEP - 0.5 + 0.5 / STEP, ALU.mult, ALU.add))
            ts(nst[:, :], nst[:, :], ROUND, ROUND, ALU.add, ALU.subtract).then_inc(s_nst, 1)
            dve.wait_ge(s_nst, 1)
            link(stt(wgt[:, :], nst[:, :], -float(STEP), tot[:, :], ALU.mult, ALU.add))
            link(ts(wgt[:, :], wgt[:, :], big[:, 0:1], None, ALU.add))
            dve.wait_ge(s_cum, 1)
            link(cp(cum[:, :], pa[0:NB, 0, 16:18]))
            for k in range(2):
                ts(totb[:, k, :], ones[0:NB, :], tot[:, k:k + 1], None, ALU.mult)
                last = ts(reach[:, k, :], iota[0:NB, :], cum[:, k:k + 1], None, ALU.is_ge)
            last.then_inc(s_reach, 1)
            dve.wait_ge(s_tab, 1)
            for k in range(2):
                link(stt(start_f[:, :], iota[0:1, :], float(STEP), pa[0:1, k, 32:32 + NSTEP], ALU.mult, ALU.add))
                ts(start_i[k][:, :], start_f[:, :], float(E), float(ROWW[k]), ALU.min, ALU.mult)
                ts(accoff_i[k][:, :], pa[0:1, k, 256:256 + NSTEP], float(MW), None, ALU.mult)
                ts(blk125[:, k, :], pa[:, k, 256:256 + NSTEP], float(BN), None, ALU.mult)
                link(cp(pre[:, k, :], pz[0:EP, k, 0:NB]))
            nc.vector.memset(oh, 0.0).then_inc(s_tabs, 1)

            dve.wait_ge(s_e3, 16)
            link(tt(sh_all, ea3, ea3, ALU.mult))
            nc.vector.tensor_reduce(tmp, sh_all, AX.X, ALU.add).then_inc(s_sq, 1)
            dve.wait_ge(s_len, 1)
            link(nc.vector.reciprocal(oh, run))
            link(ts(oh, oh, 3 ** 0.5, None, ALU.mult))
            cp(meta[:, :, 4:5].bitcast(I32), dst_i.unsqueeze(2))
            cp(meta[:, :, 5:6].bitcast(I32), src_i.unsqueeze(2))
            tt(sh_all, ea3, oh.unsqueeze(2).to_broadcast([EP, EC, 3]), ALU.mult).then_inc(s_shd, 1)
            dve.wait_ge(s_shd, 1)
            cp(meta[:, :, 3:4], meta[:, :, 0:1])

            def places(k, sem_chain, done, ready):
                nc.vector.memset(pos_f, 0.0).then_inc(sem_chain, 1)

                def one(b, n):
                    dve.wait_ge(sem_chain, n)
                    ts(oh, blk[k], iota[0:EP, bass.ds(b, 1)], None, ALU.is_equal).then_inc(sem_chain, 1)
                    dve.wait_ge(sem_chain, n + 1)
                    nc.vector.tensor_tensor_scan(run, ones_row, oh, pre[:, k, bass.ds(b, 1)], ALU.mult, ALU.add).then_inc(sem_chain, 1)
                    dve.wait_ge(sem_chain, n + 2)
                    tt(tmp, run, oh, ALU.mult).then_inc(sem_chain, 1)
                    dve.wait_ge(sem_chain, n + 3)
                    tt(pos_f, pos_f, tmp, ALU.add).then_inc(sem_chain, 1)
                with dve.Fori(0, NB) as b:
                    one(b, b * 4 + 1)
                dve.wait_ge(sem_chain, 4 * NB + 1)
                ts(pos_i[k], pos_f.unsqueeze(2), -1.0, None, ALU.add).then_inc(done, 1)
                dve.wait_ge(done, ready)

            unsorted = dve.value_load(flag_i[0:1, 0:1], min_val=0, max_val=E)
            with dve.If(unsorted != 0):
                places(0, s_pd, s_pdd, 1)
            nc.vector.memset(kl[:, :], 0.0).then_inc(s_posd, 1)
            places(1, s_ps, s_meta, 1)

            def clear(k):
                nc.vector.memset(acc[:, :], 0.0).then_inc(s_clear, 1)
                dve.wait_ge(s_clear, k + 1)

            def edge_loop(k):
                P = products[k]

                def is_step(s):
                    return not isinstance(s, int) or 0 <= s < NSTEP

                def add(s, b):
                    at_ = dve.value_load(accoff_i[k][0:1, bass.ds(s, 1)], min_val=0, max_val=(NB - 1) * MW)
                    dve.wait_ge(scattered[k], s + 1)
                    if not (isinstance(s, int) and s < 1):
                        dve.wait_ge(added[k], s)
                    mw = CNT + 1 if k == 0 else MW
                    a = acc[:, bass.ds(at_, mw)]
                    tt(a, a, pa[0:BN, b, 0:mw], ALU.add).then_inc(added[k], 1)

                def body(s, u, turn):
                    if is_step(s):
                        b = u % 2
                        R = rows[k][:, u, :].rearrange("p (t w) -> p t w", t=T)
                        G = gath[:, u % SL, :].rearrange("p (t f) -> p t f", t=T)
                        Gs = G[:, :, 0:S]
                        Gv = G[:, :, S:F].rearrange("p t (m v) -> p t m v", m=3)
                        Wt = pw[:, b, :, :]
                        M = msg[:, b, :, :]
                        vw = 96 if k == 0 else 128
                        Mv = M[:, :, 96:480].rearrange("p t (m w) -> p t m w", m=3) if k == 1 else \
                            M[:, :, 160:448].rearrange("p t (m w) -> p t m w", m=3)
                        sh = R[:, :, SH[k]:SH[k] + 3].unsqueeze(3)
                        shv = sh.to_broadcast([128, T, 3, V])
                        shs = sh.to_broadcast([128, T, 3, S])
                        tqb = tq[:, :, :].unsqueeze(2).to_broadcast([128, T, 3, S])

                        def wv(o):
                            return Wt[:, :, o:o + V].unsqueeze(2).to_broadcast([128, T, 3, V])

                        A4 = ta[:, :, :].rearrange("p t (m v) -> p t m v", m=3)
                        base = s * OPS[k]

                        def after(n):
                            dve.wait_ge(P, base + n)

                        dve.wait_ge(rows_in[k][u], (turn + 1) * 16)
                        if not (isinstance(s, int) and s < 1):
                            after(0)
                        key = R[:, :, KEY[k]:KEY[k] + 1].rearrange("p t o -> p (t o)").bitcast(I32)
                        ts(kl[:, :], key, blk125[:, k, bass.ds(s, 1)], None, ALU.subtract).then_inc(P, 1)
                        if not (isinstance(s, int) and s < 2):
                            dve.wait_ge(scattered[k], s - 1)
                        dve.wait_ge(weighted[k], s + 1)
                        dve.wait_ge(gathered[k][u % SL], (use(u, turn) + 1) * (16 * T))
                        if k == 0:
                            tt(tu[:, :, :], Wt[:, :, 0:96], R[:, :, 16:17].to_broadcast([128, T, 96]), ALU.mult).then_inc(P, 1)
                            tt(tq[:, :, :], Wt[:, :, 96:160], Gs, ALU.mult).then_inc(P, 1)
                            tt(A4, Gv, shv, ALU.mult).then_inc(P, 1)
                            after(1)
                            tt(hot[:, b, :, :], iota[:, 0:BN].unsqueeze(1).to_broadcast([128, T, BN]),
                               kl[:, :].unsqueeze(2).to_broadcast([128, T, BN]), ALU.is_equal).then_inc(P, 1)
                            after(2)
                            tt(M[:, :, 0:S], tu[:, :, 0:S], Gs, ALU.mult).then_inc(P, 1)
                            tt(Mv[:, :, :, S:96], tu[:, :, S:96].unsqueeze(2).to_broadcast([128, T, 3, V]), Gv, ALU.mult).then_inc(P, 1)
                            after(3)
                            tt(Mv[:, :, :, 0:S], tqb, shs, ALU.mult).then_inc(P, 1)
                            after(4)
                            tt(M[:, :, S:F].rearrange("p t (m v) -> p t m v", m=3), A4, wv(160), ALU.mult).then_inc(P, 1)
                        else:
                            dve.wait_ge(scaled, s + 1)
                            X = gsh[:, b, :, :]

                            def comps(o, n):
                                a = X[:, :, o:o + V]
                                return bass.AP(tensor=a.tensor, offset=a.offset, ap=[a.ap[0], a.ap[1], (192, n), (1, V)])
                            d = comps(S, 3)
                            d = bass.AP(tensor=d.tensor, offset=d.offset, ap=[d.ap[0], d.ap[1], (1, V), (192, 3)])
                            nc.vector.tensor_reduce(td[:, :, :], d, AX.X, ALU.add).then_inc(P, 1)
                            after(1)
                            tt(hot[:, b, :, :], iota[:, 0:BN].unsqueeze(1).to_broadcast([128, T, BN]),
                               kl[:, :].unsqueeze(2).to_broadcast([128, T, BN]), ALU.is_equal).then_inc(P, 1)
                            tt(A4[:, :, 0:2, :], comps(224, 2), comps(96, 2), ALU.subtract).then_inc(P, 1)
                            tt(A4[:, :, 2:3, :], comps(128, 1), comps(384, 1), ALU.subtract).then_inc(P, 1)
                            tt(M[:, :, 0:S], Wt[:, :, 0:S], Gs, ALU.mult).then_inc(P, 1)
                            tt(Mv[:, :, :, 0:S], X.rearrange("p t (m f) -> p t m f", m=3)[:, :, :, 0:S],
                               Wt[:, :, S:2 * S].unsqueeze(2).to_broadcast([128, T, 3, S]), ALU.mult).then_inc(P, 1)
                            tt(Mv[:, :, :, S:96], Gv, wv(128), ALU.mult).then_inc(P, 1)
                            after(5)
                            tt(M[:, :, S:96], td[:, :, :], Wt[:, :, 160:192], ALU.mult).then_inc(P, 1)
                            tt(Mv[:, :, :, 96:128], A4, wv(192), ALU.mult).then_inc(P, 1)
                    s1 = s - 1
                    if is_step(s1):
                        add(s1, (u + 1) % 2)
                turns(dve, body, 1)
                dve.wait_ge(added[k], NSTEP)

            def normalise(k, g, n, base):
                C = s_fin[k]

                def after(m):
                    dve.wait_ge(C, base + m)
                for j in range(GB):
                    last = nc.vector.bn_stats(stats[:, j, :], y[:, j, :])
                last.then_inc(C, 1)
                after(n + 1)
                dve.sem_inc(passed[2], 1)
                for j in range(GB):
                    last = nc.vector.bn_aggr(mv[:, j, :], stats[:, j, :])
                last.then_inc(C, 1)
                after(n + 2)
                ts(small[:, 5, :].unsqueeze(2), mv[:, :, 1:2], EPS, None, ALU.add).then_inc(C, 1)
                dve.wait_ge(s_rt[k], g + 1)
                nc.vector.reciprocal(small[:, 7, :], small[:, 6, :]).then_inc(C, 1)
                after(n + 4)

            def scaled_out(j):
                return ts(xn[:, j, :], y[:, j, :], mv[:, j, 0:1], small[:, 7, j:j + 1], ALU.subtract, ALU.mult)

            def between(g):
                first = isinstance(g, int) and g == 0
                C = s_fin[0]
                base = g * FIN[0]

                def after(m):
                    dve.wait_ge(C, base + m)
                if not first:
                    after(0)
                a = group_of(acc, g, MW)
                ts(small[:, 0, :].unsqueeze(2), a[:, :, CNT:CNT + 1], 1.0, None, ALU.max).then_inc(C, 1)
                if not first:
                    dve.wait_ge(s_at[0], g * GB)
                cp(st[:, :, 0:S], a[:, :, 0:S])
                nc.vector.tensor_reduce(st[:, :, S:96], a[:, :, S:F].rearrange("p b (m v) -> p b v m", m=3), AX.X, ALU.add)
                cp(st[:, :, 96:384], a[:, :, F:CNT]).then_inc(s_st[0], 1)
                after(1)
                nc.vector.reciprocal(small[:, 1, :], small[:, 0, :]).then_inc(C, 1)
                after(2)
                stt(small[:, 2, :], small[:, 1, :], 96 ** -0.5, attr[:, bass.ds(g * GB, GB)], ALU.mult, ALU.mult).then_inc(C, 1)
                after(3)
                tt(small[:, 3, :], small[:, 2, :], small[:, 2, :], ALU.mult).then_inc(C, 1)
                tt(y[:, :, :], group_of(x_sb, g, F), group_of(side, g, SIDE)[:, :, 0:F], ALU.add).then_inc(C, 1)
                dve.wait_ge(s_ao[0], g * GB + GB)
                after(4)
                tt(small[:, 4, :].unsqueeze(2), po[:, :, F:F + 1], small[:, 3, :].unsqueeze(2), ALU.mult).then_inc(C, 1)
                after(6)
                tt(tm[:, :, 0:F], po[:, :, 0:F], small[:, 4, :].unsqueeze(2).to_broadcast([BN, GB, F]), ALU.mult).then_inc(C, 1)
                after(7)
                tt(y[:, :, 0:S], y[:, :, 0:S], tm[:, :, 0:S], ALU.add)
                yv = y[:, :, S:F].rearrange("p b (v m) -> p b m v", m=3)
                tt(yv, yv, tm[:, :, S:F].rearrange("p b (m v) -> p b m v", m=3), ALU.add).then_inc(C, 1)
                after(8)
                normalise(0, g, 8, base)
                if not first:
                    dve.wait_ge(s_xt[1], g * GB)
                for j in range(GB):
                    last = scaled_out(j)
                last.then_inc(C, 1)
                after(13)
                cp(group_of(xp, g, F), xn[:, :, :]).then_inc(s_xn[1], 1)

            def last_stage(g):
                first = isinstance(g, int) and g == 0
                C = s_fin[1]
                base = g * FIN[1]

                def after(m):
                    dve.wait_ge(C, base + m)
                if not first:
                    after(0)
                    dve.wait_ge(s_at[1], g * GB)
                a = group_of(acc, g, MW)
                av, sv = (t[:, :, 96:MW].rearrange("p b (m w) -> p b m w", m=3) for t in (a, st[:, :, :]))
                ts(st[:, :, 0:96], a[:, :, 0:96], 1.0 / 32, None, ALU.mult)
                ts(sv[:, :, :, 0:96], av[:, :, :, 0:96], 1.0 / 32, None, ALU.mult)
                ts(sv[:, :, 0:2, 96:128], av[:, :, 1:3, 96:128], 1.0 / 32, None, ALU.mult)
                ts(sv[:, :, 2, 96:128], av[:, :, 0, 96:128], 1.0 / 32, None, ALU.mult).then_inc(s_st[1], 1)
                dve.wait_ge(s_ao[1], g * GB + GB)
                tt(tm[:, :, :], po[:, :, 0:SIDE], group_of(side, g, SIDE), ALU.add).then_inc(C, 1)
                nc.vector.memset(small[:, 0, :], 0.0).then_inc(C, 1)
                dve.wait_ge(s_act[1], g + 1)
                X = group_of(xp, g, F)
                tt(y[:, :, 0:S], X[:, :, 0:S], fs[:, :, 0:S], ALU.add)
                tv = tm[:, :, 96:192].rearrange("p b (m v) -> p b m v", m=3)
                tt(tv, tv, fs[:, :, S:96].unsqueeze(2).to_broadcast([BN, GB, 3, V]), ALU.mult).then_inc(C, 1)
                after(3)
                tt(y[:, :, S:F].rearrange("p b (v m) -> p b m v", m=3), X[:, :, S:F].rearrange("p b (v m) -> p b m v", m=3), tv,
                   ALU.add).then_inc(C, 1)
                after(4)
                normalise(1, g, 4, base)
                if not first:
                    dve.wait_ge(s_put, 16 * g)
                for j in range(GB):
                    last = scaled_out(j)
                last.then_inc(C, 1)

            dve.wait_ge(s_made, NCH)
            for u in range(2):
                dve.wait_ge(s_row0[u], 16 * CH * (NCH // 2))
            dve.wait_ge(s_metaw, 16)
            clear(0)
            link(nc.vector.memset(msg[:, :, :, CNT:CNT + 1], 1.0))
            edge_loop(0)
            groups(dve, between)
            clear(1)
            edge_loop(1)
            groups(dve, last_stage)


_INS = ["x", "src", "dst", "edge_attr_16", "edge_attr_3", "edge_attr_4", "edge_attr_64", "node_vec1",
        "L0_gnn_Wfc1", "L0_gnn_Wfc2", "L0_gnn_Wsc0", "L0_gnn_Wsc1", "L0_gnn_Wl1_0", "L0_gnn_Wl1_1",
        "L0_gnn_Wl2_s", "L0_gnn_Wl2_v", "L0_gnn_Wa",
        "L1_gnn_W_skip0", "L1_gnn_W_skip1", "L1_gnn_W_nl0", "L1_gnn_W_nl1", "L1_gnn_W_fc1", "L1_gnn_W_fc2",
        "L1_gnn_W_out_s", "L1_gnn_W_out_v"]


def kernel(**inputs):
    import numpy as _np
    import concourse.bacc as _bacc
    from concourse.bass_utils import run_bass_kernel_spmd as _run

    nc = _bacc.Bacc("TRN2", target_bir_lowering=False, num_devices=1)
    arrays, args = {}, []
    for name in _INS:
        a = _np.ascontiguousarray(inputs[name])
        arrays[f"in_{name}"] = a
        args.append(nc.dram_tensor(f"in_{name}", a.shape, mybir.dt.from_np(a.dtype), kind="ExternalInput").ap())
    args.append(nc.dram_tensor("out_0", (N, F), F32, kind="ExternalOutput").ap())
    gnn_kernel(nc, *args)
    r = _run(nc, [arrays], core_ids=[0])
    return r.results[0]["out_0"]
```

```python
from contextlib import ExitStack

import concourse.bass as bass
from concourse import mybir

F32 = mybir.dt.float32
I32 = mybir.dt.int32
ALU = mybir.AluOpType
ACT = mybir.ActivationFunctionType
AX = mybir.AxisListType

N = 3125
E = 100000
S, V = 64, 32
F = S + 3 * V
BN = 125
NB = N // BN
GB = 5
NG = NB // GB
EP = 125
EC = E // EP
TILE = 128
T = 4
STEP = T * TILE
PARTS = (2, 2)
PIECE = tuple(STEP // h for h in PARTS)
NSTEP = tuple(-(-(NB + (E - NB) // PIECE[k]) // PARTS[k]) for k in range(2))
NPIECE = tuple(NSTEP[k] * PARTS[k] for k in range(2))
UN = 8
SL = 4
CH = 40
NCH = EC // CH
SC = 4
MOVES = EC // SC
LATER = MOVES - NG * UN
WHOLE = tuple(n // UN for n in NSTEP)
SPARSE = (WHOLE[0] * UN - LATER) // SL
DENSE = WHOLE[0] - SPARSE
META = 6
MW = 480
CNT = 448
PW = 256
SIDE = 192
ROUND = 1.5 * 2 ** 23
EPS = 1e-5
assert NB * BN == N and EP * EC == E and NCH * CH == EC and NCH % 2 == 0
assert all(n % SL == 0 for n in NSTEP) and all(n <= 512 for n in NPIECE)
assert MOVES * SC == EC and DENSE * UN + SPARSE * SL == LATER and LATER % SL == 0 and UN == 2 * SL
assert NCH == 4 * NG and GB == NB // NG

ROWW = (22, 70)
SH = (17, 64)
IDX = (20, 68)
KEY = (21, 69)
KEEP = (F, SIDE)
OPS = (9, 10)
FIN = (13, 9)
ROOT = (11, 7)
READ = (7, 1)
N_W = 31


def gnn_kernel(nc, x, src, dst, edge_attr_16, edge_attr_3, edge_attr_4, edge_attr_64, node_vec1,
               Wfc1, Wfc2, Wsc0, Wsc1, Wl1_0, Wl1_1, Wl2_s, Wl2_v, Wa,
               W_skip0, W_skip1, W_nl0, W_nl1, W_fc1, W_fc2, W_out_s, W_out_v, out):
    with ExitStack() as ctx:
        def sb(name, shape, dt=F32):
            return ctx.enter_context(nc.sbuf_tensor(name, shape, dt))

        def sem(name):
            return ctx.enter_context(nc.semaphore(name))

        table = [nc.dram_tensor(f"table{k}", (N, F), F32).ap() for k in range(2)]
        ordered = [nc.dram_tensor(f"ordered{k}", (E + STEP, ROWW[k]), F32).ap() for k in range(2)]
        meta_d = nc.dram_tensor("meta", (EP, EC * META), F32).ap()
        place_d = nc.dram_tensor("place", (EP, EC), I32).ap()


        part_i = sb("part_i", [128, 1], I32)
        iota = sb("iota", [128, max(NPIECE)])
        part = sb("part", [128, 1])
        ident = sb("ident", [128, 128])

        ones = sb("ones", [128, 128])
        x_sb = sb("x_sb", [BN, NB * F])
        xp = sb("xp", [BN, NB * F])
        side = sb("side", [BN, NB * SIDE])
        acc = sb("acc", [BN, NB * MW])
        attr = sb("attr", [BN, NB])
        xn = sb("xn", [BN, GB, F])
        xT = sb("xT", [96, GB, 2, BN])
        st = sb("st", [BN, GB, MW])
        sT = sb("sT", [128, 2, 4 * BN])


        small = sb("small", [BN, 8, GB])
        stats = sb("stats", [BN, GB, 6])
        mv = sb("mv", [BN, GB, 2])

        comp = sb("comp", [96, 3])
        comp3 = sb("comp3", [96, 3])

        node_s = [sb("node_s0", [S, 2 * S]), sb("node_s1", [S, S + 96])]
        node_v = [sb("node_v0", [96, 192]), sb("node_v1", [96, 192])]
        fc1 = [sb("fc1_0", [S, 2, 128]), sb("fc1_1", [128, 128])]
        fc2 = [sb("fc2_0", [128, 192]), sb("fc2_1", [128, 224])]
        out_s = [sb("out_s0", [96, S + 1]), sb("out_s1", [96, 96])]
        out_v = [sb("out_v0", [96, V]), sb("out_v1", [128, V])]
        cnt = sb("cnt", [EP, 2, NB])
        half = sb("half", [EP, NB])
        signs = sb("signs", [EP, NB + 1])
        viol = sb("viol", [EP, 1])
        tot = sb("tot", [NB, 2])
        nst = sb("nst", [NB, 2])
        cum = sb("cum", [NB, 2])
        wgt = sb("wgt", [NB, 2])
        big = sb("big", [NB, 1])

        pre = sb("pre", [EP, 2, NB])
        blk125 = [sb(f"blk125_{k}", [128, NPIECE[k]]) for k in range(2)]
        start_i = [sb(f"start_i{k}", [1, NPIECE[k]], I32) for k in range(2)]
        accoff_i = [sb(f"accoff_i{k}", [1, NPIECE[k]], I32) for k in range(2)]
        flag_i = sb("flag_i", [1, 1], I32)
        at = sb("at", [EP, 2, CH], I32)
        rows1 = sb("rows1", [128, UN, T * ROWW[1]])
        rows0 = rows1[:, :, :].rearrange("p u w -> p (u w)")[:, 0:UN * T * ROWW[0]]
        rows = [rows0.rearrange("p (u w) -> p u w", u=UN), rows1[:, :, :]]
        tail = [rows[0][:, 0, 0:ROWW[0]], rows[1][:, UN - 1, 0:ROWW[1]]]
        gath = sb("gath", [128, SL, T * F])
        flat = sb("flat", [128, 2, T * 64])
        fs = flat[0:BN, :, :].rearrange("p b w -> p (b w)")[:, 0:GB * 96].rearrange("p (b w) -> p b w", w=96)
        efT = sb("efT", [128, 2, 2 * 128])
        hT = sb("hT", [128, 2, 2, 128])
        msg = sb("msg", [128, 2, T, MW])
        hot = sb("hot", [128, 2, T, BN])
        kl = sb("kl", [128, T])
        tu = sb("tu", [128, T, 96])
        tq = sb("tq", [128, T, S])
        ta = sb("ta", [128, T, 3 * V])
        td = sb("td", [128, T, V])
        gsh = sb("gsh", [128, 2, T, 3 * F])

        gathf = gath[:, :, :].rearrange("p u w -> p (u w)")
        isblk = gathf[0:NB, 0:128]
        totb = gathf[0:NB, 128:384].rearrange("p (k w) -> p k w", k=2)
        below = gathf[:, 384:512]
        upto = gathf[:, 512:640]
        raw_v = gathf[0:96, 640:768].rearrange("p (k v) -> p k v", k=4)
        raw_s = gathf[0:S, 768:896].rearrange("p (k v) -> p k v", k=2)
        raw_fc2 = gathf[:, 896:1088]
        reach = [gathf[0:NB, 1088:1088 + NPIECE[0]], gathf[0:NB, 1088 + NPIECE[0]:1088 + sum(NPIECE)]]
        over = 1088 + sum(NPIECE)
        iota_i = gathf[:, over:over + max(NPIECE)].bitcast(I32)


        def carve(whole, at_, *shape):
            n = 1
            for s in shape:
                n *= s
            flat = whole[0:EP, at_:at_ + n]
            return flat if len(shape) == 1 else flat.rearrange(
                "p (a b) -> p a b" if len(shape) == 2 else "p (a b c) -> p a b c",
                **dict(zip("abc", shape)))

        dst_i = acc[:, 0:EC].bitcast(I32)
        src_i = acc[:, EC:2 * EC].bitcast(I32)
        key_i = [dst_i, src_i]
        next_i = acc[:, 2 * EC:3 * EC].bitcast(I32)
        blk = [acc[:, 3 * EC:4 * EC], acc[:, 4 * EC:5 * EC]]
        gflat = gsh[:, :, :, :].rearrange("p b t w -> p (b t w)")
        oh = carve(gflat, 0, EC)
        run = carve(gflat, EC, EC)
        tmp = carve(gflat, 2 * EC, EC)
        pos_f = carve(gflat, 3 * EC, EC)
        ones_row = acc[:, 5 * EC:6 * EC]
        meta = acc[:, 6 * EC:12 * EC].rearrange("p (c m) -> p c m", m=META)
        sh_all = meta[:, :, 0:3]
        dst_at = acc[:, 13 * EC:14 * EC].bitcast(I32)
        src_at = acc[:, 12 * EC:13 * EC].bitcast(I32)
        ea3 = st[:, :, :].rearrange("p g w -> p (g w)").rearrange("p (c m) -> p c m", m=3)
        mflat = msg[:, :, :, :].rearrange("p b t w -> p (b t w)")
        y = carve(mflat, 0, GB, F)
        tm = carve(mflat, GB * F, GB, SIDE)
        row0 = carve(mflat, 0, 2, CH, ROWW[0])
        start_f = mflat[0:1, 2 * CH * (ROWW[0] + 20):2 * CH * (ROWW[0] + 20) + max(NPIECE)]
        in16 = carve(mflat, 2 * CH * ROWW[0], 2, CH, 16)
        in4 = carve(mflat, 2 * CH * (ROWW[0] + 16), 2, CH, 4)
        in64 = carve(gflat, 0, SL, SC, 64)
        inmeta = carve(gflat, SL * SC * 64, SL, SC, META)
        row1 = carve(gflat, SL * SC * (64 + META), SL, SC, ROWW[1])
        inplace = carve(gflat, SL * SC * (64 + META + ROWW[1]), SL, SC).bitcast(I32)

        pw = ctx.enter_context(nc.psum_tensor("pw", [128, 2, T, PW], F32))
        pz = ctx.enter_context(nc.psum_tensor("pz", [128, 2, 512], F32))
        pa = ctx.enter_context(nc.psum_tensor("pa", [128, 2, 512], F32))

        banks = pw[:, :, :, :].rearrange("p b (h t) w -> p b h (t w)", h=2)
        po = pw[0:BN, :, :, :].rearrange("p b t w -> p (b t) w")[:, 0:GB, :]

        s_keys = sem("s_keys")
        s_next = sem("s_next")
        s_x = sem("s_x")
        s_e3 = sem("s_e3")
        s_w = sem("s_w")
        s_iota = sem("s_iota")
        s_const = sem("s_const")
        s_zero = sem("s_zero")
        s_kron = sem("s_kron")
        s_scaled = sem("s_scaled")
        s_sort = sem("s_sort")
        s_blk = sem("s_blk")
        s_count = sem("s_count")
        s_signs = sem("s_signs")
        s_cnt = sem("s_cnt")
        s_tot = sem("s_tot")
        s_nst = sem("s_nst")
        s_cum = sem("s_cum")
        s_reach = sem("s_reach")
        s_tab = sem("s_tab")
        s_tabs = sem("s_tabs")
        s_flag = sem("s_flag")
        s_posd = sem("s_posd")
        s_pd = sem("s_pd")
        s_pdd = sem("s_pdd")
        s_ps = sem("s_ps")
        s_term = sem("s_term")
        s_placed = sem("s_placed")
        s_sq = sem("s_sq")
        s_len = sem("s_len")
        s_shd = sem("s_shd")
        s_tail = sem("s_tail")
        s_tailw = sem("s_tailw")
        s_load = [sem("s_load0"), sem("s_load1")]
        s_made = sem("s_made")
        s_row0 = [sem("s_row00"), sem("s_row01")]
        s_meta = sem("s_meta")
        s_metaw = sem("s_metaw")
        s_load1 = [sem(f"s_load1{u}") for u in range(SL)]
        s_made1 = sem("s_made1")
        s_row1 = [sem(f"s_row1{u}") for u in range(SL)]
        scaled = sem("scaled")
        s_clear = sem("s_clear")
        s_table = [sem("s_table0"), sem("s_table1")]
        s_out = sem("s_out")
        passed = [sem("passed_sp"), sem("passed_pool"), sem("passed_dve"), sem("passed_pe")]
        s_xn = [sem("s_xn0"), sem("s_xn1")]
        s_xt = [sem("s_xt0"), sem("s_xt1")]
        s_xc = [sem("s_xc0"), sem("s_xc1")]
        s_mm = [sem("s_mm0"), sem("s_mm1")]
        s_ev = [sem("s_ev0"), sem("s_ev1")]
        s_st = [sem("s_st0"), sem("s_st1")]
        s_at = [sem("s_at0"), sem("s_at1")]
        s_ac = [sem("s_ac0"), sem("s_ac1")]
        s_ao = [sem("s_ao0"), sem("s_ao1")]
        s_fin = [sem("s_fin0"), sem("s_fin1")]
        s_act = [sem("s_act0"), sem("s_act1")]
        s_rt = [sem("s_rt0"), sem("s_rt1")]
        s_put = sem("s_put")
        rows_in = [[sem(f"rows_in{k}{u}") for u in range(UN)] for k in range(2)]
        gathered = [[sem(f"gathered{k}{u}") for u in range(SL)] for k in range(2)]
        flattened = [sem("flattened0"), sem("flattened1")]
        transposed = [sem("transposed0"), sem("transposed1")]
        copied = [sem("copied0"), sem("copied1")]
        hidden = [sem("hidden0"), sem("hidden1")]
        activated = [sem("activated0"), sem("activated1")]
        weighted = [sem("weighted0"), sem("weighted1")]
        products = [sem("products0"), sem("products1")]
        scattered = [sem("scattered0"), sem("scattered1")]
        added = [sem("added0"), sem("added1")]

        block = ctx.enter_context(nc.Block())

        def turns(eng, k, body, after, moves=None):
            for u in range(UN):
                body(u, u, 0)
                if moves:
                    moves(u, u % SL, u // SL)
            with eng.Fori(1, DENSE if moves else WHOLE[k]) as i:
                for u in range(UN):
                    body(i * UN + u, u, i)
                    if moves:
                        moves(i * UN + u, u % SL, use(u, i))
            if moves:
                with eng.Fori(DENSE, WHOLE[k]) as i:
                    for u in range(UN):
                        body(i * UN + u, u, i)
                        if u % 2 == 0:
                            moves(i * SL + (DENSE * SL + u // 2), u // 2, i + DENSE)
            for s in range(WHOLE[k] * UN, NSTEP[k] + after):
                body(s, s % UN, s // UN)

        def late_moves(moves, g, part):
            for u in range(part * SL, part * SL + SL):
                moves(g * UN + (LATER + u), u % SL, g * 2 + (LATER // SL + u // SL))

        def before(s, n):
            return isinstance(s, int) and s < n

        def use(u, turn):
            return turn * (UN // SL) + u // SL

        def groups(eng, body):
            body(0)
            with eng.Fori(1, NG) as g:
                body(g)

        def staggered(eng, a, b):
            a(0)
            a(1)
            b(0)
            with eng.Fori(1, NG - 1) as g:
                a(g + 1)
                b(g)
            b(NG - 1)

        def group_of(t, g, width):
            return t[:, bass.ds(g * (GB * width), GB * width)].rearrange("p (b w) -> p b w", w=width)

        @block.sync
        def _(sp):
            last = EC - 1
            kd = dst.rearrange("(p c) -> p c", p=EP)
            ks = src.rearrange("(p c) -> p c", p=EP)
            sp.dma_start(dst_i, kd).then_inc(s_keys, 16)
            sp.dma_start(src_i, ks).then_inc(s_keys, 16)
            nxt = dst[1:1 + (EP - 1) * EC].rearrange("(p c) -> p c", p=EP - 1)
            sp.wait_ge(s_sort, 1)
            sp.dma_start(next_i[0:EP - 1, :], nxt).then_inc(s_next, 16)
            sp.dma_start(next_i[EP - 1:EP, 0:last], dst[E - EC + 1:E].rearrange("(a c) -> a c", a=1)).then_inc(s_next, 16)
            sp.dma_start(x_sb[:, :].rearrange("p (b f) -> p b f", f=F), x.rearrange("(b p) f -> p b f", p=BN)).then_inc(s_x, 16)
            with nc.allow_non_contiguous_dma(reason="one number of each node"):
                sp.dma_start(attr[:, :].unsqueeze(2), node_vec1.rearrange("(b p) f -> p b f", p=BN)).then_inc(s_x, 16)
            sp.dma_start(st[:, :, :].rearrange("p g w -> p (g w)"), edge_attr_3.rearrange("(p c) m -> p (c m)", p=EP)).then_inc(s_e3, 16)
            for k, w in enumerate((Wl1_1, Wsc1, W_nl1, W_skip1)):
                for m in range(3):
                    sp.dma_start(raw_v[m:96:3, k, :], w).then_inc(s_w, 16)
            sp.dma_start(raw_s[:, 0, :], Wl1_0).then_inc(s_w, 16)
            sp.dma_start(raw_s[:, 1, :], Wsc0).then_inc(s_w, 16)
            sp.dma_start(node_s[1][:, 0:S], W_nl0).then_inc(s_w, 16)
            sp.dma_start(node_s[1][:, S:S + 96], W_skip0).then_inc(s_w, 16)
            for h in range(2):
                sp.dma_start(raw_fc2[S * h:S * h + S, :], Wfc2).then_inc(s_w, 16)
                sp.dma_start(fc2[1][S * h:S * h + S, :], W_fc2).then_inc(s_w, 16)
            sp.dma_start(out_s[0][:, 0:S], Wl2_s).then_inc(s_w, 16)
            sp.dma_start(out_s[0][:, S:S + 1], Wa).then_inc(s_w, 16)
            sp.dma_start(out_v[0][:, :], Wl2_v).then_inc(s_w, 16)
            sp.dma_start(out_s[1][:, :], W_out_s).then_inc(s_w, 16)
            sp.dma_start(out_v[1][:, :], W_out_v).then_inc(s_w, 16)
            sp.wait_ge(s_zero, 1)
            for t in range(T):
                sp.dma_start(fc1[0][16 * t:16 * t + 16, t % 2, S * (t // 2):S * (t // 2) + S], Wfc1).then_inc(s_w, 16)
            for h in range(2):
                sp.dma_start(fc1[1][S * h:S * h + S, S * h:S * h + S], W_fc1).then_inc(s_w, 16)
            sp.wait_ge(s_tail, 1)
            for k in range(2):
                for q in range(T):
                    dram = ordered[k][E + q * TILE:E + (q + 1) * TILE, :]
                    sp.dma_start(dram, tail[k]).then_inc(s_tailw, 16)

            d16 = edge_attr_16.rearrange("(p c) f -> p (c f)", p=EP)
            d4 = edge_attr_4.rearrange("(p c) f -> p (c f)", p=EP)
            d64 = edge_attr_64.rearrange("(p c) f -> p (c f)", p=EP)
            o0 = ordered[0][0:E, :].rearrange("(p c) w -> p (c w)", p=EP)

            def load(j, u):
                for t, d, w in ((in16, d16, 16), (in4, d4, 4)):
                    sp.dma_start(t[:, u, :, :].rearrange("p c w -> p (c w)"),
                                 d[:, bass.ds(j * (CH * w), CH * w)]).then_inc(s_load[u], 16)

            def store(j, u):
                sp.wait_ge(s_made, j + 1)
                sp.sem_inc(passed[0], 1)
                with sp.If(unsorted == 0):
                    n = CH // 4 * ROWW[0]
                    for h in range(4):
                        sp.dma_start(o0[:, bass.ds(j * (4 * n) + h * n, n)],
                                     row0[:, u, :, :].rearrange("p c w -> p (c w)")[:, h * n:h * n + n]).then_inc(s_row0[u], 4 * CH)

            sp.wait_ge(s_flag, 1)
            unsorted = sp.value_load(flag_i[0:1, 0:1], min_val=0, max_val=E)
            load(0, 0)
            load(1, 1)

            with sp.Fori(0, NCH // 2 - 1) as i:
                for u in range(2):
                    store(i * 2 + u, u)
                    load(i * 2 + u + 2, u)
            for u in range(2):
                store(NCH - 2 + u, u)
            sp.wait_ge(s_meta, 1)
            sp.dma_start(place_d, src_at).then_inc(s_metaw, 16)
            for u in range(2):
                sp.wait_ge(s_row0[u], 16 * CH * (NCH // 2))
            sp.wait_ge(s_tailw, 16 * 2 * T)



            def edge_rows(k):
                flat = ordered[k].rearrange("e w -> (e w)")
                n = PIECE[k] * ROWW[k]
                w = n // 128

                def body(s, u, turn):
                    if not before(s, UN):
                        sp.wait_ge(products[k], s * OPS[k] - (UN - 1) * OPS[k])
                    for h in range(PARTS[k]):
                        at_ = sp.value_load(start_i[k][0:1, bass.ds(s * PARTS[k] + h, 1)], min_val=0, max_val=E * ROWW[k])
                        sp.dma_start(rows[k][:, u, h * w:h * w + w],
                                     flat[bass.ds(at_, n)].rearrange("(p w) -> p w", p=128)).then_inc(rows_in[k][u], 16)

                def moves(m, v, n):
                    if not before(m, SL):
                        sp.wait_ge(s_row1[v], n * (16 * SC))
                    sp.dma_start(in64[:, v, :, :].rearrange("p c w -> p (c w)"),
                                 d64[:, bass.ds(m * (SC * 64), SC * 64)]).then_inc(s_load1[v], 16)
                    sp.dma_start(inmeta[:, v, :, :].rearrange("p c w -> p (c w)"),
                                 meta_d[:, bass.ds(m * (SC * META), SC * META)]).then_inc(s_load1[v], 16)
                    sp.dma_start(inplace[:, v, :], place_d[:, bass.ds(m * SC, SC)]).then_inc(s_load1[v], 16)
                turns(sp, k, body, 0, moves if k == 0 else None)
                if k == 0:
                    with sp.Fori(0, NG) as g:
                        late_moves(moves, g, 0)
                        late_moves(moves, g, 1)

            sp.wait_ge(s_metaw, 16 * NG)
            edge_rows(0)

            for v in range(SL):
                sp.wait_ge(s_row1[v], 16 * SC * (MOVES // SL))
            edge_rows(1)

            def put(g):
                sp.wait_ge(s_fin[1], (g + 1) * FIN[1])
                sp.dma_start(out.rearrange("(b p) f -> p b f", p=BN)[:, bass.ds(g * GB, GB), :], xn[:, :, :]).then_inc(s_put, 16)
            groups(sp, put)
            sp.wait_ge(s_put, 16 * NG)

        @block.gpsimd
        def _(pool):
            nc.gpsimd.iota(iota_i, [[1, max(NPIECE)]], base=0, channel_multiplier=0).then_inc(s_iota, 1)
            nc.gpsimd.iota(part_i[:, :], [[1, 1]], base=0, channel_multiplier=1).then_inc(s_iota, 1)
            pool.wait_ge(s_term, 1)
            nc.gpsimd.tensor_tensor(pos_f, pos_f, tmp, ALU.add).then_inc(s_placed, 1)
            with pool.Fori(1, NB) as b:
                pool.wait_ge(s_term, b + 1)
                pool.wait_ge(s_placed, b)
                nc.gpsimd.tensor_tensor(pos_f, pos_f, tmp, ALU.add).then_inc(s_placed, 1)
            pool.wait_ge(s_flag, 1)
            unsorted = pool.value_load(flag_i[0:1, 0:1], min_val=0, max_val=E)
            pool.wait_ge(s_posd, 1)

            with pool.If(unsorted != 0):
                with pool.Fori(0, NCH // 2) as i:
                    for u in range(2):
                        pool.wait_ge(s_made, i * 2 + u + 1)
                        pool.sem_inc(passed[1], 1)
                        for c in range(CH):
                            pool.indirect_dma_start(ordered[0][0:E, :], bass.IndirectOffsetOnAxis(ap=at[:, u, c:c + 1], axis=0),
                                                    row0[:, u, c, :], None).then_inc(s_row0[u], 16)



            def edge_gather(k):
                pool.wait_ge(s_table[k], 16 * NG)

                def body(s, u, turn):
                    pool.wait_ge(rows_in[k][u], (turn + 1) * (16 * PARTS[k]))
                    if not before(s, SL):
                        pool.wait_ge(products[k], s * OPS[k] - (SL - 1) * OPS[k])
                    pool.sem_inc(passed[1], 1)
                    for t in range(T):
                        i_ap = rows[k][:, u, t * ROWW[k] + IDX[k]:t * ROWW[k] + IDX[k] + 1].bitcast(I32)
                        pool.indirect_dma_start(gath[:, u % SL, t * F:(t + 1) * F], None, table[k],
                                                bass.IndirectOffsetOnAxis(ap=i_ap, axis=0)).then_inc(gathered[k][u % SL], 16)

                def moves(m, v, n):
                    pool.wait_ge(s_made1, m + 1)
                    pool.sem_inc(passed[1], 1)
                    for c in range(SC):
                        pool.indirect_dma_start(ordered[1][0:E, :],
                                                bass.IndirectOffsetOnAxis(ap=inplace[:, v, c:c + 1], axis=0),
                                                row1[:, v, c, :], None).then_inc(s_row1[v], 16)
                turns(pool, k, body, 0, moves if k == 0 else None)
                if k == 0:
                    with pool.Fori(0, NG) as g:
                        late_moves(moves, g, 0)
                        late_moves(moves, g, 1)
            edge_gather(0)
            edge_gather(1)

        def node_columns(k):
            w = node_s[k].shape[1]
            return [(node_s[k][:, 0:S], 0, 0), (node_v[k][:, 0:96], 1, S),
                    (node_s[k][:, S:w], 0, F), (node_v[k][:, 96:192], 1, F + w - S)]

        @block.tensor
        def _(pe):
            def mm(o, l, r, start=True, stop=True):
                return nc.tensor.matmul(o, l, r, start=start, stop=stop)

            def node_prep_group(k, g):
                pe.wait_ge(s_xn[k], g + 1)
                first = isinstance(g, int) and g == 0
                for j in range(GB):
                    if not (first and j < 1):
                        pe.wait_ge(s_xc[k], g * GB + max(j - 1, 0))
                    pe.sem_inc(passed[3], 1)
                    nc.tensor.transpose(pz[0:S, j % 2, 0:BN], xn[:, j, 0:S], ident[0:BN, 0:BN])
                    nc.tensor.transpose(pz[0:96, j % 2, 128:128 + BN], xn[:, j, S:F],
                                        ident[0:BN, 0:BN]).then_inc(s_xt[k], 1)

                for j in range(GB):
                    pe.wait_ge(s_xc[k], g * GB + j + 1)
                    if not (first and j < 1):
                        pe.wait_ge(s_ev[k], g * (2 * GB) + 2 * max(j - 1, 0))
                    for n, (w, c, col) in enumerate(node_columns(k)):
                        rws = S if c == 0 else 96
                        last = mm(pa[0:BN, j % 2, col:col + w.shape[1]], xT[0:rws, j, c, :], w)
                    last.then_inc(s_mm[k], 1)


            def finish_group(k, g):
                first = isinstance(g, int) and g == 0
                vw = 96 if k == 0 else 128
                pe.wait_ge(s_st[k], g + 1)
                for j in range(GB + 1):
                    if j < GB:
                        if not (first and j < 1):
                            pe.wait_ge(s_ac[k], g * GB + max(j - 1, 0))
                        nc.tensor.transpose(pz[0:96, j % 2, 0:BN], st[:, j, 0:96], ident[0:BN, 0:BN])
                        for m in range(3):
                            last = nc.tensor.transpose(pz[0:vw, j % 2, BN * (m + 1):BN * (m + 2)],
                                                       st[:, j, 96 + vw * m:96 + vw * (m + 1)], ident[0:BN, 0:BN])
                        last.then_inc(s_at[k], 1)
                    if j >= 1:
                        q = j - 1
                        if j == 1 and not first:
                            pe.wait_ge(s_fin[k], g * FIN[k] + (READ[k] - FIN[k]))
                        pe.wait_ge(s_ac[k], g * GB + q + 1)
                        sw = S if k == 0 else 96
                        mm(po[:, q, 0:sw], sT[0:96, q % 2, 0:BN], out_s[k][:, 0:sw])
                        if k == 0:
                            mm(po[:, q, F:F + 1], sT[0:96, q % 2, 0:BN], out_s[0][:, S:S + 1])
                        for m in range(3):
                            last = mm(po[:, q, sw + V * m:sw + V * (m + 1)], sT[0:vw, q % 2, BN * (m + 1):BN * (m + 2)],
                                      out_v[k][0:vw, :])
                        last.then_inc(s_ao[k], 1)

            def edge_loop(k):
                w1, w2 = fc1[k], fc2[k]
                ww = w2.shape[1]
                ew = 16 if k == 0 else 64

                def is_step(s):
                    return not isinstance(s, int) or 0 <= s < NSTEP[k]

                def body(s, u, turn):
                    if is_step(s):
                        pe.wait_ge(flattened[k], s + 1)
                        if not (isinstance(s, int) and s < 1):
                            pe.wait_ge(copied[k], s)
                        pe.sem_inc(passed[3], 1)
                        if k == 0:
                            last = nc.tensor.transpose(pz[0:T * ew, 0, 0:128], flat[:, u % 2, 0:T * ew], ident[:, :])
                        else:
                            for j in range(2):
                                last = nc.tensor.transpose(pz[:, 0, 128 * j:128 * (j + 1)], flat[:, u % 2, 128 * j:128 * (j + 1)], ident[:, :])
                        last.then_inc(transposed[k], 1)
                    s1, b1 = s - 1, (u + 1) % 2
                    if is_step(s1):
                        pe.wait_ge(copied[k], s1 + 1)
                        if not (isinstance(s1, int) and s1 < 1):
                            pe.wait_ge(activated[k], s1)
                        if k == 0:
                            for j in range(2):
                                last = mm(pz[:, 1, 128 * j:128 * (j + 1)], w1[:, j, :], efT[0:S, b1, 0:128])
                        else:
                            last = mm(pz[:, 1, 0:256], w1[:, :], efT[:, b1, :])
                        last.then_inc(hidden[k], 1)
                    s2, b2 = s - 2, u % 2
                    if is_step(s2):
                        pe.wait_ge(activated[k], s2 + 1)
                        if not (isinstance(s2, int) and s2 < 2):
                            pe.wait_ge(products[k], s2 * OPS[k] - OPS[k])
                        for t in (0, 2, 1, 3):
                            h = S * (t // 2)
                            last = mm(pw[:, b2, t, 0:ww], hT[h:h + S, b2, t % 2, :], w2[h:h + S, :])
                        last.then_inc(weighted[k], 1)
                    s3, b3 = s - 3, (u + 1) % 2
                    if is_step(s3):
                        pe.wait_ge(products[k], s3 * OPS[k] + OPS[k])

                        if PARTS[k] == 1 and not before(s3, 2):
                            pe.wait_ge(added[k], s3 - 1)
                        mw = CNT + 1 if k == 0 else MW
                        n = T // PARTS[k]
                        for h in range(PARTS[k]):
                            if PARTS[k] == 2 and not before(s3, 1):
                                pe.wait_ge(added[k], s3 * 2 + (h - 1))
                            for t in range(h * n, h * n + n):
                                last = mm(pa[0:BN, h if PARTS[k] == 2 else b3, 0:mw], hot[:, b3, t, :], msg[:, b3, t, 0:mw],
                                          start=(t == h * n), stop=(t == h * n + n - 1))
                            last.then_inc(scattered[k], 1)
                turns(pe, k, body, 3)

            pe.wait_ge(s_const, 1)
            pe.wait_ge(s_cnt, 1)
            for k in range(2):
                mm(pa[0:NB, 0, k:k + 1], cnt[:, k, :], ones[0:EP, 0:1])
            mm(pa[0:1, 0, 8:9], viol[:, :], ones[0:EP, 0:1]).then_inc(s_tot, 1)
            pe.wait_ge(s_nst, 1)
            mm(pa[0:NB, 0, 16:18], upto[0:NB, 0:NB], nst[:, :]).then_inc(s_cum, 1)
            pe.wait_ge(s_reach, 1)
            for k in range(2):
                mm(banks[0:1, 0, k, 0:NPIECE[k]], wgt[:, k:k + 1], reach[k])
                mm(banks[:, 1, k, 0:NPIECE[k]], isblk, reach[k])
                mm(pz[0:EP, k, 0:NB], below[0:EP, 0:EP], cnt[:, k, :], stop=False)
                last = mm(pz[0:EP, k, 0:NB], totb[:, k, 0:EP], below[0:NB, 0:NB], start=False)
            last.then_inc(s_tab, 1)

            pe.wait_ge(s_tabs, 1)
            pe.wait_ge(s_w, 16 * N_W)
            pe.wait_ge(s_scaled, 1)

            groups(pe, lambda g: node_prep_group(0, g))
            pe.wait_ge(s_ev[0], 2 * NB)
            edge_loop(0)
            pe.wait_ge(added[0], NPIECE[0])

            staggered(pe, lambda g: finish_group(0, g), lambda g: node_prep_group(1, g))
            pe.wait_ge(s_ev[1], 2 * NB)
            edge_loop(1)
            pe.wait_ge(added[1], NPIECE[1])
            groups(pe, lambda g: finish_group(1, g))

        @block.scalar
        def _(act):
            def node_prep_group(k, g, aside=None):
                first = isinstance(g, int) and g == 0
                for j in range(GB):
                    act.wait_ge(s_xt[k], g * GB + j + 1)
                    if not first:
                        act.wait_ge(s_mm[k], g * GB + j + 1 - GB)
                    nc.scalar.copy(xT[0:S, j, 0, :], pz[0:S, j % 2, 0:BN])
                    nc.scalar.copy(xT[:, j, 1, :], pz[0:96, j % 2, 128:128 + BN]).then_inc(s_xc[k], 1)
                if aside:
                    aside(0)
                staging = xp if k == 0 else x_sb
                for j in range(GB):
                    act.wait_ge(s_mm[k], g * GB + j + 1)
                    b = g * GB + j
                    t_out = staging[:, bass.ds(b * F, F)]
                    s_out_ = side[:, bass.ds(b * SIDE, KEEP[k])]
                    if k == 0:
                        a = attr[:, bass.ds(b, 1)]
                        nc.scalar.activation(t_out, pa[0:BN, j % 2, 0:F], ACT.Copy, scale=a).then_inc(s_ev[k], 1)
                        nc.scalar.activation(s_out_, pa[0:BN, j % 2, F:F + KEEP[k]], ACT.Copy, scale=a).then_inc(s_ev[k], 1)
                    else:
                        nc.scalar.copy(t_out, pa[0:BN, j % 2, 0:F]).then_inc(s_ev[k], 1)
                        nc.scalar.copy(s_out_, pa[0:BN, j % 2, F:F + KEEP[k]]).then_inc(s_ev[k], 1)
                    if aside and j >= GB - 3:
                        aside(j - (GB - 4))
                act.wait_ge(s_ev[k], g * (2 * GB) + 2 * GB)
                act.dma_start(table[k].rearrange("(b p) f -> p b f", p=BN)[:, bass.ds(g * GB, GB), :],
                              group_of(staging, g, F)).then_inc(s_table[k], 16)

            def finish_group(k, g, aside=None):
                first = isinstance(g, int) and g == 0
                for j in range(GB):
                    if aside and j == GB - 2:
                        aside()
                    act.wait_ge(s_at[k], g * GB + j + 1)
                    if not (first and j < 2):
                        act.wait_ge(s_ao[k], g * GB + j - 1 if j >= 2 else g * GB)
                    if k == 0:
                        nc.scalar.copy(sT[0:96, j % 2, :], pz[0:96, j % 2, 0:4 * BN]).then_inc(s_ac[k], 1)
                    else:
                        nc.scalar.copy(sT[0:96, j % 2, 0:BN], pz[0:96, j % 2, 0:BN])
                        nc.scalar.copy(sT[:, j % 2, BN:4 * BN], pz[:, j % 2, BN:4 * BN]).then_inc(s_ac[k], 1)

            def gates(g):
                act.wait_ge(s_fin[1], g * FIN[1] + 2)
                nc.scalar.activation(fs[:, :, 0:S], tm[:, :, 0:S], ACT.Silu)
                nc.scalar.activation(fs[:, :, S:96], tm[:, :, S:96], ACT.Sigmoid).then_inc(s_act[1], 1)

            def root(k, g):
                act.wait_ge(s_fin[k], g * FIN[k] + ROOT[k])
                nc.scalar.activation(small[:, 6, :], small[:, 5, :], ACT.Sqrt).then_inc(s_rt[k], 1)

            def moves(m, v, n):
                act.wait_ge(s_load1[v], (n + 1) * 48)
                if not before(m, SL):
                    act.wait_ge(s_row1[v], n * (16 * SC))
                r = row1[:, v, :, :]
                nc.scalar.copy(r[:, :, 0:64], in64[:, v, :, :])
                nc.scalar.copy(r[:, :, 64:68], inmeta[:, v, :, 0:4])
                nc.scalar.copy(r[:, :, 68:70].bitcast(I32), inmeta[:, v, :, 4:6].bitcast(I32)).then_inc(s_made1, 1)

            def edge_loop(k):
                def is_step(s):
                    return not isinstance(s, int) or 0 <= s < NSTEP[k]

                ew = 16 if k == 0 else 64

                def body(s, u, turn):
                    if is_step(s):
                        act.wait_ge(rows_in[k][u], (turn + 1) * (16 * PARTS[k]))
                        if not (isinstance(s, int) and s < 2):
                            act.wait_ge(transposed[k], s - 1)
                        if k == 0:
                            f = flat[:, u % 2, 0:T * ew].rearrange("p (t w) -> p t w", t=T)
                            r = rows[k][:, u, :].rearrange("p (t w) -> p t w", t=T)[:, :, 0:ew]
                        else:
                            f = flat[:, u % 2, :].rearrange("p (j h w) -> p j h w", j=2, h=2)
                            r = rows[k][:, u, :].rearrange("p (h j w) -> p j h w", h=2, j=2)[:, :, :, 0:ew]
                        nc.scalar.copy(f, r).then_inc(flattened[k], 1)
                    s1, b1 = s - 1, (u + 1) % 2
                    if is_step(s1):
                        act.wait_ge(transposed[k], s1 + 1)
                        if not (isinstance(s1, int) and s1 < 2):
                            act.wait_ge(hidden[k], s1 - 1)
                        if k == 0:
                            nc.scalar.copy(efT[0:S, b1, 0:128], pz[0:S, 0, 0:128]).then_inc(copied[k], 1)
                        else:
                            nc.scalar.copy(efT[:, b1, :], pz[:, 0, 0:256]).then_inc(copied[k], 1)
                    s2, b2 = s - 2, u % 2
                    if is_step(s2):
                        act.wait_ge(hidden[k], s2 + 1)
                        if not (isinstance(s2, int) and s2 < 2):
                            act.wait_ge(weighted[k], s2 - 1)
                        h = hT[:, b2, :, :].rearrange("p j e -> p (j e)")
                        if k == 0:
                            nc.scalar.activation(h, pz[:, 1, 0:256], ACT.Silu, scale=0.25).then_inc(activated[k], 1)
                        else:
                            nc.scalar.activation(h, pz[:, 1, 0:256], ACT.Relu).then_inc(activated[k], 1)
                            u2, turn2 = (u - 2) % UN, s2 // UN if isinstance(s2, int) else turn - 1 if u < 2 else turn
                            act.wait_ge(gathered[1][u2 % SL], (use(u2, turn2) + 1) * (16 * T))
                            if not (isinstance(s2, int) and s2 < 2):
                                act.wait_ge(products[1], s2 * OPS[1] - OPS[1])
                            for t in range(T):
                                for m in range(3):
                                    h_m = rows[1][:, u2, t * ROWW[1] + SH[1] + m:t * ROWW[1] + SH[1] + m + 1]
                                    last = nc.scalar.activation(gsh[:, b2, t, m * F:(m + 1) * F], gath[:, u2 % SL, t * F:(t + 1) * F],
                                                                ACT.Copy, scale=h_m)
                            last.then_inc(scaled, 1)

                turns(act, k, body, 2, moves if k == 0 else None)

            act.wait_ge(s_blk, 1)
            junk = (run, pos_f)

            def count(b, u, n):
                if n is not None:
                    act.wait_ge(s_signs, n)
                nc.scalar.activation(junk[u], blk[1], ACT.Sign, bias=half[:, bass.ds(b, 1)],
                                     accum_out=signs[:, bass.ds(b, 1)]).then_inc(s_signs, 1)
            for b in range(NB % 2 + 2):
                count(b, b % 2, b - 1 if b >= 2 else None)
            with act.Fori(1, NB // 2) as i:
                for u in range(2):
                    count(i * 2 + 1 + u, (1 + u) % 2, i * 2 + u)

            act.wait_ge(s_w, 16 * N_W)
            act.wait_ge(s_const, 1)
            inv8, inv32 = S ** -0.5, V ** -0.5
            nc.scalar.mul(node_s[0][:, 0:S], raw_s[:, 0, :], inv8)
            nc.scalar.mul(node_s[0][:, S:2 * S], raw_s[:, 1, :], inv8)
            for m in range(3):
                is_m = comp[:, m:m + 1]
                nc.scalar.activation(node_v[0][:, V * m:V * m + V], raw_v[:, 0, :], ACT.Copy, scale=is_m)
                nc.scalar.activation(node_v[0][:, 96:192].rearrange("p (v m) -> p v m", m=3)[:, :, m], raw_v[:, 1, :], ACT.Copy, scale=is_m)
                nc.scalar.activation(node_v[1][:, V * m:V * m + V], raw_v[:, 2, :], ACT.Copy, scale=is_m)
                last = nc.scalar.activation(node_v[1][:, 96 + V * m:96 + V * m + V], raw_v[:, 3, :], ACT.Copy, scale=is_m)
                if m == 2:
                    last.then_inc(s_kron, 1)
            act.wait_ge(s_kron, 1)
            nc.scalar.mul(node_v[0][:, :], node_v[0][:, :], inv32)
            for o, i, w in ((0, 0, 64), (64, 128, 32), (96, 64, 64), (160, 160, 32)):
                nc.scalar.mul(fc2[0][:, o:o + w], raw_fc2[:, i:i + w], inv8)
            for k, w in ((0, S + 1), (1, 96)):
                nc.scalar.mul(out_s[k][S:96, 0:w], out_s[k][S:96, 0:w], 3 ** -0.5)
            nc.scalar.mul(out_v[1][96:128, :], out_v[1][96:128, :], 2 ** -0.5).then_inc(s_scaled, 1)

            act.wait_ge(s_x, 32)

            def prep(g):
                if not (isinstance(g, int) and g == 0):
                    act.wait_ge(s_xt[0], g * GB)
                nc.scalar.copy(xn[:, :, :], group_of(x_sb, g, F)).then_inc(s_xn[0], 1)
                n = NCH // NG

                def chunk(i):
                    assemble(g * n + i, i % 2, g * (n // 2) + i // 2)
                if before(g, 1):
                    node_prep_group(0, g)
                    act.wait_ge(s_posd, 1)
                    for i in range(n):
                        chunk(i)
                else:
                    m = EC // (NG - 1) * META
                    act.wait_ge(s_shd, 2)
                    part_g = bass.ds(g * m - m, m)
                    act.dma_start(meta_d[:, part_g], meta.rearrange("p c m -> p (c m)")[:, part_g]).then_inc(s_metaw, 16)
                    node_prep_group(0, g, chunk)

            act.wait_ge(s_sq, 1)
            nc.scalar.activation(run, tmp, ACT.Sqrt).then_inc(s_len, 1)

            def assemble(j, u, turn):
                act.wait_ge(s_load[u], (turn + 1) * 32)
                if not (isinstance(turn, int) and turn == 0):
                    act.wait_ge(s_row0[u], turn * (16 * CH))
                c = bass.ds(j * CH, CH)
                r0 = row0[:, u, :, :]
                nc.scalar.copy(r0[:, :, 0:16], in16[:, u, :, :])
                nc.scalar.copy(r0[:, :, 16:20], in4[:, u, :, :])
                ri = r0.bitcast(I32)
                nc.scalar.copy(ri[:, :, IDX[0]:IDX[0] + 1], src_i[:, c].unsqueeze(2))
                nc.scalar.copy(ri[:, :, KEY[0]:KEY[0] + 1], dst_i[:, c].unsqueeze(2))
                nc.scalar.copy(at[:, u, :], dst_at[:, c]).then_inc(s_made, 1)
            groups(act, prep)

            edge_loop(0)

            def finish_first_layer(g):
                finish_group(0, g)
                if before(g, 1):
                    late_moves(moves, 0, 1)

            def between(g):
                last = isinstance(g, int) and g == NG - 1
                root(0, g)
                if not last:
                    late_moves(moves, g + 1, 0)
                node_prep_group(1, g)
                if not last:
                    late_moves(moves, g + 1, 1)
            late_moves(moves, 0, 0)
            staggered(act, finish_first_layer, between)
            edge_loop(1)

            def last_stage(g):
                gates(g)
                if isinstance(g, int) and g == NG - 1:
                    root(1, g)
                else:
                    finish_group(1, g + 1, lambda: root(1, g))
            finish_group(1, 0)
            last_stage(0)
            with act.Fori(1, NG - 1) as g:
                last_stage(g)
            last_stage(NG - 1)

        @block.vector
        def _(dve):
            chain = [0]

            def link(ins):
                chain[0] += 1
                ins.then_inc(s_sort, 1)
                dve.wait_ge(s_sort, chain[0])

            tt, ts, stt, cp = nc.vector.tensor_tensor, nc.vector.tensor_scalar, nc.vector.scalar_tensor_tensor, nc.vector.tensor_copy
            link(nc.vector.memset(next_i[:, EC - 1:EC], N))
            nc.vector.memset(fc1[0][:, :, :], 0.0)
            nc.vector.memset(fc1[1][:, :], 0.0).then_inc(s_zero, 1)
            nc.vector.memset(ones_row, 1.0)
            nc.vector.memset(ones[:, :], 1.0)
            for k in range(2):
                link(nc.vector.memset(tail[k], 0.0))
            for k in range(2):
                last = nc.vector.memset(tail[k][:, KEY[k]:KEY[k] + 1].bitcast(I32), 2 * N)
            last.then_inc(s_tail, 1)
            link(nc.vector.memset(dst_at, 0))
            dve.wait_ge(s_iota, 2)
            cp(iota[:, :], iota_i[:, :])
            link(cp(part[:, :], part_i[:, :]))
            ts(half[:, :], iota[0:EP, 0:NB], -1.0, 0.5, ALU.mult, ALU.add)
            nc.vector.memset(signs[:, NB:NB + 1], -float(EC))
            dve.wait_ge(s_keys, 32)
            link(ts(oh, key_i[1], 1.0 / BN, 0.5 / BN - 0.5, ALU.mult, ALU.add))
            ts(blk[1], oh, ROUND, ROUND, ALU.add, ALU.subtract).then_inc(s_blk, 1)
            link(ts(tmp, key_i[0], 1.0 / BN, 0.5 / BN - 0.5, ALU.mult, ALU.add))
            link(ts(blk[0], tmp, ROUND, ROUND, ALU.add, ALU.subtract))
            r96 = part[0:96, 0:1].to_broadcast([96, 3])
            link(ts(comp3[:, :], r96, 1.0 / 3, -1.0 / 3, ALU.mult, ALU.add))
            link(ts(comp3[:, :], comp3[:, :], ROUND, ROUND, ALU.add, ALU.subtract))
            link(stt(comp3[:, :], comp3[:, :], 3.0, iota[0:96, 0:3], ALU.mult, ALU.add))
            ts(comp[:, :], comp3[:, :], part[0:96, 0:1], None, ALU.is_equal)
            ts(ident[:, :], iota[:, 0:128], part[:, 0:1], None, ALU.is_equal)
            ts(below, iota[:, 0:128], part[:, 0:1], None, ALU.is_gt)
            ts(upto, iota[:, 0:128], part[:, 0:1], None, ALU.is_ge).then_inc(s_const, 1)
            ts(big[:, :], part[0:NB, :], NB - 1.0, 1e6, ALU.is_equal, ALU.mult)
            ts(isblk, part[0:NB, 0:1].to_broadcast([NB, 128]), NB - 1.0, None, ALU.is_lt)
            junk = (tmp, oh)

            def count(b, u, n):
                if n is not None:
                    dve.wait_ge(s_count, n)
                ts(junk[u], blk[0], iota[0:EP, bass.ds(b, 1)], 0.0, ALU.is_equal, ALU.add,
                   accum_out=cnt[:, 0, bass.ds(b, 1)]).then_inc(s_count, 1)
            for b in range(NB % 2 + 2):
                count(b, b % 2, b - 1 if b >= 2 else None)
            with dve.Fori(1, NB // 2) as i:
                for u in range(2):
                    count(i * 2 + 1 + u, (1 + u) % 2, i * 2 + u)
            dve.wait_ge(s_count, NB)
            dve.wait_ge(s_next, 32)
            link(tt(tmp, dst_i, next_i, ALU.is_gt))
            nc.vector.reduce_sum(viol[:, :], tmp, AX.X)
            dve.wait_ge(s_signs, NB)
            link(tt(cnt[:, 1, :], signs[:, 0:NB], signs[:, 1:NB + 1], ALU.subtract))
            ts(cnt[:, 1, :], cnt[:, 1, :], 0.5, None, ALU.mult).then_inc(s_cnt, 1)
            dve.wait_ge(s_tot, 1)
            cp(flag_i[0:1, 0:1], pa[0:1, 0, 8:9]).then_inc(s_flag, 1)
            link(cp(tot[:, :], pa[0:NB, 0, 0:2]))
            for k in range(2):
                last = ts(nst[:, k:k + 1], tot[:, k:k + 1], 1.0 / PIECE[k],
                          (PIECE[k] - 1.0) / PIECE[k] - 0.5 + 0.5 / PIECE[k], ALU.mult, ALU.add)
            link(last)
            ts(nst[:, :], nst[:, :], ROUND, ROUND, ALU.add, ALU.subtract).then_inc(s_nst, 1)
            dve.wait_ge(s_nst, 1)
            for k in range(2):
                last = stt(wgt[:, k:k + 1], nst[:, k:k + 1], -float(PIECE[k]), tot[:, k:k + 1], ALU.mult, ALU.add)
            link(last)
            link(ts(wgt[:, :], wgt[:, :], big[:, 0:1], None, ALU.add))
            dve.wait_ge(s_cum, 1)
            link(cp(cum[:, :], pa[0:NB, 0, 16:18]))
            for k in range(2):
                ts(totb[:, k, :], ones[0:NB, :], tot[:, k:k + 1], None, ALU.mult)
                last = ts(reach[k], iota[0:NB, 0:NPIECE[k]], cum[:, k:k + 1], None, ALU.is_ge)
            last.then_inc(s_reach, 1)
            dve.wait_ge(s_tab, 1)
            for k in range(2):
                n = NPIECE[k]
                link(stt(start_f[:, 0:n], iota[0:1, 0:n], float(PIECE[k]), banks[0:1, 0, k, 0:n], ALU.mult, ALU.add))
                ts(start_i[k][:, :], start_f[:, 0:n], float(E), float(ROWW[k]), ALU.min, ALU.mult)
                ts(accoff_i[k][:, :], banks[0:1, 1, k, 0:n], float(MW), None, ALU.mult)
                ts(blk125[k][:, :], banks[:, 1, k, 0:n], float(BN), None, ALU.mult)
                link(cp(pre[:, k, :], pz[0:EP, k, 0:NB]))
            nc.vector.memset(oh, 0.0).then_inc(s_tabs, 1)

            dve.wait_ge(s_e3, 16)
            link(tt(sh_all, ea3, ea3, ALU.mult))
            nc.vector.tensor_reduce(tmp, sh_all, AX.X, ALU.add).then_inc(s_sq, 1)
            dve.wait_ge(s_len, 1)
            link(nc.vector.reciprocal(oh, run))
            link(ts(oh, oh, 3 ** 0.5, None, ALU.mult))
            cp(meta[:, :, 4:5].bitcast(I32), dst_i.unsqueeze(2))
            cp(meta[:, :, 5:6].bitcast(I32), src_i.unsqueeze(2))
            tt(sh_all, ea3, oh.unsqueeze(2).to_broadcast([EP, EC, 3]), ALU.mult).then_inc(s_shd, 1)
            dve.wait_ge(s_shd, 1)
            cp(meta[:, :, 3:4], meta[:, :, 0:1]).then_inc(s_shd, 1)

            def rank(k, b, chain, n):
                dve.wait_ge(chain, n)
                ts(oh, blk[k], iota[0:EP, bass.ds(b, 1)], None, ALU.is_equal).then_inc(chain, 1)
                dve.wait_ge(chain, n + 1)
                nc.vector.tensor_tensor_scan(run, ones_row, oh, pre[:, k, bass.ds(b, 1)], ALU.mult, ALU.add).then_inc(chain, 1)
                dve.wait_ge(chain, n + 2)
                if k == 1 and not before(b, 1):
                    dve.wait_ge(s_placed, b)
                return tt(tmp, run, oh, ALU.mult)

            unsorted = dve.value_load(flag_i[0:1, 0:1], min_val=0, max_val=E)
            with dve.If(unsorted != 0):
                nc.vector.memset(pos_f, 0.0).then_inc(s_pd, 1)
                with dve.Fori(0, NB) as b:
                    rank(0, b, s_pd, b * 4 + 1).then_inc(s_pd, 1)
                    dve.wait_ge(s_pd, b * 4 + 4)
                    tt(pos_f, pos_f, tmp, ALU.add).then_inc(s_pd, 1)
                dve.wait_ge(s_pd, 4 * NB + 1)
                ts(dst_at, pos_f, -1.0, None, ALU.add).then_inc(s_pdd, 1)
                dve.wait_ge(s_pdd, 1)
            nc.vector.memset(kl[:, :], 0.0).then_inc(s_posd, 1)
            nc.vector.memset(pos_f, 0.0).then_inc(s_ps, 1)

            def places(b):
                rank(1, b, s_ps, b * 2 + 1).then_inc(s_term, 1)
            places(0)
            with dve.Fori(1, NB) as b:
                dve.wait_ge(s_term, b)
                places(b)
            dve.wait_ge(s_placed, NB)
            ts(src_at, pos_f, -1.0, None, ALU.add).then_inc(s_meta, 1)
            dve.wait_ge(s_meta, 1)

            def clear(k):
                nc.vector.memset(acc[:, :], 0.0).then_inc(s_clear, 1)
                dve.wait_ge(s_clear, k + 1)

            def edge_loop(k):
                P = products[k]

                def is_step(s):
                    return not isinstance(s, int) or 0 <= s < NSTEP[k]

                def add(s, b, parts):
                    for h in parts:
                        q = s * PARTS[k] + h
                        at_ = dve.value_load(accoff_i[k][0:1, bass.ds(q, 1)], min_val=0, max_val=(NB - 1) * MW)
                        dve.wait_ge(scattered[k], q + 1)
                        if not before(q, 1):
                            dve.wait_ge(added[k], q)
                        mw = CNT + 1 if k == 0 else MW
                        a = acc[:, bass.ds(at_, mw)]
                        tt(a, a, pa[0:BN, h if PARTS[k] == 2 else b, 0:mw], ALU.add).then_inc(added[k], 1)

                def early(s, b):
                    if is_step(s):
                        add(s, b, range(PARTS[k] - 1))

                def body(s, u, turn):
                    if is_step(s):
                        b = u % 2
                        R = rows[k][:, u, :].rearrange("p (t w) -> p t w", t=T)
                        G = gath[:, u % SL, :].rearrange("p (t f) -> p t f", t=T)
                        Gs = G[:, :, 0:S]
                        Gv = G[:, :, S:F].rearrange("p t (m v) -> p t m v", m=3)
                        Wt = pw[:, b, :, :]
                        M = msg[:, b, :, :]
                        vw = 96 if k == 0 else 128
                        Mv = M[:, :, 96:480].rearrange("p t (m w) -> p t m w", m=3) if k == 1 else \
                            M[:, :, 160:448].rearrange("p t (m w) -> p t m w", m=3)
                        sh = R[:, :, SH[k]:SH[k] + 3].unsqueeze(3)
                        shv = sh.to_broadcast([128, T, 3, V])
                        shs = sh.to_broadcast([128, T, 3, S])
                        tqb = tq[:, :, :].unsqueeze(2).to_broadcast([128, T, 3, S])

                        def wv(o):
                            return Wt[:, :, o:o + V].unsqueeze(2).to_broadcast([128, T, 3, V])

                        A4 = ta[:, :, :].rearrange("p t (m v) -> p t m v", m=3)
                        base = s * OPS[k]

                        def after(n):
                            dve.wait_ge(P, base + n)

                        dve.wait_ge(rows_in[k][u], (turn + 1) * (16 * PARTS[k]))
                        if not (isinstance(s, int) and s < 1):
                            after(0)
                        key = R[:, :, KEY[k]:KEY[k] + 1].rearrange("p t o -> p (t o)").bitcast(I32)
                        n = T // PARTS[k]
                        for h in range(PARTS[k]):
                            last = ts(kl[:, h * n:h * n + n], key[:, h * n:h * n + n],
                                      blk125[k][:, bass.ds(s * PARTS[k] + h, 1)], None, ALU.subtract)
                        last.then_inc(P, 1)
                        if not before(s, 2):
                            dve.wait_ge(scattered[k], s * PARTS[k] - PARTS[k])
                        dve.wait_ge(weighted[k], s + 1)
                        dve.wait_ge(gathered[k][u % SL], (use(u, turn) + 1) * (16 * T))
                        if k == 0:
                            tt(tu[:, :, :], Wt[:, :, 0:96], R[:, :, 16:17].to_broadcast([128, T, 96]), ALU.mult).then_inc(P, 1)
                            tt(tq[:, :, :], Wt[:, :, 96:160], Gs, ALU.mult).then_inc(P, 1)
                            tt(A4, Gv, shv, ALU.mult).then_inc(P, 1)
                            after(1)
                            tt(hot[:, b, :, :], iota[:, 0:BN].unsqueeze(1).to_broadcast([128, T, BN]),
                               kl[:, :].unsqueeze(2).to_broadcast([128, T, BN]), ALU.is_equal).then_inc(P, 1)
                            after(2)
                            tt(M[:, :, 0:S], tu[:, :, 0:S], Gs, ALU.mult).then_inc(P, 1)
                            tt(Mv[:, :, :, S:96], tu[:, :, S:96].unsqueeze(2).to_broadcast([128, T, 3, V]), Gv, ALU.mult).then_inc(P, 1)
                            after(3)
                            tt(Mv[:, :, :, 0:S], tqb, shs, ALU.mult).then_inc(P, 1)
                            early(s - 1, (u + 1) % 2)
                            after(4)
                            tt(M[:, :, S:F].rearrange("p t (m v) -> p t m v", m=3), A4, wv(160), ALU.mult).then_inc(P, 1)
                        else:
                            dve.wait_ge(scaled, s + 1)
                            X = gsh[:, b, :, :]

                            def comps(o, n):
                                a = X[:, :, o:o + V]
                                return bass.AP(tensor=a.tensor, offset=a.offset, ap=[a.ap[0], a.ap[1], (192, n), (1, V)])
                            d = comps(S, 3)
                            d = bass.AP(tensor=d.tensor, offset=d.offset, ap=[d.ap[0], d.ap[1], (1, V), (192, 3)])
                            nc.vector.tensor_reduce(td[:, :, :], d, AX.X, ALU.add).then_inc(P, 1)
                            after(1)
                            tt(hot[:, b, :, :], iota[:, 0:BN].unsqueeze(1).to_broadcast([128, T, BN]),
                               kl[:, :].unsqueeze(2).to_broadcast([128, T, BN]), ALU.is_equal).then_inc(P, 1)
                            tt(A4[:, :, 0:2, :], comps(224, 2), comps(96, 2), ALU.subtract).then_inc(P, 1)
                            tt(A4[:, :, 2:3, :], comps(128, 1), comps(384, 1), ALU.subtract).then_inc(P, 1)
                            tt(M[:, :, 0:S], Wt[:, :, 0:S], Gs, ALU.mult).then_inc(P, 1)
                            tt(Mv[:, :, :, 0:S], X.rearrange("p t (m f) -> p t m f", m=3)[:, :, :, 0:S],
                               Wt[:, :, S:2 * S].unsqueeze(2).to_broadcast([128, T, 3, S]), ALU.mult).then_inc(P, 1)
                            tt(Mv[:, :, :, S:96], Gv, wv(128), ALU.mult).then_inc(P, 1)
                            early(s - 1, (u + 1) % 2)
                            after(5)
                            tt(M[:, :, S:96], td[:, :, :], Wt[:, :, 160:192], ALU.mult).then_inc(P, 1)
                            tt(Mv[:, :, :, 96:128], A4, wv(192), ALU.mult).then_inc(P, 1)
                    elif PARTS[k] == 2:
                        early(s - 1, (u + 1) % 2)
                    s1 = s - 1
                    if is_step(s1):
                        add(s1, (u + 1) % 2, (PARTS[k] - 1,))
                turns(dve, k, body, 1)
                dve.wait_ge(added[k], NPIECE[k])

            def normalise(k, g, n, base):
                C = s_fin[k]

                def after(m):
                    dve.wait_ge(C, base + m)
                for j in range(GB):
                    last = nc.vector.bn_stats(stats[:, j, :], y[:, j, :])
                last.then_inc(C, 1)
                after(n + 1)
                dve.sem_inc(passed[2], 1)
                for j in range(GB):
                    last = nc.vector.bn_aggr(mv[:, j, :], stats[:, j, :])
                last.then_inc(C, 1)
                after(n + 2)
                ts(small[:, 5, :].unsqueeze(2), mv[:, :, 1:2], EPS, None, ALU.add).then_inc(C, 1)
                dve.wait_ge(s_rt[k], g + 1)
                nc.vector.reciprocal(small[:, 7, :], small[:, 6, :]).then_inc(C, 1)
                after(n + 4)

            def scaled_out(j):
                return ts(xn[:, j, :], y[:, j, :], mv[:, j, 0:1], small[:, 7, j:j + 1], ALU.subtract, ALU.mult)

            def stage_sums(g):
                if not before(g, 1):
                    dve.wait_ge(s_at[0], g * GB)
                a = group_of(acc, g, MW)
                cp(st[:, :, 0:S], a[:, :, 0:S])
                nc.vector.tensor_reduce(st[:, :, S:96], a[:, :, S:F].rearrange("p b (m v) -> p b v m", m=3), AX.X, ALU.add)
                cp(st[:, :, 96:384], a[:, :, F:CNT]).then_inc(s_st[0], 1)

            def between(g):
                first = isinstance(g, int) and g == 0
                C = s_fin[0]
                base = g * FIN[0]

                def after(m):
                    dve.wait_ge(C, base + m)
                if not first:
                    after(0)
                a = group_of(acc, g, MW)
                ts(small[:, 0, :].unsqueeze(2), a[:, :, CNT:CNT + 1], 1.0, None, ALU.max).then_inc(C, 1)
                after(1)
                nc.vector.reciprocal(small[:, 1, :], small[:, 0, :]).then_inc(C, 1)
                after(2)
                stt(small[:, 2, :], small[:, 1, :], 96 ** -0.5, attr[:, bass.ds(g * GB, GB)], ALU.mult, ALU.mult).then_inc(C, 1)
                after(3)
                tt(small[:, 3, :], small[:, 2, :], small[:, 2, :], ALU.mult).then_inc(C, 1)
                tt(y[:, :, :], group_of(x_sb, g, F), group_of(side, g, SIDE)[:, :, 0:F], ALU.add).then_inc(C, 1)
                dve.wait_ge(s_ao[0], g * GB + GB)
                after(4)
                tt(small[:, 4, :].unsqueeze(2), po[:, :, F:F + 1], small[:, 3, :].unsqueeze(2), ALU.mult).then_inc(C, 1)
                after(6)
                tt(tm[:, :, 0:F], po[:, :, 0:F], small[:, 4, :].unsqueeze(2).to_broadcast([BN, GB, F]), ALU.mult).then_inc(C, 1)
                after(7)
                tt(y[:, :, 0:S], y[:, :, 0:S], tm[:, :, 0:S], ALU.add)
                yv = y[:, :, S:F].rearrange("p b (v m) -> p b m v", m=3)
                tt(yv, yv, tm[:, :, S:F].rearrange("p b (m v) -> p b m v", m=3), ALU.add).then_inc(C, 1)
                after(8)
                normalise(0, g, 8, base)
                if not first:
                    dve.wait_ge(s_xt[1], g * GB)
                for j in range(GB):
                    last = scaled_out(j)
                last.then_inc(C, 1)
                after(13)
                cp(group_of(xp, g, F), xn[:, :, :]).then_inc(s_xn[1], 1)

            def stage_last_sums(g):
                if not before(g, 1):
                    dve.wait_ge(s_at[1], g * GB)
                a = group_of(acc, g, MW)
                av, sv = (t[:, :, 96:MW].rearrange("p b (m w) -> p b m w", m=3) for t in (a, st[:, :, :]))
                ts(st[:, :, 0:96], a[:, :, 0:96], 1.0 / 32, None, ALU.mult)
                ts(sv[:, :, :, 0:96], av[:, :, :, 0:96], 1.0 / 32, None, ALU.mult)
                ts(sv[:, :, 0:2, 96:128], av[:, :, 1:3, 96:128], 1.0 / 32, None, ALU.mult)
                ts(sv[:, :, 2, 96:128], av[:, :, 0, 96:128], 1.0 / 32, None, ALU.mult).then_inc(s_st[1], 1)

            def last_stage(g):
                first = isinstance(g, int) and g == 0
                C = s_fin[1]
                base = g * FIN[1]

                def after(m):
                    dve.wait_ge(C, base + m)
                if not first:
                    after(0)
                dve.wait_ge(s_ao[1], g * GB + GB)
                tt(tm[:, :, :], po[:, :, 0:SIDE], group_of(side, g, SIDE), ALU.add).then_inc(C, 1)
                nc.vector.memset(small[:, 0, :], 0.0).then_inc(C, 1)
                dve.wait_ge(s_act[1], g + 1)
                X = group_of(xp, g, F)
                tt(y[:, :, 0:S], X[:, :, 0:S], fs[:, :, 0:S], ALU.add)
                tv = tm[:, :, 96:192].rearrange("p b (m v) -> p b m v", m=3)
                tt(tv, tv, fs[:, :, S:96].unsqueeze(2).to_broadcast([BN, GB, 3, V]), ALU.mult).then_inc(C, 1)
                after(3)
                tt(y[:, :, S:F].rearrange("p b (v m) -> p b m v", m=3), X[:, :, S:F].rearrange("p b (v m) -> p b m v", m=3), tv,
                   ALU.add).then_inc(C, 1)
                after(4)
                normalise(1, g, 4, base)
                if not first:
                    dve.wait_ge(s_put, 16 * g)
                for j in range(GB):
                    last = scaled_out(j)
                last.then_inc(C, 1)

            dve.wait_ge(s_made, NCH)
            for u in range(2):
                dve.wait_ge(s_row0[u], 16 * CH * (NCH // 2))
            dve.wait_ge(s_metaw, 16 * NG)
            clear(0)
            link(nc.vector.memset(msg[:, :, :, CNT:CNT + 1], 1.0))
            edge_loop(0)
            staggered(dve, stage_sums, between)
            clear(1)
            edge_loop(1)
            staggered(dve, stage_last_sums, last_stage)


_INS = ["x", "src", "dst", "edge_attr_16", "edge_attr_3", "edge_attr_4", "edge_attr_64", "node_vec1",
        "L0_gnn_Wfc1", "L0_gnn_Wfc2", "L0_gnn_Wsc0", "L0_gnn_Wsc1", "L0_gnn_Wl1_0", "L0_gnn_Wl1_1",
        "L0_gnn_Wl2_s", "L0_gnn_Wl2_v", "L0_gnn_Wa",
        "L1_gnn_W_skip0", "L1_gnn_W_skip1", "L1_gnn_W_nl0", "L1_gnn_W_nl1", "L1_gnn_W_fc1", "L1_gnn_W_fc2",
        "L1_gnn_W_out_s", "L1_gnn_W_out_v"]


def kernel(**inputs):
    import numpy as _np
    import concourse.bacc as _bacc
    from concourse.bass_utils import run_bass_kernel_spmd as _run

    nc = _bacc.Bacc("TRN2", target_bir_lowering=False, num_devices=1)
    arrays, args = {}, []
    for name in _INS:
        a = _np.ascontiguousarray(inputs[name])
        arrays[f"in_{name}"] = a
        args.append(nc.dram_tensor(f"in_{name}", a.shape, mybir.dt.from_np(a.dtype), kind="ExternalInput").ap())
    args.append(nc.dram_tensor("out_0", (N, F), F32, kind="ExternalOutput").ap())
    gnn_kernel(nc, *args)
    r = _run(nc, [arrays], core_ids=[0])
    return r.results[0]["out_0"]
```
